# Optimizing a Trainium2 kernel written in Bass

```python
import numpy as np
import jax
import jax.numpy as jnp

def _softmax(x, axis=-1):
    return jax.nn.softmax(x, axis=axis)

def _gelu(x):
    return jax.nn.gelu(x, approximate=True)

def _silu(x):
    return jax.nn.silu(x)

def _sigmoid(x):
    return jax.nn.sigmoid(x)

def _layernorm(x, axis=-1, eps=1e-05):
    m = jnp.mean(x, axis=axis, keepdims=True)
    v = jnp.var(x, axis=axis, keepdims=True)
    return (x - m) / jnp.sqrt(v + eps)

def _scatter_add(tgt, idx, src, axis=0):
    return tgt.at[idx].add(src)

def _segment_sum(src, seg, n):
    return jax.ops.segment_sum(src, seg, n)
kernel_name = 'mk_hybrid_d1_jaxref_r8_34913c'

def setup_inputs(seed: int=0):
    np.random.seed(seed)
    _w = jnp.asarray

    def _L0_attn_a_setup():
        import jax, jax.numpy as jnp
        import numpy as np
        DM, EXP, N, K, FRAC = (128, 2, 16, 4, 16)
        D = DM * EXP
        DTR = D // FRAC
        EPS = 1e-06

        def _mamba_block(x, rms_w, in_W, in_b, conv_w, conv_b, A_log, dbc_W, dbc_b, dup_W, dup_b, out_W, out_b):
            residual = x
            h = x * jax.lax.rsqrt(jnp.mean(x * x, axis=-1, keepdims=True) + EPS) * rms_w
            proj = h @ in_W + in_b
            x1, g = (proj[..., :D], proj[..., D:])
            xt = jnp.transpose(x1, (0, 2, 1))
            xc = jax.lax.conv_general_dilated(xt, conv_w[:, None, :], window_strides=(1,), padding=[(K - 1, 0)], feature_group_count=D, dimension_numbers=('NCH', 'OIH', 'NCH'))
            xc = xc + conv_b[:, None]
            x1 = jax.nn.silu(jnp.transpose(xc, (0, 2, 1)))
            A = -jnp.exp(A_log)
            dbc = x1 @ dbc_W + dbc_b
            delta, Bm, Cm = (dbc[..., :DTR], dbc[..., DTR:DTR + N], dbc[..., DTR + N:])
            delta = jax.nn.softplus(delta @ dup_W + dup_b)
            A_disc = jnp.exp(delta[..., None] * A)
            B_x = delta[..., None] * Bm[:, :, None, :] * x1[..., None]
            Ad_t = jnp.transpose(A_disc, (1, 0, 2, 3))
            Bx_t = jnp.transpose(B_x, (1, 0, 2, 3))

            def step(hc, inp):
                a, b = inp
                hc = a * hc + b
                return (hc, hc)
            h0 = jnp.zeros((x.shape[0], D, N), x1.dtype)
            _, hs = jax.lax.scan(step, h0, (Ad_t, Bx_t))
            y = jnp.einsum('tbdn,btn->btd', hs, Cm)
            y = jax.nn.silu(g) * y
            out = y @ out_W + out_b
            return out + residual
        key = jax.random.key(seed)
        ks = jax.random.split(key, 12)
        s = lambda fan: 1.0 / np.sqrt(fan)
        x = jax.random.normal(ks[0], (2, 128, DM), jnp.float32)
        rms_w = jnp.ones((DM,), jnp.float32)
        in_W = jax.random.normal(ks[1], (DM, 2 * D), jnp.float32) * s(DM)
        in_b = jax.random.normal(ks[2], (2 * D,), jnp.float32) * s(DM)
        conv_w = jax.random.normal(ks[3], (D, K), jnp.float32) * s(K)
        conv_b = jax.random.normal(ks[4], (D,), jnp.float32) * s(K)
        A_log = jnp.log(jnp.tile(jnp.arange(1, N + 1, dtype=jnp.float32), (D, 1)))
        dbc_W = jax.random.normal(ks[5], (D, DTR + 2 * N), jnp.float32) * s(D)
        dbc_b = jax.random.normal(ks[6], (DTR + 2 * N,), jnp.float32) * s(D)
        dup_W = jax.random.normal(ks[7], (DTR, D), jnp.float32) * s(DTR)
        dup_b = jax.random.normal(ks[8], (D,), jnp.float32) * s(DTR)
        out_W = jax.random.normal(ks[9], (D, DM), jnp.float32) * s(D)
        out_b = jax.random.normal(ks[10], (DM,), jnp.float32) * s(D)
        return dict(x=x, rms_w=rms_w, in_W=in_W, in_b=in_b, conv_w=conv_w, conv_b=conv_b, A_log=A_log, dbc_W=dbc_W, dbc_b=dbc_b, dup_W=dup_W, dup_b=dup_b, out_W=out_W, out_b=out_b)
    _L0_attn_a_in = _L0_attn_a_setup()

    def _L0_attn_b_setup():
        import jax, jax.numpy as jnp
        import numpy as np
        D = 128
        HEADS = 16
        LN_EPS = 1e-05
        SHEP_EPS = 0.0001
        SHEP_P = 2

        def _shepards_mha(Q, K, V):
            q2 = jnp.sum(Q * Q, axis=-1, keepdims=True)
            k2 = jnp.sum(K * K, axis=-1, keepdims=True)
            sq = q2 + jnp.swapaxes(k2, -1, -2) - 2.0 * jnp.einsum('bhqd,bhkd->bhqk', Q, K)
            dist = jnp.sqrt(jnp.maximum(sq, 0.0))
            W = (SHEP_EPS + dist) ** (-SHEP_P)
            W = W / (SHEP_EPS + jnp.sum(W, axis=-1, keepdims=True))
            return jnp.einsum('bhqk,bhkd->bhqd', W, V)
        key = jax.random.key(seed)
        k1, k2, k3 = jax.random.split(key, 3)
        b, t, d = (2, 256, D)
        X = jax.random.normal(k1, (b, t, d), dtype=jnp.float32)
        W_in = jax.random.normal(k2, (4 * d, d), dtype=jnp.float32) * (1.0 / np.sqrt(d))
        b_in = jnp.zeros((4 * d,), dtype=jnp.float32)
        W_out = jax.random.normal(k3, (d, d), dtype=jnp.float32) * (1.0 / np.sqrt(d))
        b_out = jnp.zeros((d,), dtype=jnp.float32)
        return {'X': X, 'W_in': W_in, 'b_in': b_in, 'W_out': W_out, 'b_out': b_out}
    _L0_attn_b_in = _L0_attn_b_setup()

    def _L0_ffn_setup():
        import jax, jax.numpy as jnp
        import numpy as np
        B, S, D = (2, 64, 128)
        E, K, I = (16, 8, 128)
        I_SH = 128
        ROUTE_SCALE = 2.826
        key = jax.random.key(seed)
        ks = jax.random.split(key, 8)
        s = 0.02
        return {'x': jax.random.normal(ks[0], (B, S, D), dtype=jnp.float32), 'gate_w': jax.random.normal(ks[1], (E, D), dtype=jnp.float32) * s, 'expert_bias': jnp.zeros((E,), dtype=jnp.float32), 'w_gate': jax.random.normal(ks[2], (E, I, D), dtype=jnp.float32) * s, 'w_up': jax.random.normal(ks[3], (E, I, D), dtype=jnp.float32) * s, 'w_down': jax.random.normal(ks[4], (E, D, I), dtype=jnp.float32) * s, 'shared_gate_w': jax.random.normal(ks[5], (I_SH, D), dtype=jnp.float32) * s, 'shared_up_w': jax.random.normal(ks[6], (I_SH, D), dtype=jnp.float32) * s, 'shared_down_w': jax.random.normal(ks[7], (D, I_SH), dtype=jnp.float32) * s}
    _L0_ffn_in = _L0_ffn_setup()
    _d = {'L0_attn_a_x': _L0_attn_a_in['x'], 'L0_attn_a_rms_w': _L0_attn_a_in['rms_w'], 'L0_attn_a_in_W': _L0_attn_a_in['in_W'], 'L0_attn_a_in_b': _L0_attn_a_in['in_b'], 'L0_attn_a_conv_w': _L0_attn_a_in['conv_w'], 'L0_attn_a_conv_b': _L0_attn_a_in['conv_b'], 'L0_attn_a_A_log': _L0_attn_a_in['A_log'], 'L0_attn_a_dbc_W': _L0_attn_a_in['dbc_W'], 'L0_attn_a_dbc_b': _L0_attn_a_in['dbc_b'], 'L0_attn_a_dup_W': _L0_attn_a_in['dup_W'], 'L0_attn_a_dup_b': _L0_attn_a_in['dup_b'], 'L0_attn_a_out_W': _L0_attn_a_in['out_W'], 'L0_attn_a_out_b': _L0_attn_a_in['out_b'], 'L0_attn_b_W_in': _L0_attn_b_in['W_in'], 'L0_attn_b_b_in': _L0_attn_b_in['b_in'], 'L0_attn_b_W_out': _L0_attn_b_in['W_out'], 'L0_attn_b_b_out': _L0_attn_b_in['b_out'], 'L0_ffn_gate_w': _L0_ffn_in['gate_w'], 'L0_ffn_expert_bias': _L0_ffn_in['expert_bias'], 'L0_ffn_w_gate': _L0_ffn_in['w_gate'], 'L0_ffn_w_up': _L0_ffn_in['w_up'], 'L0_ffn_w_down': _L0_ffn_in['w_down'], 'L0_ffn_shared_gate_w': _L0_ffn_in['shared_gate_w'], 'L0_ffn_shared_up_w': _L0_ffn_in['shared_up_w'], 'L0_ffn_shared_down_w': _L0_ffn_in['shared_down_w']}
    _x0 = _d['L0_attn_a_x']
    _d['L0_attn_a_x'] = jax.random.normal(jax.random.fold_in(jax.random.key(seed), 1), (16, 256, 128), dtype=_x0.dtype)
    del _x0
    return _d

def reference(L0_attn_a_x, L0_attn_a_rms_w, L0_attn_a_in_W, L0_attn_a_in_b, L0_attn_a_conv_w, L0_attn_a_conv_b, L0_attn_a_A_log, L0_attn_a_dbc_W, L0_attn_a_dbc_b, L0_attn_a_dup_W, L0_attn_a_dup_b, L0_attn_a_out_W, L0_attn_a_out_b, L0_attn_b_W_in, L0_attn_b_b_in, L0_attn_b_W_out, L0_attn_b_b_out, L0_ffn_gate_w, L0_ffn_expert_bias, L0_ffn_w_gate, L0_ffn_w_up, L0_ffn_w_down, L0_ffn_shared_gate_w, L0_ffn_shared_up_w, L0_ffn_shared_down_w):

    def _L0_attn_a_ref(x, rms_w, in_W, in_b, conv_w, conv_b, A_log, dbc_W, dbc_b, dup_W, dup_b, out_W, out_b):
        import jax, jax.numpy as jnp
        import numpy as np
        DM, EXP, N, K, FRAC = (128, 2, 16, 4, 16)
        D = DM * EXP
        DTR = D // FRAC
        EPS = 1e-06

        def _mamba_block(x, rms_w, in_W, in_b, conv_w, conv_b, A_log, dbc_W, dbc_b, dup_W, dup_b, out_W, out_b):
            residual = x
            h = x * jax.lax.rsqrt(jnp.mean(x * x, axis=-1, keepdims=True) + EPS) * rms_w
            proj = h @ in_W + in_b
            x1, g = (proj[..., :D], proj[..., D:])
            xt = jnp.transpose(x1, (0, 2, 1))
            xc = jax.lax.conv_general_dilated(xt, conv_w[:, None, :], window_strides=(1,), padding=[(K - 1, 0)], feature_group_count=D, dimension_numbers=('NCH', 'OIH', 'NCH'))
            xc = xc + conv_b[:, None]
            x1 = jax.nn.silu(jnp.transpose(xc, (0, 2, 1)))
            A = -jnp.exp(A_log)
            dbc = x1 @ dbc_W + dbc_b
            delta, Bm, Cm = (dbc[..., :DTR], dbc[..., DTR:DTR + N], dbc[..., DTR + N:])
            delta = jax.nn.softplus(delta @ dup_W + dup_b)
            A_disc = jnp.exp(delta[..., None] * A)
            B_x = delta[..., None] * Bm[:, :, None, :] * x1[..., None]
            Ad_t = jnp.transpose(A_disc, (1, 0, 2, 3))
            Bx_t = jnp.transpose(B_x, (1, 0, 2, 3))

            def step(hc, inp):
                a, b = inp
                hc = a * hc + b
                return (hc, hc)
            h0 = jnp.zeros((x.shape[0], D, N), x1.dtype)
            _, hs = jax.lax.scan(step, h0, (Ad_t, Bx_t))
            y = jnp.einsum('tbdn,btn->btd', hs, Cm)
            y = jax.nn.silu(g) * y
            out = y @ out_W + out_b
            return out + residual
        return _mamba_block(x, rms_w, in_W, in_b, conv_w, conv_b, A_log, dbc_W, dbc_b, dup_W, dup_b, out_W, out_b)

    def _L0_attn_b_ref(X, W_in, b_in, W_out, b_out):
        import jax, jax.numpy as jnp
        import numpy as np
        D = 128
        HEADS = 16
        LN_EPS = 1e-05
        SHEP_EPS = 0.0001
        SHEP_P = 2

        def _shepards_mha(Q, K, V):
            q2 = jnp.sum(Q * Q, axis=-1, keepdims=True)
            k2 = jnp.sum(K * K, axis=-1, keepdims=True)
            sq = q2 + jnp.swapaxes(k2, -1, -2) - 2.0 * jnp.einsum('bhqd,bhkd->bhqk', Q, K)
            dist = jnp.sqrt(jnp.maximum(sq, 0.0))
            W = (SHEP_EPS + dist) ** (-SHEP_P)
            W = W / (SHEP_EPS + jnp.sum(W, axis=-1, keepdims=True))
            return jnp.einsum('bhqk,bhkd->bhqd', W, V)
        b, t, d = X.shape
        h = HEADS
        dh = d // h
        mu = jnp.mean(X, axis=-1, keepdims=True)
        var = jnp.mean((X - mu) ** 2, axis=-1, keepdims=True)
        Xn = (X - mu) / jnp.sqrt(var + LN_EPS)
        P = jnp.einsum('btd,ed->bte', Xn, W_in) + b_in
        P = P.reshape(b, t, h, 4 * dh).transpose(0, 2, 1, 3)
        Q, K, V, G = jnp.split(P, 4, axis=-1)
        A = _shepards_mha(Q, K, V)
        O = (G * A).transpose(0, 2, 1, 3).reshape(b, t, d)
        return X + jnp.einsum('btd,ed->bte', O, W_out) + b_out

    def _L0_ffn_ref(x, gate_w, expert_bias, w_gate, w_up, w_down, shared_gate_w, shared_up_w, shared_down_w):
        import jax, jax.numpy as jnp
        import numpy as np
        B, S, D = (2, 64, 128)
        E, K, I = (16, 8, 128)
        I_SH = 128
        ROUTE_SCALE = 2.826
        gates = jnp.einsum('bsd,ed->bse', x, gate_w)
        scores = jax.nn.sigmoid(gates.astype(jnp.float32))
        sel_scores = scores + expert_bias
        _, inds = jax.lax.top_k(sel_scores, K)
        selected = jnp.take_along_axis(scores, inds, axis=-1)
        selected = selected / selected.sum(axis=-1, keepdims=True)
        selected = selected * ROUTE_SCALE
        onehot = jax.nn.one_hot(inds, E, dtype=selected.dtype)
        combine = jnp.einsum('bske,bsk->bse', onehot, selected)
        hg = jnp.einsum('bsd,eid->bsei', x, w_gate)
        hu = jnp.einsum('bsd,eid->bsei', x, w_up)
        h = jax.nn.silu(hg) * hu
        ye = jnp.einsum('bsei,edi->bsed', h, w_down)
        y = jnp.einsum('bsed,bse->bsd', ye, combine).astype(x.dtype)
        g = jnp.einsum('bsd,id->bsi', x, shared_gate_w)
        u = jnp.einsum('bsd,id->bsi', x, shared_up_w)
        y = y + jnp.einsum('bsi,di->bsd', jax.nn.silu(g) * u, shared_down_w)
        return y
    x = L0_attn_a_x
    x = x + _L0_attn_a_ref(_layernorm(x, axis=-1), L0_attn_a_rms_w, L0_attn_a_in_W, L0_attn_a_in_b, L0_attn_a_conv_w, L0_attn_a_conv_b, L0_attn_a_A_log, L0_attn_a_dbc_W, L0_attn_a_dbc_b, L0_attn_a_dup_W, L0_attn_a_dup_b, L0_attn_a_out_W, L0_attn_a_out_b)
    x = x + _L0_ffn_ref(_layernorm(x, axis=-1), L0_ffn_gate_w, L0_ffn_expert_bias, L0_ffn_w_gate, L0_ffn_w_up, L0_ffn_w_down, L0_ffn_shared_gate_w, L0_ffn_shared_up_w, L0_ffn_shared_down_w)
    x = x + _L0_attn_b_ref(_layernorm(x, axis=-1), L0_attn_b_W_in, L0_attn_b_b_in, L0_attn_b_W_out, L0_attn_b_b_out)
    x = x + _L0_ffn_ref(_layernorm(x, axis=-1), L0_ffn_gate_w, L0_ffn_expert_bias, L0_ffn_w_gate, L0_ffn_w_up, L0_ffn_w_down, L0_ffn_shared_gate_w, L0_ffn_shared_up_w, L0_ffn_shared_down_w)
    return x

_drawn_inputs = setup_inputs


def setup_inputs(seed=0):
    import zlib

    import numpy as np

    out = dict(_drawn_inputs(seed))
    spreads = {'L0_attn_a_rms_w': (1.0, 0.2),
     'L0_attn_b_b_in': (0.0, 0.329),
     'L0_attn_b_b_out': (0.0, 0.317),
     'L0_ffn_expert_bias': (0.0, 0.8)}
    factors = {'L0_ffn_gate_w': 8.0,
     'L0_ffn_w_gate': 8.0,
     'L0_ffn_w_up': 8.0,
     'L0_ffn_w_down': 8.0,
     'L0_ffn_shared_gate_w': 8.0,
     'L0_ffn_shared_up_w': 8.0,
     'L0_ffn_shared_down_w': 8.0}
    for name, (base, spread) in spreads.items():
        noise = np.random.default_rng([zlib.crc32(name.encode()), seed]).standard_normal(out[name].shape)
        drawn = base * np.exp(spread * noise) if base else spread * noise
        out[name] = jnp.asarray(drawn.astype(out[name].dtype))
    for name, factor in factors.items():
        out[name] = (out[name] * factor).astype(out[name].dtype)
    return out
```

```python
import concourse.bass as bass
from concourse import mybir
from contextlib import ExitStack

FP32 = mybir.dt.float32
FP16 = mybir.dt.float16
ALU = mybir.AluOpType
ACT = mybir.ActivationFunctionType
AX = mybir.AxisListType

P = 128
NB, T, DM = 16, 256, 128
TT = T // P
NT = NB * TT
DI, NS, DTR, KC = 256, 16, 16, 4
DC = DI // P
NE = 16
TOPK = 8
ROUTE_SCALE = 2.826
QC = 4 * P
NQ = NB * T // QC
NH, DH = 16, 8
HG = 4
LN_EPS = 1e-5
RMS_EPS = 1e-6
SHEP_EPS = 1e-4
TAKEN = -1e30


class Chain:

    def __init__(self, eng, sem):
        self.eng, self.sem, self.n = eng, sem, 0

    def link(self, ins):
        self.n += 1
        ins.then_inc(self.sem, 1)
        self.eng.wait_ge(self.sem, self.n)

    def end(self):
        if self.n:
            self.eng.sem_inc(self.sem, -self.n)
        self.n = 0


def take(eng, sem, n=1):
    eng.wait_ge(sem, n)
    eng.sem_inc(sem, -n)


def broadcast(ap, shape):
    return ap.to_broadcast(shape)


def mamba_layer(nc, sems, x_sb, w, ident, half):
    ctx = ExitStack()
    with ctx:
        def sb(name, shape, dt=FP32):
            return ctx.enter_context(nc.sbuf_tensor("m_" + name, shape, dt))

        def pb(name, dt=FP32, width=512):
            return ctx.enter_context(nc.psum_tensor("m_" + name, [P, width], dt))

        def sem(name):
            return sems.enter_context(nc.semaphore("m_" + name))

        in_w = sb("in_w", [P, 2 * DI])
        in_b = sb("in_b", [P, 2 * DC])
        rms_w = sb("rms_w", [P, 1])
        conv_w = sb("conv_w", [P, DC, KC])
        conv_b = sb("conv_b", [P, DC])
        neg_a = sb("neg_a", [P, DC, NS])
        dbc_w = sb("dbc_w", [P, DC, P])
        dbc_b = sb("dbc_b", [P, 1])
        dup_w = sb("dup_w", [3 * DTR, DI])
        dup_b = sb("dup_b", [P, DC])
        out_w = sb("out_w", [P, DC, DM])
        out_b = sb("out_b", [P, DM])
        pick = sb("pick", [96, 2 * NS, P], FP16)

        stats = sb("stats", [P, TT, 6])
        mv = sb("mv", [P, TT, 2])
        nrm = sb("nrm", [P, 4, TT])
        xn = sb("xn", [P, TT, DM])
        z = sb("z", [P, TT, DM])
        hT = sb("hT", [P, T])
        xpad = sb("xpad", [P, DC, KC - 1 + T])
        conv = sb("conv", [P, DC, T])
        xs = sb("xs", [P, DC, T])
        bcd = sb("bcd", [P, T])
        bc_hi = sb("bc_hi", [96, T], FP16)
        sp_in = sb("sp_in", [P, DC, T])
        sp = sb("sp", [P, DC, T])
        res = sb("res", [P, 2, TT, DM])
        gate = sb("gate", [P, 2, DC, T])
        delta = sb("delta", [P, 2, DC, T])
        dx = sb("dx", [P, 2, DC, T])
        bc = sb("bc", [96, 2, T], FP16)
        decay = sb("decay", [P, 2, 2, DC, T])
        h = sb("h", [P, 2, 2, DC, T])
        c_sb = sb("c_sb", [P, 2, T])
        hc = sb("hc", [P, 4, 2, DC, T])
        yg = sb("yg", [P, DC, T])

        b_ps = [pb("b_ps0"), pb("b_ps1")]
        c_ps = [pb("c_ps0"), pb("c_ps1")]
        y_ps = pb("y_ps")
        t0, t1, t2 = pb("t0"), pb("t1"), pb("t2")

        w_loaded = sem("w_loaded")
        w_ready = {e: sem("w_ready_" + e) for e in ("act", "dve", "pool", "pe")}
        setup_done = {e: sem("setup_done_" + e) for e in ("act", "dve", "pe")}
        pool_chain, dve_chain, act_chain = sem("pool_chain"), sem("dve_chain"), sem("act_chain")
        stats_ready, norm_ready, xn_ready, res_ready = (sem(n) for n in ("stats_ready", "norm_ready", "xn_ready", "res_ready"))
        z_ready, zT_ready, hT_ready = sem("z_ready"), sem("zT_ready"), sem("hT_ready")
        x1_ready, g_ready, xpad_ready, conv_ready, xs_ready = (sem(n) for n in ("x1_ready", "g_ready", "xpad_ready", "conv_ready", "xs_ready"))
        dbc_ready, bcd_ready, bc_hi_ready, bc_ready = (sem(n) for n in ("dbc_ready", "bcd_ready", "bc_hi_ready", "bc_ready"))
        dup_ready, sp_in_ready, sp_ready, delta_ready = (sem(n) for n in ("dup_ready", "sp_in_ready", "sp_ready", "delta_ready"))
        t2_free = sem("t2_free")
        b_ready, c_ready, decay_ready = sem("b_ready"), sem("c_ready"), sem("decay_ready")
        core_chain = sem("core_chain")
        h_ready, c_sb_ready = sem("h_ready"), sem("c_sb_ready")
        hc_dve, hc_pool = sem("hc_dve"), sem("hc_pool")
        y_ready, yg_ready, o_ready = sem("y_ready"), sem("yg_ready"), sem("o_ready")

        PAIRS = NS // 2
        POOL_PAIRS = (1, 4)

        def rank(m):
            mine = [k for k in range(m + 1) if (k in POOL_PAIRS) == (m in POOL_PAIRS)]
            return len(mine)

        LOADS = [(in_w, w["in_w"]), (in_b, w["in_b"]), (rms_w, w["rms_w"]), (conv_w, w["conv_w"]),
                 (conv_b, w["conv_b"]), (neg_a, w["a_log"]), (dbc_w, w["dbc_w"]), (dbc_b, w["dbc_b"]),
                 (dup_b, w["dup_b"]), (out_w, w["out_w"]), (out_b, w["out_b"])]

        def batches(eng, body, prologue, epilogue):
            prologue()
            body(0, 0, first=True)
            with eng.Fori(0, NB // 2 - 1) as i:
                body(i * 2 + 1, 1)
                body(i * 2 + 2, 0)
            body(NB - 1, (NB - 1) % 2, last=True)
            epilogue()

        block = ctx.enter_context(nc.Block())

        @block.sync
        def _(sp_eng):
            for dst, src in LOADS:
                sp_eng.dma_start(dst[:], src).then_inc(w_loaded, 16)
            sp_eng.dma_start(dup_w[2 * DTR:3 * DTR, :], w["dup_w"]).then_inc(w_loaded, 16)
            sp_eng.wait_ge(w_loaded, 16 * (len(LOADS) + 1))
            for s in w_ready.values():
                sp_eng.sem_inc(s, 1)

        @block.gpsimd
        def _(pool):
            chain = Chain(pool, pool_chain)
            chain.link(nc.gpsimd.memset(pick[:], 0.0))
            nc.gpsimd.memset(bc[:], 0.0)
            nc.gpsimd.memset(xpad[:, :, 0:KC - 1], 0.0)
            chain.link(nc.gpsimd.memset(decay[:, :, :, :, 0:1], 0.0))
            for base in (0, -64):
                chain.link(nc.gpsimd.affine_select(out=pick[:], in_=pick[:], compare_op=ALU.not_equal, fill=1.0,
                                                   base=base, pattern=[[-1, 2 * NS], [0, P]], channel_multiplier=1))
            chain.end()
            pool.wait_ge(w_ready["pool"], 1)
            for s in setup_done.values():
                pool.sem_inc(s, 1)

            def norm():
                c = Chain(pool, pool_chain)
                take(pool, stats_ready)
                c.link(nc.gpsimd.tensor_scalar(nrm[:, 1, :], mv[:, :, 1], LN_EPS, 1.0, ALU.add, ALU.mult))
                c.link(nc.gpsimd.tensor_tensor(nrm[:, 0, :], nrm[:, 1, :], half[:, 0:TT], ALU.pow))
                c.link(nc.gpsimd.tensor_tensor(nrm[:, 1, :], nrm[:, 0, :], nrm[:, 0, :], ALU.mult))
                c.link(nc.gpsimd.tensor_tensor(nrm[:, 1, :], nrm[:, 1, :], mv[:, :, 1], ALU.mult))
                c.link(nc.gpsimd.tensor_scalar(nrm[:, 1, :], nrm[:, 1, :], RMS_EPS, 1.0, ALU.add, ALU.mult))
                c.link(nc.gpsimd.tensor_tensor(nrm[:, 2, :], nrm[:, 1, :], half[:, 0:TT], ALU.pow))
                nc.gpsimd.tensor_tensor(nrm[:, 3, :], nrm[:, 2, :], nrm[:, 0, :], ALU.mult).then_inc(norm_ready, 1)
                c.end()

            def residual(b, p):
                c = Chain(pool, pool_chain)
                take(pool, xn_ready)
                c.link(nc.gpsimd.tensor_tensor(res[:, p], x_sb[:, bass.ds(b * TT, TT), :], xn[:], ALU.add))
                for tt in range(TT):
                    ins = nc.gpsimd.tensor_tensor(res[:, p, tt], res[:, p, tt], out_b[:], ALU.add)
                ins.then_inc(res_ready, 1)
                c.end()

            def prologue():
                norm()
                residual(0, 0)

            def body(b, p, first=False, last=False):
                for m in range(PAIRS):
                    if m == 0 and not last:
                        norm()
                    if m == 5 and not last:
                        residual(b + 1, 1 - p)
                    if m in POOL_PAIRS:
                        k = rank(m)
                        pool.wait_ge(c_sb_ready, k)
                        pool.wait_ge(h_ready, k)
                        for n in range(2):
                            for c in range(DC):
                                ins = nc.gpsimd.tensor_tensor(hc[:, m % 4, n, c], h[:, m % 2, n, c], c_sb[:, n], ALU.mult)
                        ins.then_inc(hc_pool, 1)
                pool.sem_inc(c_sb_ready, -len(POOL_PAIRS))
                pool.sem_inc(h_ready, -len(POOL_PAIRS))

            batches(pool, body, prologue, lambda: None)

        @block.tensor
        def _(pe):
            pe.wait_ge(w_ready["pe"], 1)
            pe.wait_ge(setup_done["pe"], 1)
            pe.sem_inc(t2_free, 1)

            def transpose_z():
                take(pe, z_ready)
                for tt in range(TT):
                    ins = nc.tensor.transpose(t0[:, tt * P:(tt + 1) * P], z[:, tt], ident[:])
                ins.then_inc(zT_ready, 1)

            def project_in():
                take(pe, hT_ready)
                for c in range(DC):
                    ins = nc.tensor.matmul(t1[:, c * T:(c + 1) * T], in_w[:, c * P:(c + 1) * P], hT[:], start=True, stop=True)
                ins.then_inc(x1_ready, 1)
                for c in range(DC):
                    ins = nc.tensor.matmul(t0[:, c * T:(c + 1) * T], in_w[:, (DC + c) * P:(DC + c + 1) * P], hT[:], start=True, stop=True)
                ins.then_inc(g_ready, 1)

            def project_dbc():
                take(pe, xs_ready)
                for c in range(DC):
                    ins = nc.tensor.matmul(t1[:, 0:T], dbc_w[:, c], xs[:, c], start=(c == 0), stop=(c == DC - 1))
                ins.then_inc(dbc_ready, 1)

            def project_delta():
                take(pe, bcd_ready)
                take(pe, t2_free)
                for c in range(DC):
                    ins = nc.tensor.matmul(t2[:, c * T:(c + 1) * T], dup_w[2 * DTR:3 * DTR, c * P:(c + 1) * P],
                                           bcd[2 * DTR:3 * DTR, :], start=True, stop=True)
                ins.then_inc(dup_ready, 1)

            def project_out():
                take(pe, t2_free)
                for tt in range(TT):
                    for c in range(DC):
                        ins = nc.tensor.matmul(t2[:, tt * DM:(tt + 1) * DM], yg[:, c, tt * P:(tt + 1) * P], out_w[:, c],
                                               start=(c == 0), stop=(c == DC - 1))
                ins.then_inc(o_ready, 1)

            def spread(m, p):
                for n in range(2):
                    ins = nc.tensor.matmul(c_ps[m % 2][:, n * T:(n + 1) * T], pick[:, NS + 2 * m + n], bc[:, p], start=True, stop=True)
                ins.then_inc(c_ready, 1)
                for n in range(2):
                    ins = nc.tensor.matmul(b_ps[m % 2][:, n * T:(n + 1) * T], pick[:, 2 * m + n], bc[:, p], start=True, stop=True)
                ins.then_inc(b_ready, 1)

            def wait_hc(m, first=False, ended=False):
                if m in POOL_PAIRS:
                    pe.wait_ge(hc_pool, rank(m))
                elif m == PAIRS - 1:
                    if not first:
                        pe.wait_ge(hc_dve, 1 + (rank(m) if ended else 0))
                else:
                    pe.wait_ge(hc_dve, rank(m) + (0 if first else 1))

            def add_states(m):
                for n in range(2):
                    ins = nc.tensor.matmul(y_ps[:], ident[:], hc[:, m % 4, n].rearrange("p c t -> p (c t)"),
                                           start=(m == 0 and n == 0), stop=(m == PAIRS - 1 and n == 1))
                if m == PAIRS - 1:
                    ins.then_inc(y_ready, 1)

            def prologue():
                transpose_z()
                project_in()
                project_dbc()
                project_delta()
                take(pe, bc_ready)
                spread(0, 0)

            def body(b, p, first=False, last=False):
                for m in range(PAIRS):
                    wait_hc((m - 1) % PAIRS, first)
                    if m == PAIRS - 1 and not last:
                        take(pe, bc_ready)
                        spread(0, 1 - p)
                    elif m < PAIRS - 1:
                        spread(m + 1, p)
                    if m == 1 and not first:
                        take(pe, yg_ready)
                    if m > 0:
                        add_states(m - 1)
                    elif not first:
                        add_states(PAIRS - 1)
                    if m == 1 and not first:
                        project_out()
                    if not last:
                        if m == 1:
                            transpose_z()
                        if m == 2:
                            project_in()
                        if m == 4:
                            project_dbc()
                        if m == 5:
                            project_delta()
                if not last:
                    pe.sem_inc(hc_dve, -(PAIRS - len(POOL_PAIRS) - (1 if first else 0)))
                pe.sem_inc(hc_pool, -len(POOL_PAIRS))

            def epilogue():
                wait_hc(PAIRS - 1, ended=True)
                add_states(PAIRS - 1)
                take(pe, yg_ready)
                project_out()

            batches(pe, body, prologue, epilogue)

        @block.scalar
        def _(act):
            act.wait_ge(w_ready["act"], 1)
            act.wait_ge(setup_done["act"], 1)
            chain = Chain(act, act_chain)
            nc.scalar.preload_act_table_set("natural_log_exp_and_others")
            chain.link(nc.scalar.activation(neg_a[:], neg_a[:], ACT.Exp))
            chain.link(nc.scalar.activation(neg_a[:], neg_a[:], ACT.Copy, scale=-1.0))
            chain.end()

            def scale_hT():
                take(act, zT_ready)
                nc.scalar.activation(hT[:], t0[:, 0:T], ACT.Copy, scale=rms_w[:, 0:1]).then_inc(hT_ready, 1)

            def pad_x():
                take(act, x1_ready)
                for c in range(DC):
                    ins = nc.scalar.activation(xpad[:, c, KC - 1:], t1[:, c * T:(c + 1) * T], ACT.Identity, bias=in_b[:, c:c + 1])
                ins.then_inc(xpad_ready, 1)

            def silus(p):
                take(act, g_ready)
                for c in range(DC):
                    nc.scalar.activation(gate[:, p, c], t0[:, c * T:(c + 1) * T], ACT.Silu, bias=in_b[:, DC + c:DC + c + 1])
                take(act, conv_ready)
                for c in range(DC):
                    ins = nc.scalar.activation(xs[:, c], conv[:, c], ACT.Silu, bias=conv_b[:, c:c + 1])
                ins.then_inc(xs_ready, 1)
                nc.scalar.preload_act_table_set("natural_log_exp_and_others")

            def read_dbc(p):
                take(act, dbc_ready)
                nc.scalar.activation(bcd[:], t1[:, 0:T], ACT.Identity, bias=dbc_b[:, 0:1]).then_inc(bcd_ready, 1)
                nc.scalar.activation(bc[0:2 * NS, p], t1[0:2 * NS, 0:T], ACT.Identity, bias=dbc_b[0:2 * NS, 0:1])
                nc.scalar.activation(bc_hi[64:96], t1[64:96, 0:T], ACT.Identity, bias=dbc_b[64:96, 0:1]).then_inc(bc_hi_ready, 1)

            def softplus():
                c = Chain(act, act_chain)
                take(act, sp_in_ready)
                c.link(nc.scalar.activation(sp[:], sp_in[:], ACT.Abs))
                c.link(nc.scalar.activation(sp[:], sp[:], ACT.Exp, scale=-1.0))
                nc.scalar.activation(sp[:], sp[:], ACT.Ln, bias=1.0).then_inc(sp_ready, 1)
                c.end()

            def decays(m, p):
                for n in range(2):
                    for c in range(DC):
                        ins = nc.scalar.activation(decay[:, m % 2, n, c, 1:T], delta[:, p, c, 1:T], ACT.Exp,
                                                   scale=neg_a[:, c, 2 * m + n:2 * m + n + 1])
                ins.then_inc(decay_ready, 1)
                if m in POOL_PAIRS:
                    nc.scalar.activation(c_sb[:].rearrange("p n t -> p (n t)"), c_ps[m % 2][:], ACT.Copy).then_inc(c_sb_ready, 1)

            def prologue():
                scale_hT()
                pad_x()
                silus(0)
                read_dbc(0)
                softplus()
                take(act, delta_ready)
                take(act, c_ready)
                decays(0, 0)

            def body(b, p, first=False, last=False):
                for m in range(PAIRS):
                    if not last:
                        if m == 1:
                            scale_hT()
                        if m == 2:
                            pad_x()
                        if m == 4:
                            silus(1 - p)
                        if m == 5:
                            read_dbc(1 - p)
                        if m == 6:
                            softplus()
                    if m < PAIRS - 1 or not last:
                        act.wait_ge(c_ready, m + 1)
                    if m == PAIRS - 1 and not last:
                        take(act, delta_ready)
                        decays(0, 1 - p)
                    elif m < PAIRS - 1:
                        decays(m + 1, p)
                if not last:
                    act.sem_inc(c_ready, -PAIRS)

            batches(act, body, prologue, lambda: None)

        @block.vector
        def _(dve):
            dve.wait_ge(w_ready["dve"], 1)
            dve.wait_ge(setup_done["dve"], 1)

            def statistics(b):
                c = Chain(dve, dve_chain)
                for tt in range(TT):
                    ins = nc.vector.bn_stats(stats[:, tt], x_sb[:, bass.ds(b * TT + tt, 1), :].rearrange("p o d -> p (o d)"))
                c.link(ins)
                for tt in range(TT):
                    ins = nc.vector.bn_aggr(mv[:, tt], stats[:, tt])
                ins.then_inc(stats_ready, 1)
                c.end()

            def normalise(b):
                take(dve, norm_ready)
                for tt in range(TT):
                    ins = nc.vector.tensor_scalar(xn[:, tt], x_sb[:, bass.ds(b * TT + tt, 1), :].rearrange("p o d -> p (o d)"), mv[:, tt, 0:1], nrm[:, 0, tt:tt + 1], ALU.subtract, ALU.mult)
                ins.then_inc(xn_ready, 1)
                for tt in range(TT):
                    ins = nc.vector.tensor_scalar(z[:, tt], x_sb[:, bass.ds(b * TT + tt, 1), :].rearrange("p o d -> p (o d)"), mv[:, tt, 0:1], nrm[:, 3, tt:tt + 1], ALU.subtract, ALU.mult)
                ins.then_inc(z_ready, 1)

            def convolve():
                c = Chain(dve, dve_chain)
                take(dve, xpad_ready)
                for ch in range(DC):
                    ins = nc.vector.tensor_scalar(conv[:, ch], xpad[:, ch, 0:T], conv_w[:, ch, 0:1], None, ALU.mult)
                for k in range(1, KC):
                    c.link(ins)
                    for ch in range(DC):
                        ins = nc.vector.scalar_tensor_tensor(conv[:, ch], xpad[:, ch, k:k + T], conv_w[:, ch, k:k + 1], conv[:, ch], ALU.mult, ALU.add)
                ins.then_inc(conv_ready, 1)
                c.end()

            def split_bc(p):
                take(dve, bc_hi_ready)
                nc.vector.tensor_tensor(bc[64:96, p], bcd[64:96], bc_hi[64:96], ALU.subtract).then_inc(bc_ready, 1)

            def read_dup():
                take(dve, dup_ready)
                for c in range(DC):
                    ins = nc.vector.tensor_scalar(sp_in[:, c], t2[:, c * T:(c + 1) * T], dup_b[:, c:c + 1], None, ALU.add)
                ins.then_inc(sp_in_ready, 1)

            def make_delta(p):
                c = Chain(dve, dve_chain)
                take(dve, sp_ready)
                dve.sem_inc(t2_free, 1)
                c.link(nc.vector.scalar_tensor_tensor(delta[:, p], sp_in[:], 0.0, sp[:], ALU.max, ALU.add))
                dve.sem_inc(delta_ready, 1)
                c.link(nc.vector.tensor_tensor(dx[:, p], delta[:, p], xs[:], ALU.mult))
                take(dve, res_ready)
                c.end()

            def gate_y(p):
                take(dve, y_ready)
                nc.vector.tensor_tensor(yg[:].rearrange("p c t -> p (c t)"), y_ps[:], gate[:, p].rearrange("p c t -> p (c t)"), ALU.mult).then_inc(yg_ready, 1)

            def update(b, p):
                take(dve, o_ready)
                nc.vector.tensor_tensor(x_sb[:, bass.ds(b * TT, TT), :], t2[:, 0:TT * DM].rearrange("p (a d) -> p a d", a=TT), res[:, p], ALU.add).then_inc(t2_free, 1)

            def inputs(m, p):
                out = h[:, m % 2]
                b4 = b_ps[m % 2][:].rearrange("p (n c t) -> p n c t", n=2, c=1).to_broadcast([P, 2, DC, T])
                d4 = dx[:, p].rearrange("p (n c) t -> p n c t", n=1).to_broadcast([P, 2, DC, T])
                nc.vector.tensor_tensor(out, b4, d4, ALU.mult).then_inc(core_chain, 1)

            def flat(ap):
                return ap.rearrange("p n c t -> p (n c t)")

            def prologue():
                statistics(0)
                normalise(0)
                convolve()
                split_bc(0)
                read_dup()
                make_delta(0)
                take(dve, b_ready)
                inputs(0, 0)

            def body(b, p, first=False, last=False):
                done = 1
                for m in range(PAIRS):
                    if m == 1 and not first:
                        gate_y(1 - p)
                    if not last:
                        if m == 0:
                            statistics(b + 1)
                        if m == 1:
                            normalise(b + 1)
                        if m == 3:
                            convolve()
                        if m == 5:
                            split_bc(1 - p)
                        if m == 6:
                            read_dup()
                        if m == 7:
                            make_delta(1 - p)
                    if m == 2 and not first:
                        update(b - 1, 1 - p)
                    dve.wait_ge(core_chain, done)
                    dve.wait_ge(decay_ready, m + 1)
                    ins = nc.vector.tensor_tensor_scan(flat(h[:, m % 2]), flat(decay[:, m % 2]), flat(h[:, m % 2]), 0.0, ALU.mult, ALU.add)
                    if m in POOL_PAIRS:
                        ins.then_inc(h_ready, 1)
                    else:
                        ins.then_inc(core_chain, 1)
                        done += 1
                    scanned = done
                    if m < PAIRS - 1 or not last:
                        dve.wait_ge(b_ready, m + 1)
                        inputs((m + 1) % PAIRS, p if m < PAIRS - 1 else 1 - p)
                        done += 1
                    if m not in POOL_PAIRS:
                        dve.wait_ge(core_chain, scanned)
                        c4 = c_ps[m % 2][:].rearrange("p (n c t) -> p n c t", n=2, c=1).to_broadcast([P, 2, DC, T])
                        nc.vector.tensor_tensor(hc[:, m % 4], h[:, m % 2], c4, ALU.mult).then_inc(hc_dve, 1)
                dve.sem_inc(decay_ready, -PAIRS)
                if not last:
                    dve.sem_inc(b_ready, -PAIRS)
                    dve.sem_inc(core_chain, 1 - done)

            def epilogue():
                gate_y((NB - 1) % 2)
                update(NB - 1, (NB - 1) % 2)

            batches(dve, body, prologue, epilogue)


class ExpertWeights:

    def __init__(self, nc, ctx):
        def sb(name, shape, dt=FP16):
            return ctx.enter_context(nc.sbuf_tensor("ew_" + name, shape, dt))

        self.gate_up = [sb(f"gate_up{i}", [P, NE + 1, 2, P]) for i in range(2)]
        self.down = [sb(f"down{i}", [P, NE + 1, DM]) for i in range(2)]
        self.router = [sb(f"router{i}", [P, NE]) for i in range(2)]
        self.bias = sb("bias", [P, NE], FP32)
        self.pick = sb("pick", [4 * NE, NE, P])


def split_expert_weights(nc, ew, w):
    ctx = ExitStack()
    with ctx:
        def sb(name, shape):
            return ctx.enter_context(nc.sbuf_tensor("s_" + name, shape, FP32))

        raw = [sb("gate_up", [P, NE + 1, 2, P]), sb("down", [P, NE + 1, DM]), sb("router", [P, NE])]
        halves = [ew.gate_up, ew.down, ew.router]
        loaded = ctx.enter_context(nc.semaphore("s_loaded"))
        upper = ctx.enter_context(nc.semaphore("s_upper"))
        made = ctx.enter_context(nc.semaphore("s_made"))
        block = ctx.enter_context(nc.Block())

        @block.sync
        def _(sp):
            for dst, name in zip(raw, ("gate_up", "down", "router")):
                sp.dma_start(dst[:], w[name]).then_inc(loaded, 16)
            sp.dma_start(ew.bias[:], w["expert_bias"]).then_inc(loaded, 16)
            sp.wait_ge(loaded, 64)

        @block.scalar
        def _(act):
            act.wait_ge(loaded, 64)
            for src, dst in zip(raw, halves):
                nc.scalar.activation(dst[0][:], src[:], ACT.Copy).then_inc(upper, 1)

        @block.vector
        def _(dve):
            for n, (src, dst) in enumerate(zip(raw, halves)):
                dve.wait_ge(upper, n + 1)
                nc.vector.tensor_tensor(dst[1][:], src[:], dst[0][:], ALU.subtract)

        @block.gpsimd
        def _(pool):
            nc.gpsimd.memset(ew.pick[:], 0.0).then_inc(made, 1)
            for n, base in enumerate((0, -2 * NE)):
                pool.wait_ge(made, n + 1)
                nc.gpsimd.affine_select(out=ew.pick[:], in_=ew.pick[:], compare_op=ALU.not_equal, fill=1.0, base=base,
                                        pattern=[[-1, NE], [0, P]], channel_multiplier=1).then_inc(made, 1)


def expert_layer(nc, sems, layer, x_sb, ew, ident, half):
    ctx = ExitStack()
    with ctx:
        tag = f"e{layer}_"

        def sb(name, shape, dt=FP32):
            return ctx.enter_context(nc.sbuf_tensor(tag + name, shape, dt))

        def pb(name):
            return ctx.enter_context(nc.psum_tensor(tag + name, [P, 512], FP32))

        def sem(name):
            return sems.enter_context(nc.semaphore(tag + name))

        NTQ = QC // P
        STEPS = NE + 1
        RING = 4

        stats = sb("stats", [P, NTQ, 6])
        mv = sb("mv", [P, NTQ, 2])
        nrm = sb("nrm", [P, 2, NTQ])
        xn = sb("xn", [P, NTQ, DM])
        x_hi, x_lo = sb("x_hi", [P, 2, QC], FP16), sb("x_lo", [P, 2, QC], FP16)
        th = sb("th", [P, NTQ, NE])
        score = sb("score", [P, NTQ, NE])
        sel = sb("sel", [P, NTQ, NE])
        top = sb("top", [P, NTQ, TOPK])
        left = sb("left", [P, NTQ, NE])
        chosen = sb("chosen", [P, NTQ, NE])
        total = sb("total", [P, 2, NTQ])
        comb = sb("comb", [P, NTQ, 4 * NE])
        c_hi = sb("c_hi", [4 * NE, QC], FP16)
        cT = sb("cT", [4 * NE, 2, QC], FP16)
        s = sb("s", [P, 2, QC])
        su = sb("su", [P, 2, QC])
        h = sb("h", [P, RING + 1, QC])
        h_hi, h_lo = sb("h_hi", [P, RING + 1, QC], FP16), sb("h_lo", [P, RING + 1, QC], FP16)
        yT = sb("yT", [P, QC])

        g_ps, u_ps, c_ps = [pb("g0"), pb("g1")], [pb("u0"), pb("u1")], [pb("c0"), pb("c1")]
        y_ps, t_ps = pb("y"), pb("t")

        zeroed = {e: sem("zeroed_" + e) for e in ("dve",)}
        pool_chain, dve_chain, core_chain = sem("pool_chain"), sem("dve_chain"), sem("core_chain")
        stats_ready, norm_ready, xn_ready, xT_ready = (sem(n) for n in ("stats_ready", "norm_ready", "xn_ready", "xT_ready"))
        x_hi_ready, x_ready, gates_ready, th_ready = (sem(n) for n in ("x_hi_ready", "x_ready", "gates_ready", "th_ready"))
        comb_ready, combT_ready, c_hi_ready, cT_ready = (sem(n) for n in ("comb_ready", "combT_ready", "c_hi_ready", "cT_ready"))
        g_ready, u_ready, s_ready, h_ready, h_hi_ready, h_lo_ready = (sem(n) for n in ("g_ready", "u_ready", "s_ready", "h_ready", "h_hi_ready", "h_lo_ready"))
        banks_free = sem("banks_free")
        y_ready, yT_ready, o_ready = sem("y_ready"), sem("yT_ready"), sem("o_ready")

        def place(e):
            return e % RING if e < NE else RING

        def chunks(eng, body, prologue, epilogue):
            prologue()
            body(0, 0, first=True)
            with eng.Fori(0, NQ // 2 - 1) as i:
                body(i * 2 + 1, 1)
                body(i * 2 + 2, 0)
            body(NQ - 1, (NQ - 1) % 2, last=True)
            epilogue()

        def tile(q, tt):
            return x_sb[:, bass.ds(q * NTQ + tt, 1), :].rearrange("p o d -> p (o d)")

        block = ctx.enter_context(nc.Block())

        @block.gpsimd
        def _(pool):
            nc.gpsimd.memset(comb[:], 0.0).then_inc(zeroed["dve"], 1)

            def norm():
                c = Chain(pool, pool_chain)
                take(pool, stats_ready)
                c.link(nc.gpsimd.tensor_scalar(nrm[:, 1], mv[:, :, 1], LN_EPS, 1.0, ALU.add, ALU.mult))
                nc.gpsimd.tensor_tensor(nrm[:, 0], nrm[:, 1], half[:, 0:NTQ], ALU.pow).then_inc(norm_ready, 1)
                c.end()

            def lower(e):
                pool.wait_ge(h_hi_ready, e + 1)
                k = place(e)
                nc.gpsimd.tensor_tensor(h_lo[:, k], h[:, k], h_hi[:, k], ALU.subtract).then_inc(h_lo_ready, 1)

            def body(q, p, first=False, last=False):
                for e in range(STEPS):
                    if e == 5 and not last:
                        norm()
                    lower(e)
                pool.sem_inc(h_hi_ready, -STEPS)

            chunks(pool, body, norm, lambda: None)

        @block.tensor
        def _(pe):
            def transpose_x():
                take(pe, xn_ready)
                for tt in range(NTQ):
                    ins = nc.tensor.transpose(t_ps[:, tt * P:(tt + 1) * P], xn[:, tt], ident[:])
                ins.then_inc(xT_ready, 1)

            def route(p):
                take(pe, x_ready)
                for tt in range(NTQ):
                    own = slice(tt * P, (tt + 1) * P)
                    for n, (a, r) in enumerate(((x_hi, 0), (x_hi, 1), (x_lo, 0))):
                        ins = nc.tensor.matmul(t_ps[:, tt * NE:(tt + 1) * NE], a[:, p, own], ew.router[r][:], start=(n == 0), stop=(n == 2))
                ins.then_inc(gates_ready, 1)

            def transpose_comb():
                take(pe, comb_ready)
                for tt in range(NTQ):
                    ins = nc.tensor.transpose(t_ps[0:4 * NE, tt * P:(tt + 1) * P], comb[:, tt], ident[:])
                ins.then_inc(combT_ready, 1)

            def up(e, p, first):
                bank = (e + p) % 2
                if not first or e >= 2:
                    pe.wait_ge(banks_free, e - 1 if first else e + 1)
                for side, ps, ready in ((0, g_ps, g_ready), (1, u_ps, None)):
                    for n, (r, a) in enumerate(((0, x_hi), (0, x_lo), (1, x_hi))):
                        ins = nc.tensor.matmul(ps[bank][:], ew.gate_up[r][:, e, side], a[:, p], start=(n == 0), stop=(n == 2))
                    if ready:
                        ins.then_inc(ready, 1)
                if e < NE:
                    ins = nc.tensor.matmul(c_ps[bank][:], ew.pick[:, e], cT[:, p], start=True, stop=True)
                ins.then_inc(u_ready, 1)

            def down(e):
                for n, (r, a) in enumerate(((0, h_hi), (0, h_lo), (1, h_hi))):
                    ins = nc.tensor.matmul(y_ps[:], ew.down[r][:, e], a[:, place(e)], start=(e == 0 and n == 0), stop=(e == NE and n == 2))
                if e == NE:
                    ins.then_inc(y_ready, 1)

            def transpose_y():
                for tt in range(NTQ):
                    ins = nc.tensor.transpose(t_ps[:, tt * P:(tt + 1) * P], yT[:, tt * P:(tt + 1) * P], ident[:])
                ins.then_inc(o_ready, 1)

            def prologue():
                transpose_x()
                route(0)
                transpose_comb()
                take(pe, cT_ready)

            def body(q, p, first=False, last=False):
                for e in range(STEPS):
                    up(e, p, first)
                    if e == 3 and not first:
                        take(pe, yT_ready)
                        transpose_y()
                    if e >= 3 or not first:
                        pe.wait_ge(h_lo_ready, e - 2 if first else e + 1)
                        down((e - 3) % STEPS)
                    if not last:
                        if e == 7:
                            transpose_x()
                        if e == 9:
                            route(1 - p)
                        if e == 13:
                            transpose_comb()
                        if e == 16:
                            take(pe, cT_ready)
                if not last:
                    pe.sem_inc(banks_free, -(STEPS - 2 if first else STEPS))
                    pe.sem_inc(h_lo_ready, -(STEPS - 3 if first else STEPS))

            def epilogue():
                for n in range(3):
                    pe.wait_ge(h_lo_ready, STEPS + n + 1)
                    down(STEPS - 3 + n)
                take(pe, yT_ready)
                transpose_y()

            chunks(pe, body, prologue, epilogue)

        @block.scalar
        def _(act):
            nc.scalar.preload_act_table(ACT.Silu)

            def upper_x(p):
                take(act, xT_ready)
                nc.scalar.activation(x_hi[:, p], t_ps[:], ACT.Copy).then_inc(x_hi_ready, 1)

            def squash():
                take(act, gates_ready)
                nc.scalar.activation(th[:].rearrange("p a e -> p (a e)"), t_ps[:, 0:NTQ * NE], ACT.Tanh, scale=0.5).then_inc(th_ready, 1)

            def upper_c(p):
                take(act, combT_ready)
                nc.scalar.activation(cT[0:2 * NE, p], t_ps[0:2 * NE, :], ACT.Copy)
                nc.scalar.activation(c_hi[2 * NE:4 * NE], t_ps[2 * NE:4 * NE, :], ACT.Copy).then_inc(c_hi_ready, 1)

            def silu(e, p):
                act.wait_ge(g_ready, e + 1)
                nc.scalar.activation(s[:, (e + p) % 2], g_ps[(e + p) % 2][:], ACT.Silu).then_inc(s_ready, 1)

            def upper_h(e, n):
                act.wait_ge(h_ready, n)
                act.sem_inc(banks_free, 1)
                nc.scalar.activation(h_hi[:, place(e)], h[:, place(e)], ACT.Copy).then_inc(h_hi_ready, 1)

            def read_y():
                take(act, y_ready)
                nc.scalar.activation(yT[:], y_ps[:], ACT.Copy).then_inc(yT_ready, 1)

            def prologue():
                upper_x(0)
                squash()
                upper_c(0)

            def body(q, p, first=False, last=False):
                for e in range(STEPS):
                    silu(e, p)
                    if e > 0:
                        upper_h(e - 1, e if first else e + 1)
                    elif not first:
                        upper_h(NE, 1)
                    if e == 3 and not first:
                        read_y()
                    if not last:
                        if e == 8:
                            upper_x(1 - p)
                        if e == 10:
                            squash()
                        if e == 14:
                            upper_c(1 - p)
                act.sem_inc(g_ready, -STEPS)
                if not last:
                    act.sem_inc(h_ready, -(STEPS - 1 if first else STEPS))

            def epilogue():
                upper_h(NE, STEPS + 1)
                read_y()

            chunks(act, body, prologue, epilogue)

        @block.vector
        def _(dve):
            take(dve, zeroed["dve"])

            def statistics(q):
                c = Chain(dve, dve_chain)
                for tt in range(NTQ):
                    ins = nc.vector.bn_stats(stats[:, tt], tile(q, tt))
                c.link(ins)
                for tt in range(NTQ):
                    ins = nc.vector.bn_aggr(mv[:, tt], stats[:, tt])
                ins.then_inc(stats_ready, 1)
                c.end()

            def normalise(q):
                take(dve, norm_ready)
                for tt in range(NTQ):
                    ins = nc.vector.tensor_scalar(xn[:, tt], tile(q, tt), mv[:, tt, 0:1], nrm[:, 0, tt:tt + 1], ALU.subtract, ALU.mult)
                ins.then_inc(xn_ready, 1)

            def lower_x(p):
                take(dve, x_hi_ready)
                nc.vector.tensor_tensor(x_lo[:, p], t_ps[:], x_hi[:, p], ALU.subtract).then_inc(x_ready, 1)

            def choose():
                c = Chain(dve, dve_chain)
                take(dve, th_ready)
                c.link(nc.vector.tensor_scalar(score[:], th[:], 1.0, 0.5, ALU.add, ALU.mult))
                c.link(nc.vector.tensor_tensor(sel[:], score[:], ew.bias[:].rearrange("p (o e) -> p o e", o=1).to_broadcast([P, NTQ, NE]), ALU.add))
                for tt in range(NTQ):
                    ins = nc.vector.max(top[:, tt], sel[:, tt])
                c.link(ins)
                for tt in range(NTQ):
                    ins = nc.vector.match_replace(left[:, tt], top[:, tt], sel[:, tt], TAKEN)
                c.link(ins)
                c.link(nc.vector.scalar_tensor_tensor(chosen[:], left[:], TAKEN, score[:], ALU.is_equal, ALU.mult))
                c.link(nc.vector.tensor_reduce(total[:, 0], chosen[:], AX.X, ALU.add))
                c.link(nc.vector.reciprocal(total[:, 1], total[:, 0]))
                for k in range(2):
                    r = total[:, 1].rearrange("p (a o) -> p a o", o=1).to_broadcast([P, NTQ, NE])
                    ins = nc.vector.scalar_tensor_tensor(comb[:, :, 2 * k * NE:(2 * k + 1) * NE], chosen[:], ROUTE_SCALE, r, ALU.mult, ALU.mult)
                ins.then_inc(comb_ready, 1)
                c.end()

            def lower_c(p):
                take(dve, c_hi_ready)
                rows = slice(2 * NE, 4 * NE)
                nc.vector.tensor_tensor(cT[rows, p], t_ps[rows, :], c_hi[rows], ALU.subtract).then_inc(cT_ready, 1)

            def hidden(e, p):
                bank = (e + p) % 2
                dve.wait_ge(s_ready, e + 1)
                dve.wait_ge(u_ready, e + 1)
                if e == NE:
                    nc.vector.tensor_tensor(h[:, place(e)], s[:, bank], u_ps[bank][:], ALU.mult).then_inc(h_ready, 1)
                    return
                nc.vector.tensor_tensor(su[:, bank], s[:, bank], u_ps[bank][:], ALU.mult).then_inc(core_chain, 1)
                dve.wait_ge(core_chain, e + 1)
                nc.vector.tensor_tensor(h[:, place(e)], su[:, bank], c_ps[bank][:], ALU.mult).then_inc(h_ready, 1)

            def update(q):
                take(dve, o_ready)
                xs = x_sb[:, bass.ds(q * NTQ, NTQ), :]
                nc.vector.tensor_tensor(xs, t_ps[:].rearrange("p (a d) -> p a d", a=NTQ), xs, ALU.add)

            def prologue():
                statistics(0)
                normalise(0)
                lower_x(0)
                choose()
                lower_c(0)

            def body(q, p, first=False, last=False):
                for e in range(STEPS):
                    hidden(e, p)
                    if e == 4 and not first:
                        update(q - 1)
                    if not last:
                        if e == 4:
                            statistics(q + 1)
                        if e == 6:
                            normalise(q + 1)
                        if e == 8:
                            lower_x(1 - p)
                        if e == 11:
                            choose()
                        if e == 15:
                            lower_c(1 - p)
                dve.sem_inc(s_ready, -STEPS)
                dve.sem_inc(u_ready, -STEPS)
                dve.sem_inc(core_chain, -NE)

            chunks(dve, body, prologue, lambda: update(NQ - 1))


def attention_layer(nc, sems, x_sb, w, ident, ident16, half):
    ctx = ExitStack()
    with ctx:
        def sb(name, shape, dt=FP32):
            return ctx.enter_context(nc.sbuf_tensor("a_" + name, shape, dt))

        def pb(name, width=512):
            return ctx.enter_context(nc.psum_tensor("a_" + name, [P, width], FP32))

        def sem(name):
            return sems.enter_context(nc.semaphore("a_" + name))

        W = NH * DH
        SLOT = 32

        qkvg_w = sb("qkvg_w", [P, 4 * W])
        qkvg_b = sb("qkvg_b", [P, 4 * W])
        out_w = sb("out_w", [P, DM])
        out_b = sb("out_b", [P, DM])

        stats = sb("stats", [P, TT, 6])
        mv = sb("mv", [P, TT, 2])
        nrm = sb("nrm", [P, 4, TT])
        xn = sb("xn", [P, TT, DM])
        z = sb("z", [P, TT, DM])
        zT = sb("zT", [P, T])
        res = sb("res", [P, 2, TT, DM])
        qkvg = sb("qkvg", [P, 2, TT, 4 * W])
        qk = sb("qk", [P, TT, 2, NH, SLOT], FP16)
        square = sb("square", [P, TT, 2 * W])
        norms = sb("norms", [P, 2, TT, 2 * NH])
        qkT = sb("qkT", [P, 2, HG, T], FP16)
        v = sb("v", [P, 2, TT, NH, SLOT])
        d = sb("d", [P, 2, NH, TT * T])
        avT = sb("avT", [P, HG, T])
        den = sb("den", [P, 2, TT, NH])
        o = sb("o", [P, TT, W])
        oT = sb("oT", [P, T])

        near = sb("near", [P, 1])

        s_ps = [pb("s0"), pb("s1")]
        av_ps = [pb("av0"), pb("av1")]
        t_ps = [pb("t0"), pb("t1")]
        u_ps = pb("u", 1024)

        loaded = sem("loaded")
        near_made = sem("near_made")
        w_ready = {e: sem("w_ready_" + e) for e in ("dve", "pool", "pe")}
        made = {e: sem("made_" + e) for e in ("dve", "pe")}
        pool_chain, dve_chain, act_chain, d_chain = sem("pool_chain"), sem("dve_chain"), sem("act_chain"), sem("d_chain")
        stats_ready, norm_ready, z_ready, zT_ps_ready, zT_ready = (sem(n) for n in ("stats_ready", "norm_ready", "z_ready", "zT_ps_ready", "zT_ready"))
        p_ready, qkvg_ready, hi_ready, sq_ready, v_ready, res_ready = (sem(n) for n in ("p_ready", "qkvg_ready", "hi_ready", "sq_ready", "v_ready", "res_ready"))
        qk_ready, qkT_ps_ready, qkT_ready = sem("qk_ready"), sem("qkT_ps_ready"), sem("qkT_ready")
        s_ready, s_free, d_ready, w_done = sem("s_ready"), sem("s_free"), sem("d_ready"), sem("w_done")
        av_ready, avT_ready, u_ready, o_ready, oT_ps_ready, oT_ready, y_ready = (
            sem(n) for n in ("av_ready", "avT_ready", "u_ready", "o_ready", "oT_ps_ready", "oT_ready", "y_ready"))

        def batches(eng, body, prologue, epilogue):
            prologue()
            body(0, 0, first=True)
            with eng.Fori(0, NB // 2 - 1) as i:
                body(i * 2 + 1, 1)
                body(i * 2 + 2, 0)
            body(NB - 1, (NB - 1) % 2, last=True)
            epilogue()

        def tile(b, tt):
            return x_sb[:, bass.ds(b * TT + tt, 1), :].rearrange("p o d -> p (o d)")

        def heads(p, part):
            return qkvg[:, p, :, part * W:(part + 1) * W].rearrange("p a (h d) -> p a h d", d=DH)

        block = ctx.enter_context(nc.Block())

        @block.sync
        def _(sp):
            for dst, name in ((qkvg_w, "qkvg_w"), (qkvg_b, "qkvg_b"), (out_w, "attn_out_w"), (out_b, "attn_out_b")):
                sp.dma_start(dst[:], w[name]).then_inc(loaded, 16)
            sp.wait_ge(loaded, 64)
            for s in w_ready.values():
                sp.sem_inc(s, 1)

        @block.gpsimd
        def _(pool):
            chain = Chain(pool, pool_chain)
            nc.gpsimd.memset(qk[:], 0.0)
            chain.link(nc.gpsimd.memset(v[:], 0.0))
            nc.gpsimd.memset(qk[:, :, 0, :, 26:28], 1.0)
            nc.gpsimd.memset(qk[:, :, 1, :, 24:26], 1.0)
            chain.link(nc.gpsimd.memset(v[:, :, :, :, DH:DH + 1], 1.0))
            chain.end()
            for s in made.values():
                pool.sem_inc(s, 1)
            pool.wait_ge(w_ready["pool"], 1)

            def norm():
                c = Chain(pool, pool_chain)
                take(pool, stats_ready)
                c.link(nc.gpsimd.tensor_scalar(nrm[:, 1], mv[:, :, 1], LN_EPS, 1.0, ALU.add, ALU.mult))
                c.link(nc.gpsimd.tensor_tensor(nrm[:, 0], nrm[:, 1], half[:, 0:TT], ALU.pow))
                c.link(nc.gpsimd.tensor_tensor(nrm[:, 1], nrm[:, 0], nrm[:, 0], ALU.mult))
                c.link(nc.gpsimd.tensor_tensor(nrm[:, 1], nrm[:, 1], mv[:, :, 1], ALU.mult))
                c.link(nc.gpsimd.tensor_scalar(nrm[:, 1], nrm[:, 1], LN_EPS, 1.0, ALU.add, ALU.mult))
                c.link(nc.gpsimd.tensor_tensor(nrm[:, 2], nrm[:, 1], half[:, 0:TT], ALU.pow))
                nc.gpsimd.tensor_tensor(nrm[:, 3], nrm[:, 2], nrm[:, 0], ALU.mult).then_inc(norm_ready, 1)
                c.end()

            def pack(b, p):
                c = Chain(pool, pool_chain)
                take(pool, qkvg_ready)
                for side in range(2):
                    ins = nc.gpsimd.tensor_scalar(qk[:, :, side, :, 0:DH], heads(p, side), 1.0, 1.0, ALU.mult, ALU.mult)
                ins.then_inc(hi_ready, 1)
                for side, at in ((0, 2 * DH), (1, DH)):
                    nc.gpsimd.tensor_scalar(qk[:, :, side, :, at:at + DH], heads(p, side), 1.0, 1.0, ALU.mult, ALU.mult)
                qk_cols = qkvg[:, p, :, 0:2 * W]
                nc.gpsimd.tensor_tensor(square[:], qk_cols, qk_cols, ALU.mult).then_inc(sq_ready, 1)
                nc.gpsimd.tensor_scalar(v[:, p, :, :, 0:DH], heads(p, 2), 1.0, 1.0, ALU.mult, ALU.mult).then_inc(v_ready, 1)
                c.link(nc.gpsimd.tensor_tensor(res[:, p], x_sb[:, bass.ds(b * TT, TT), :], xn[:], ALU.add))
                for tt in range(TT):
                    ins = nc.gpsimd.tensor_tensor(res[:, p, tt], res[:, p, tt], out_b[:], ALU.add)
                ins.then_inc(res_ready, 1)
                c.end()

            def prologue():
                norm()
                pack(0, 0)

            def body(b, p, first=False, last=False):
                if not last:
                    norm()
                    pack(b + 1, 1 - p)

            batches(pool, body, prologue, lambda: None)

        @block.tensor
        def _(pe):
            pe.wait_ge(w_ready["pe"], 1)
            pe.wait_ge(made["pe"], 1)
            pe.sem_inc(s_free, 2)

            def transpose_z():
                take(pe, z_ready)
                for tt in range(TT):
                    ins = nc.tensor.transpose(t_ps[0][:, tt * P:(tt + 1) * P], z[:, tt], ident[:])
                ins.then_inc(zT_ps_ready, 1)

            def project():
                take(pe, zT_ready)
                for tt in range(TT):
                    nc.tensor.matmul(t_ps[tt][:], zT[:, tt * P:(tt + 1) * P], qkvg_w[:], start=True, stop=True).then_inc(p_ready, 1)

            def transpose_qk():
                take(pe, qk_ready)
                for tt in range(TT):
                    t16 = t_ps[tt][:].bitcast(FP16)
                    for side in range(2):
                        for g in range(HG):
                            k = side * HG + g
                            ins = nc.tensor.transpose(t16[:, k * P:(k + 1) * P], qk[:, tt, side, 4 * g:4 * g + 4].rearrange("p h k -> p (h k)"), ident16[:])
                    ins.then_inc(qkT_ps_ready, 1)

            def score(h):
                g, j = divmod(h, 4)
                rows = slice(SLOT * j, SLOT * (j + 1))
                pe.wait_ge(s_free, h + 1)
                for kc in range(TT):
                    ins = nc.tensor.matmul(s_ps[h % 2][:, kc * T:(kc + 1) * T], qkT[rows, 1, g, kc * P:(kc + 1) * P], qkT[rows, 0, g, :], start=True, stop=True)
                ins.then_inc(s_ready, 1)

            def scores(first, last):
                for h in range(first, last):
                    score(h)

            def weigh(g, p):
                pe.wait_ge(w_done, g + 1)
                for kc in range(TT):
                    for j in range(4):
                        h = 4 * g + j
                        ins = nc.tensor.matmul(av_ps[g // 2][SLOT * j:SLOT * (j + 1), (g % 2) * T:(g % 2 + 1) * T],
                                               v[:, p, kc, h], d[:, p, h, kc * T:(kc + 1) * T], start=(kc == 0), stop=(kc == TT - 1))
                if g % 2:
                    ins.then_inc(av_ready, 1)

            def transpose_av():
                take(pe, avT_ready)
                for tt in range(TT):
                    for g in range(HG):
                        ins = nc.tensor.transpose(u_ps[:, tt * 512 + g * P:tt * 512 + (g + 1) * P], avT[:, g, tt * P:(tt + 1) * P], ident[:])
                ins.then_inc(u_ready, 1)

            def transpose_o():
                take(pe, o_ready)
                for tt in range(TT):
                    ins = nc.tensor.transpose(u_ps[:, tt * P:(tt + 1) * P], o[:, tt], ident[:])
                ins.then_inc(oT_ps_ready, 1)

            def project_out():
                take(pe, oT_ready)
                for tt in range(TT):
                    ins = nc.tensor.matmul(u_ps[:, 512 + tt * DM:512 + (tt + 1) * DM], oT[:, tt * P:(tt + 1) * P], out_w[:], start=True, stop=True)
                ins.then_inc(y_ready, 1)

            def prologue():
                transpose_z()
                project()
                transpose_qk()
                take(pe, qkT_ready, TT)
                scores(0, NH)
                pe.sem_inc(s_free, -NH)

            def body(b, p, first=False, last=False):
                if not first:
                    transpose_av()
                if not last:
                    transpose_z()
                if not first:
                    transpose_o()
                if not last:
                    project()
                if not first:
                    project_out()
                if not last:
                    transpose_qk()
                    take(pe, qkT_ready, TT)
                take(pe, v_ready)
                for g, upto in enumerate((5, 11, NH, NH)):
                    if not last:
                        scores((0, 5, 11, NH)[g], upto)
                    weigh(g, p)
                pe.sem_inc(w_done, -HG)
                if not last:
                    pe.sem_inc(s_free, -NH)

            def epilogue():
                transpose_av()
                transpose_o()
                project_out()

            batches(pe, body, prologue, epilogue)

        @block.scalar
        def _(act):
            def body(b, p, first=False, last=False):
                def group(g):
                    return d[:, p, 4 * g:4 * g + 4].rearrange("p h k -> p (h k)")

                for g in range(HG):
                    act.wait_ge(d_ready, g + 1)
                    nc.scalar.activation(group(g), group(g), ACT.Sqrt).then_inc(act_chain, 1)
                act.sem_inc(d_ready, -HG)
                nc.scalar.preload_act_table_set("natural_log_exp_and_others")
                for g in range(HG + 1):
                    if g < HG:
                        act.wait_ge(act_chain, g + 1)
                        nc.scalar.activation(group(g), group(g), ACT.Ln, bias=near[:, 0:1]).then_inc(act_chain, 1)
                    if g > 0:
                        act.wait_ge(act_chain, HG + g)
                        nc.scalar.activation(group(g - 1), group(g - 1), ACT.Exp, scale=-2.0).then_inc(w_done, 1)
                act.sem_inc(act_chain, -2 * HG)

            act.wait_ge(near_made, 1)
            batches(act, body, lambda: None, lambda: None)

        @block.vector
        def _(dve):
            nc.vector.memset(near[:], SHEP_EPS).then_inc(near_made, 1)
            dve.wait_ge(w_ready["dve"], 1)
            dve.wait_ge(made["dve"], 1)

            def statistics(b):
                c = Chain(dve, dve_chain)
                for tt in range(TT):
                    ins = nc.vector.bn_stats(stats[:, tt], tile(b, tt))
                c.link(ins)
                for tt in range(TT):
                    ins = nc.vector.bn_aggr(mv[:, tt], stats[:, tt])
                ins.then_inc(stats_ready, 1)
                c.end()

            def normalise(b):
                take(dve, norm_ready)
                for out, k in ((xn, 0), (z, 3)):
                    for tt in range(TT):
                        ins = nc.vector.tensor_scalar(out[:, tt], tile(b, tt), mv[:, tt, 0:1], nrm[:, k, tt:tt + 1], ALU.subtract, ALU.mult)
                ins.then_inc(z_ready, 1)

            def read_zT():
                take(dve, zT_ps_ready)
                nc.vector.tensor_copy(zT[:], t_ps[0][:, 0:T]).then_inc(zT_ready, 1)

            def read_qkvg(p):
                for tt in range(TT):
                    dve.wait_ge(p_ready, tt + 1)
                    ins = nc.vector.tensor_tensor(qkvg[:, p, tt], t_ps[tt][:], qkvg_b[:], ALU.add)
                dve.sem_inc(p_ready, -TT)
                c = Chain(dve, dve_chain)
                c.link(ins)
                dve.sem_inc(qkvg_ready, 1)
                c.end()

            def split_qk(p):
                c = Chain(dve, dve_chain)
                take(dve, hi_ready)
                for side, at in ((0, DH), (1, 2 * DH)):
                    nc.vector.tensor_tensor(qk[:, :, side, :, at:at + DH], heads(p, side), qk[:, :, side, :, 0:DH], ALU.subtract)
                take(dve, sq_ready)
                c.link(nc.vector.tensor_reduce(norms[:, 0], square[:].rearrange("p a (h d) -> p a h d", d=DH), AX.X, ALU.add))
                c.link(nc.vector.tensor_scalar(norms[:, 1], norms[:, 0], -0.5, None, ALU.mult))
                for side, at in ((0, 24), (1, 26)):
                    ins = nc.vector.tensor_copy(qk[:, :, side, :, at], norms[:, 1, :, side * NH:(side + 1) * NH])
                c.link(ins)
                for side, at in ((0, 24), (1, 26)):
                    ins = nc.vector.tensor_tensor(qk[:, :, side, :, at + 1], norms[:, 1, :, side * NH:(side + 1) * NH], qk[:, :, side, :, at], ALU.subtract)
                ins.then_inc(qk_ready, 1)
                c.end()

            def read_qkT():
                for tt in range(TT):
                    dve.wait_ge(qkT_ps_ready, tt + 1)
                    nc.vector.tensor_copy(qkT[:, :, :, tt * P:(tt + 1) * P].rearrange("p s g t -> p (s g) t"),
                                          t_ps[tt][:].bitcast(FP16).rearrange("p (k t) -> p k t", t=P)).then_inc(qkT_ready, 1)
                dve.sem_inc(qkT_ps_ready, -TT)

            def distances(p):
                for h in range(NH + 1):
                    if h < NH:
                        dve.wait_ge(s_ready, h + 1)
                        nc.vector.tensor_scalar(d[:, p, h], s_ps[h % 2][:], -2.0, 0.0, ALU.mult, ALU.max).then_inc(d_chain, 1)
                    if h > 0:
                        dve.wait_ge(d_chain, h)
                        dve.sem_inc(s_free, 1)
                        if h % 4 == 0:
                            dve.sem_inc(d_ready, 1)
                dve.sem_inc(s_ready, -NH)
                dve.sem_inc(d_chain, -NH)

            def read_av():
                take(dve, av_ready, 2)
                for k in range(2):
                    ins = nc.vector.tensor_copy(avT[:, 2 * k:2 * k + 2].rearrange("p g t -> p (g t)"), av_ps[k][:])
                ins.then_inc(avT_ready, 1)

            def norm_and_gate(p):
                c = Chain(dve, dve_chain)
                take(dve, u_ready)
                u = u_ps[:].rearrange("p (a h k) -> p a h k", a=TT, k=SLOT)
                oh = o[:].rearrange("p a (h d) -> p a h d", d=DH)
                c.link(nc.vector.tensor_scalar(den[:, 0], u[:, :, :, DH], SHEP_EPS, None, ALU.add))
                c.link(nc.vector.reciprocal(den[:, 1], den[:, 0]))
                c.link(nc.vector.tensor_tensor(oh, u[:, :, :, 0:DH], den[:, 1].rearrange("p a (h o) -> p a h o", o=1).to_broadcast([P, TT, NH, DH]), ALU.mult))
                nc.vector.tensor_tensor(oh, oh, heads(p, 3), ALU.mult).then_inc(o_ready, 1)
                c.end()

            def read_oT():
                take(dve, oT_ps_ready)
                nc.vector.tensor_copy(oT[:], u_ps[:, 0:T]).then_inc(oT_ready, 1)

            def update(b, p):
                take(dve, y_ready)
                take(dve, res_ready)
                nc.vector.tensor_tensor(x_sb[:, bass.ds(b * TT, TT), :], u_ps[:, 512:512 + TT * DM].rearrange("p (a d) -> p a d", a=TT), res[:, p], ALU.add)

            def prologue():
                statistics(0)
                normalise(0)
                read_zT()
                read_qkvg(0)
                split_qk(0)
                read_qkT()
                distances(0)

            def body(b, p, first=False, last=False):
                if not last:
                    statistics(b + 1)
                if not first:
                    read_av()
                if not last:
                    normalise(b + 1)
                if not first:
                    norm_and_gate(1 - p)
                if not last:
                    read_zT()
                if not first:
                    read_oT()
                    update(b - 1, 1 - p)
                if not last:
                    read_qkvg(1 - p)
                    split_qk(1 - p)
                    read_qkT()
                    distances(1 - p)

            def epilogue():
                read_av()
                norm_and_gate((NB - 1) % 2)
                read_oT()
                update(NB - 1, (NB - 1) % 2)

            batches(dve, body, prologue, epilogue)


def program(nc, x, w, out, layers=("mamba", "experts", "attention", "experts")):
    ctx = ExitStack()
    sems = ctx
    with ctx:
        x_sb = ctx.enter_context(nc.sbuf_tensor("x_sb", [P, NT, DM], FP32))
        ident = ctx.enter_context(nc.sbuf_tensor("ident", [P, P], FP32))
        ident16 = ctx.enter_context(nc.sbuf_tensor("ident16", [P, P], FP16))
        half = ctx.enter_context(nc.sbuf_tensor("half", [P, QC // P], FP32))
        x_loaded = ctx.enter_context(nc.semaphore("x_loaded"))
        made = ctx.enter_context(nc.semaphore("constants_made"))

        with nc.Block() as block:
            @block.sync
            def _(sp):
                sp.dma_start(x_sb[:], x.rearrange("b (n p) d -> p (b n) d", p=P)).then_inc(x_loaded, 16)
                sp.wait_ge(x_loaded, 16)

            @block.gpsimd
            def _(pool):
                nc.gpsimd.memset(half[:], -0.5)
                nc.gpsimd.memset(ident[:], 0.0)
                nc.gpsimd.memset(ident16[:], 0.0).then_inc(made, 1)
                pool.wait_ge(made, 1)
                for i in (ident, ident16):
                    nc.gpsimd.affine_select(out=i[:], in_=i[:], compare_op=ALU.not_equal, fill=1.0, base=0,
                                            pattern=[[-1, P]], channel_multiplier=1)

        ew = ExpertWeights(nc, ctx)
        split_expert_weights(nc, ew, w)
        for n, layer in enumerate(layers):
            if layer == "mamba":
                mamba_layer(nc, sems, x_sb, w, ident, half)
            if layer == "experts":
                expert_layer(nc, sems, n, x_sb, ew, ident, half)
            if layer == "attention":
                attention_layer(nc, sems, x_sb, w, ident, ident16, half)

        stored = ctx.enter_context(nc.semaphore("stored"))
        with nc.Block() as block:
            @block.sync
            def _(sp):
                sp.dma_start(out.rearrange("b (n p) d -> p (b n) d", p=P), x_sb[:]).then_inc(stored, 16)
                sp.wait_ge(stored, 16)


def layout(v):
    import numpy as np
    g = {k: np.asarray(a) for k, a in v.items()}
    a = {k[len("L0_attn_a_"):]: g[k] for k in g if k.startswith("L0_attn_a_")}
    b = {k[len("L0_attn_b_"):]: g[k] for k in g if k.startswith("L0_attn_b_")}
    f = {k[len("L0_ffn_"):]: g[k] for k in g if k.startswith("L0_ffn_")}

    def chunks(m):
        return m.reshape(-1, P, *m.shape[1:]).swapaxes(0, 1)

    def spread(m):
        bc, dl = m[..., DTR:], m[..., :DTR]
        zero = np.zeros((*m.shape[:-1], 16), m.dtype)
        return np.concatenate([bc, dl, zero, bc, zero, zero], -1)

    def rows(m):
        return np.repeat(m.reshape(1, -1), P, 0)

    w = {
        "in_w": a["in_W"], "in_b": a["in_b"].reshape(-1, P).T, "rms_w": a["rms_w"].reshape(P, 1),
        "conv_w": chunks(a["conv_w"]), "conv_b": a["conv_b"].reshape(-1, P).T, "a_log": chunks(a["A_log"]),
        "dbc_w": chunks(spread(a["dbc_W"])), "dbc_b": spread(a["dbc_b"]).reshape(P, 1),
        "dup_w": a["dup_W"], "dup_b": a["dup_b"].reshape(-1, P).T,
        "out_w": chunks(a["out_W"]), "out_b": rows(a["out_b"]),
    }
    w["gate_up"] = np.stack([np.concatenate([f["w_gate"], f["shared_gate_w"][None]]),
                             np.concatenate([f["w_up"], f["shared_up_w"][None]])]).transpose(3, 1, 0, 2)
    w["down"] = np.concatenate([f["w_down"], f["shared_down_w"][None]]).transpose(2, 0, 1)
    w["router"] = f["gate_w"].T
    w["expert_bias"] = rows(f["expert_bias"])
    q = b["W_in"].reshape(NH, 4, DH, DM).transpose(1, 0, 2, 3).reshape(4 * NH * DH, DM)
    w["qkvg_w"] = q.T
    w["qkvg_b"] = rows(b["b_in"].reshape(NH, 4, DH).transpose(1, 0, 2))
    w["attn_out_w"] = b["W_out"].T
    w["attn_out_b"] = rows(b["b_out"])
    return {k: np.ascontiguousarray(m) for k, m in w.items()}


def kernel(**inputs):
    import numpy as np
    import concourse.bacc as bacc
    from concourse.bass_utils import run_bass_kernel_spmd as run

    nc = bacc.Bacc("TRN2", target_bir_lowering=False, num_devices=1)
    x = np.ascontiguousarray(inputs["L0_attn_a_x"])
    arrays = {"x": x, **{"w_" + k: m for k, m in layout(inputs).items()}}
    dram = {k: nc.dram_tensor(k, m.shape, FP32, kind="ExternalInput").ap() for k, m in arrays.items()}
    out = nc.dram_tensor("out", x.shape, FP32, kind="ExternalOutput").ap()
    program(nc, dram["x"], {k[2:]: a for k, a in dram.items() if k != "x"}, out)
    r = run(nc, [arrays], core_ids=[0])
    return r.results[0]["out"]
```

```python
import concourse.bass as bass
from concourse import mybir
from contextlib import ExitStack

FP32 = mybir.dt.float32
FP16 = mybir.dt.float16
ALU = mybir.AluOpType
ACT = mybir.ActivationFunctionType
AX = mybir.AxisListType

P = 128
NB, T, DM = 16, 256, 128
TT = T // P
NT = NB * TT
DI, NS, DTR, KC = 256, 16, 16, 4
DC = DI // P
NE = 16
TOPK = 8
ROUTE_SCALE = 2.826
QC = 4 * P
NQ = NB * T // QC
NH, DH = 16, 8
HG = 4
LN_EPS = 1e-5
RMS_EPS = 1e-6
SHEP_EPS = 1e-4
TAKEN = -1e30


class Chain:

    def __init__(self, eng, sem):
        self.eng, self.sem, self.n = eng, sem, 0

    def link(self, ins):
        self.n += 1
        ins.then_inc(self.sem, 1)
        self.eng.wait_ge(self.sem, self.n)

    def end(self):
        if self.n:
            self.eng.sem_inc(self.sem, -self.n)
        self.n = 0


def take(eng, sem, n=1):
    eng.wait_ge(sem, n)
    eng.sem_inc(sem, -n)


class Lagged:

    def __init__(self, eng, sem, lag, n, which=None):
        self.eng, self.sem, self.lag, self.n = eng, sem, lag, n
        self.which = range(n) if which is None else which

    def count(self, start, stop):
        return sum(1 for k in range(start, stop) if k % self.n in self.which)

    def start(self, first):
        return max(0, -self.lag) if first else -self.lag

    def wait(self, k, first=False):
        c = self.count(self.start(first), k + 1)
        if k % self.n in self.which and c > 0:
            self.eng.wait_ge(self.sem, c)

    def end(self, first, last):
        if not last:
            self.eng.sem_inc(self.sem, -self.count(self.start(first), self.n - self.lag))


def mamba_layer(nc, sems, x_sb, w, ident, half):
    ctx = ExitStack()
    with ctx:
        def sb(name, shape, dt=FP32):
            return ctx.enter_context(nc.sbuf_tensor("m_" + name, shape, dt))

        def pb(name, dt=FP32, width=512):
            return ctx.enter_context(nc.psum_tensor("m_" + name, [P, width], dt))

        def sem(name):
            return sems.enter_context(nc.semaphore("m_" + name))

        in_w = sb("in_w", [P, 2 * DI])
        in_b = sb("in_b", [P, 2 * DC])
        rms_w = sb("rms_w", [P, 1])
        conv_w = sb("conv_w", [P, DC, KC])
        conv_b = sb("conv_b", [P, DC])
        neg_a = sb("neg_a", [P, DC, NS])
        dbc_w = sb("dbc_w", [P, DC, P])
        dbc_b = sb("dbc_b", [P, 1])
        dup_w = sb("dup_w", [3 * DTR + 1, DI])
        out_w = sb("out_w", [P, DC, DM])
        out_b = sb("out_b", [P, DM])
        pick = sb("pick", [96, 2 * NS, P], FP16)

        stats = sb("stats", [P, TT, 6])
        mv = sb("mv", [P, TT, 2])
        nrm = sb("nrm", [P, 4, TT])
        xn = sb("xn", [P, TT, DM])
        z = sb("z", [P, TT, DM])
        hT = sb("hT", [P, T])
        xpad = sb("xpad", [P, DC, KC - 1 + T])
        conv = sb("conv", [P, DC, T])
        xs = sb("xs", [P, DC, T])
        bcd = sb("bcd", [P, T])
        bc_hi = sb("bc_hi", [96, T], FP16)
        sp = sb("sp", [P, DC, T])
        gate = sb("gate", [P, 2, DC, T])
        delta = sb("delta", [P, 2, DC, T])
        dx = sb("dx", [P, 2, DC, T])
        bc = sb("bc", [96, 2, T], FP16)
        decay = sb("decay", [P, 4, 2, DC, T])
        h = sb("h", [P, 4, 2, DC, T])
        c_sb = sb("c_sb", [P, 2, 2 * T])
        hc = sb("hc", [P, 4, 2, DC, T])
        yg = sb("yg", [P, DC, T])

        b_ps = [pb("b_ps0"), pb("b_ps1")]
        c_ps = [pb("c_ps0"), pb("c_ps1")]
        y_ps = pb("y_ps")
        t0, t1, t2 = pb("t0"), pb("t1"), pb("t2")

        w_loaded = sem("w_loaded")
        w_ready = {e: sem("w_ready_" + e) for e in ("act", "dve", "pool", "pe")}
        setup_done = {e: sem("setup_done_" + e) for e in ("act", "dve", "pe")}
        pool_chain, dve_chain, act_chain = sem("pool_chain"), sem("dve_chain"), sem("act_chain")
        stats_ready, norm_ready, xn_ready, res_ready = (sem(n) for n in ("stats_ready", "norm_ready", "xn_ready", "res_ready"))
        delta_made, dx_ready = sem("delta_made"), sem("dx_ready")
        z_ready, zT_ready, hT_ready = sem("z_ready"), sem("zT_ready"), sem("hT_ready")
        x1_ready, g_ready, xpad_ready, conv_ready, xs_ready = (sem(n) for n in ("x1_ready", "g_ready", "xpad_ready", "conv_ready", "xs_ready"))
        dbc_ready, bcd_ready, bc_hi_ready, bc_ready = (sem(n) for n in ("dbc_ready", "bcd_ready", "bc_hi_ready", "bc_ready"))
        dup_ready, sp_ready, delta_ready = (sem(n) for n in ("dup_ready", "sp_ready", "delta_ready"))
        t2_free = sem("t2_free")
        b_ready, c_ready, decay_ready = sem("b_ready"), sem("c_ready"), sem("decay_ready")
        core_chain, hc_chain, c_chain = sem("core_chain"), sem("hc_chain"), sem("c_chain")
        b_free, c_free, decay_free, h_free, c_sb_free = (sem(n) for n in ("b_free", "c_free", "decay_free", "h_free", "c_sb_free"))
        h_ready, c_sb_ready = sem("h_ready"), sem("c_sb_ready")
        hc_dve, hc_pool = sem("hc_dve"), sem("hc_pool")
        y_ready, yg_ready, o_ready = sem("y_ready"), sem("yg_ready"), sem("o_ready")

        PAIRS = NS // 2
        LAG = 2
        POOL_PAIRS = (1, 2, 3, 4, 6, 7)
        DVE_PAIRS = tuple(m for m in range(PAIRS) if m not in POOL_PAIRS)

        NORM_AFTER, RES_AFTER = 2, 6

        def c_place(m):
            return POOL_PAIRS.index(m) % 2

        LOADS = [(in_w, w["in_w"]), (in_b, w["in_b"]), (rms_w, w["rms_w"]), (conv_w, w["conv_w"]),
                 (conv_b, w["conv_b"]), (neg_a, w["a_log"]), (dbc_w, w["dbc_w"]), (dbc_b, w["dbc_b"]),
                 (out_w, w["out_w"]), (out_b, w["out_b"])]

        def tile(b, tt):
            return x_sb[:, bass.ds(b * TT + tt, 1), :].rearrange("p o d -> p (o d)")

        def batches(eng, body, prologue, epilogue):
            prologue()
            body(0, 0, first=True)
            with eng.Fori(0, NB // 2 - 2) as i:
                body(i * 2 + 1, 1)
                body(i * 2 + 2, 0)
            body(NB - 3, (NB - 3) % 2)
            body(NB - 2, (NB - 2) % 2, ahead=False)
            body(NB - 1, (NB - 1) % 2, ahead=False, last=True)
            epilogue()

        block = ctx.enter_context(nc.Block())

        @block.sync
        def _(sp_eng):
            for dst, src in LOADS:
                sp_eng.dma_start(dst[:], src).then_inc(w_loaded, 16)
            sp_eng.dma_start(dup_w[2 * DTR:3 * DTR + 1, :], w["dup_w"]).then_inc(w_loaded, 16)
            sp_eng.wait_ge(w_loaded, 16 * (len(LOADS) + 1))
            for s in w_ready.values():
                sp_eng.sem_inc(s, 1)

        @block.gpsimd
        def _(pool):
            chain = Chain(pool, pool_chain)
            chain.link(nc.gpsimd.memset(pick[:], 0.0))
            nc.gpsimd.memset(bc[:], 0.0)
            nc.gpsimd.memset(xpad[:, :, 0:KC - 1], 0.0)
            chain.link(nc.gpsimd.memset(decay[:, :, :, :, 0:1], 0.0))
            for base in (0, -64):
                chain.link(nc.gpsimd.affine_select(out=pick[:], in_=pick[:], compare_op=ALU.not_equal, fill=1.0,
                                                   base=base, pattern=[[-1, 2 * NS], [0, P]], channel_multiplier=1))
            chain.end()
            pool.wait_ge(w_ready["pool"], 1)
            for s in setup_done.values():
                pool.sem_inc(s, 1)

            def norm():
                c = Chain(pool, pool_chain)
                take(pool, stats_ready)
                c.link(nc.gpsimd.tensor_scalar(nrm[:, 1, :], mv[:, :, 1], LN_EPS, 1.0, ALU.add, ALU.mult))
                c.link(nc.gpsimd.tensor_tensor(nrm[:, 0, :], nrm[:, 1, :], half[:, 0:TT], ALU.pow))
                c.link(nc.gpsimd.tensor_tensor(nrm[:, 1, :], nrm[:, 0, :], nrm[:, 0, :], ALU.mult))
                c.link(nc.gpsimd.tensor_tensor(nrm[:, 1, :], nrm[:, 1, :], mv[:, :, 1], ALU.mult))
                c.link(nc.gpsimd.tensor_scalar(nrm[:, 1, :], nrm[:, 1, :], RMS_EPS, 1.0, ALU.add, ALU.mult))
                c.link(nc.gpsimd.tensor_tensor(nrm[:, 2, :], nrm[:, 1, :], half[:, 0:TT], ALU.pow))
                nc.gpsimd.tensor_tensor(nrm[:, 3, :], nrm[:, 2, :], nrm[:, 0, :], ALU.mult).then_inc(norm_ready, 1)
                c.end()

            def residual(b):
                c = Chain(pool, pool_chain)
                take(pool, xn_ready)
                own = x_sb[:, bass.ds(b * TT, TT), :]
                c.link(nc.gpsimd.tensor_tensor(own, own, xn[:], ALU.add))
                c.link(nc.gpsimd.tensor_tensor(own, own, out_b[:].rearrange("p (o d) -> p o d", o=1).to_broadcast([P, TT, DM]), ALU.add))
                c.end()
                pool.sem_inc(res_ready, 1)

            def split_bc(p):
                take(pool, bc_hi_ready)
                c = Chain(pool, pool_chain)
                c.link(nc.gpsimd.tensor_tensor(bc[64:96, p], bcd[64:96], bc_hi[64:96], ALU.subtract))
                c.end()
                pool.sem_inc(bc_ready, 1)

            def make_dx(p):
                take(pool, delta_made)
                nc.gpsimd.tensor_tensor(dx[:, p], delta[:, p], xs[:], ALU.mult).then_inc(dx_ready, 1)

            def prologue():
                for b in range(2):
                    norm()
                    residual(b)
                    if b == 0:
                        split_bc(0)
                        make_dx(0)

            states, c_copied = Lagged(pool, h_ready, 0, PAIRS, POOL_PAIRS), Lagged(pool, c_sb_ready, 0, PAIRS, POOL_PAIRS)

            def body(b, p, first=False, ahead=True, last=False):
                for n, m in enumerate(POOL_PAIRS):
                    if m == 6 and not last:
                        make_dx(1 - p)
                    c_copied.wait(m, first)
                    states.wait(m, first)
                    for c in range(DC):
                        ins = nc.gpsimd.tensor_tensor(hc[:, m % 4, :, c], h[:, m % 4, :, c],
                                                      c_sb[:, c_place(m)].rearrange("p (n t) -> p n t", n=2), ALU.mult)
                    ins.then_inc(hc_chain, 1)
                    pool.wait_ge(hc_chain, n + 1)
                    pool.sem_inc(hc_pool, 1)
                    pool.sem_inc(h_free, 1)
                    pool.sem_inc(c_sb_free, 1)
                    if m == NORM_AFTER and ahead:
                        norm()
                    if m == 4 and not last:
                        split_bc(1 - p)
                    if m == RES_AFTER and ahead:
                        residual(b + 2)
                states.end(first, last)
                c_copied.end(first, last)
                pool.sem_inc(hc_chain, -len(POOL_PAIRS))

            batches(pool, body, prologue, lambda: None)

        @block.tensor
        def _(pe):
            pe.wait_ge(w_ready["pe"], 1)
            pe.wait_ge(setup_done["pe"], 1)
            pe.sem_inc(t2_free, 1)
            inputs_made = Lagged(pe, b_free, 1, PAIRS)
            c_copied = Lagged(pe, c_free, 1, PAIRS, POOL_PAIRS)
            products = {"dve": Lagged(pe, hc_dve, LAG, PAIRS, DVE_PAIRS), "pool": Lagged(pe, hc_pool, LAG, PAIRS, POOL_PAIRS)}

            def transpose_z():
                take(pe, z_ready)
                for tt in range(TT):
                    ins = nc.tensor.transpose(t0[:, tt * P:(tt + 1) * P], z[:, tt], ident[:])
                ins.then_inc(zT_ready, 1)

            def project_in():
                take(pe, hT_ready)
                for c in range(DC):
                    ins = nc.tensor.matmul(t1[:, c * T:(c + 1) * T], in_w[:, c * P:(c + 1) * P], hT[:], start=True, stop=True)
                ins.then_inc(x1_ready, 1)
                for c in range(DC):
                    ins = nc.tensor.matmul(t0[:, c * T:(c + 1) * T], in_w[:, (DC + c) * P:(DC + c + 1) * P], hT[:], start=True, stop=True)
                ins.then_inc(g_ready, 1)

            def project_dbc():
                take(pe, xs_ready)
                for c in range(DC):
                    ins = nc.tensor.matmul(t1[:, 0:T], dbc_w[:, c], xs[:, c], start=(c == 0), stop=(c == DC - 1))
                ins.then_inc(dbc_ready, 1)

            def project_delta():
                take(pe, bcd_ready)
                take(pe, t2_free)
                for c in range(DC):
                    ins = nc.tensor.matmul(t2[:, c * T:(c + 1) * T], dup_w[2 * DTR:3 * DTR + 1, c * P:(c + 1) * P],
                                           bcd[2 * DTR:3 * DTR + 1, :], start=True, stop=True)
                ins.then_inc(dup_ready, 1)

            def project_out():
                take(pe, t2_free)
                for tt in range(TT):
                    for c in range(DC):
                        ins = nc.tensor.matmul(t2[:, tt * DM:(tt + 1) * DM], yg[:, c, tt * P:(tt + 1) * P], out_w[:, c],
                                               start=(c == 0), stop=(c == DC - 1))
                ins.then_inc(o_ready, 1)

            def spread(m, p):
                for n in range(2):
                    ins = nc.tensor.matmul(c_ps[m % 2][:, n * T:(n + 1) * T], pick[:, NS + 2 * m + n], bc[:, p], start=True, stop=True)
                if m in POOL_PAIRS:
                    ins.then_inc(c_ready, 1)
                for n in range(2):
                    ins = nc.tensor.matmul(b_ps[m % 2][:, n * T:(n + 1) * T], pick[:, 2 * m + n], bc[:, p], start=True, stop=True)
                ins.then_inc(b_ready, 1)

            def wait_banks(m, first):
                inputs_made.wait(m, first)
                c_copied.wait(m, first)
                products["dve"].wait(m, first)

            def wait_products(m, first=False):
                products["dve"].wait(m, first)
                products["pool"].wait(m, first)

            def add_states(m):
                for n in range(2):
                    ins = nc.tensor.matmul(y_ps[:], ident[:], hc[:, m % 4, n].rearrange("p c t -> p (c t)"),
                                           start=(m == 0 and n == 0), stop=(m == PAIRS - 1 and n == 1))
                if m == PAIRS - 1:
                    ins.then_inc(y_ready, 1)

            def prologue():
                transpose_z()
                project_in()
                project_dbc()
                project_delta()
                transpose_z()
                project_in()
                take(pe, bc_ready)
                spread(0, 0)

            def body(b, p, first=False, ahead=True, last=False):
                for m in range(PAIRS):
                    if m < PAIRS - 1 or not last:
                        wait_banks(m - 1, first)
                    if m == PAIRS - 1 and not last:
                        take(pe, bc_ready)
                        spread(0, 1 - p)
                    elif m < PAIRS - 1:
                        spread(m + 1, p)
                    if m == LAG and not first:
                        take(pe, yg_ready)
                    if m >= LAG or not first:
                        wait_products(m - LAG, first)
                        add_states((m - LAG) % PAIRS)
                    if m == LAG and not first:
                        project_out()
                    if m == 3 and not last:
                        project_dbc()
                    if m == 4 and not last:
                        project_delta()
                    if m == 6 and ahead:
                        transpose_z()
                    if m == 7 and ahead:
                        project_in()
                inputs_made.end(first, last)
                c_copied.end(first, last)
                products["dve"].end(first, last)
                products["pool"].end(first, last)

            def epilogue():
                for m in range(PAIRS - LAG, PAIRS):
                    wait_products(m)
                    add_states(m)
                take(pe, yg_ready)
                project_out()

            batches(pe, body, prologue, epilogue)

        @block.scalar
        def _(act):
            act.wait_ge(w_ready["act"], 1)
            act.wait_ge(setup_done["act"], 1)
            chain = Chain(act, act_chain)
            nc.scalar.preload_act_table_set("natural_log_exp_and_others")
            chain.link(nc.scalar.activation(neg_a[:], neg_a[:], ACT.Exp))
            chain.link(nc.scalar.activation(neg_a[:], neg_a[:], ACT.Copy, scale=-1.0))
            chain.end()

            def scale_hT():
                take(act, zT_ready)
                nc.scalar.activation(hT[:], t0[:, 0:T], ACT.Copy, scale=rms_w[:, 0:1]).then_inc(hT_ready, 1)

            def pad_x():
                take(act, x1_ready)
                for c in range(DC):
                    ins = nc.scalar.activation(xpad[:, c, KC - 1:], t1[:, c * T:(c + 1) * T], ACT.Identity, bias=in_b[:, c:c + 1])
                ins.then_inc(xpad_ready, 1)

            def silus(p):
                take(act, g_ready)
                take(act, conv_ready)
                for c in range(DC):
                    nc.scalar.activation(gate[:, p, c], t0[:, c * T:(c + 1) * T], ACT.Silu, bias=in_b[:, DC + c:DC + c + 1])
                for c in range(DC):
                    ins = nc.scalar.activation(xs[:, c], conv[:, c], ACT.Silu, bias=conv_b[:, c:c + 1])
                ins.then_inc(xs_ready, 1)
                nc.scalar.preload_act_table_set("natural_log_exp_and_others")

            def read_dbc(p):
                take(act, dbc_ready)
                nc.scalar.activation(bcd[:], t1[:, 0:T], ACT.Identity, bias=dbc_b[:, 0:1]).then_inc(bcd_ready, 1)
                nc.scalar.activation(bc[0:2 * NS, p], t1[0:2 * NS, 0:T], ACT.Identity, bias=dbc_b[0:2 * NS, 0:1])
                nc.scalar.activation(bc_hi[64:96], t1[64:96, 0:T], ACT.Identity, bias=dbc_b[64:96, 0:1]).then_inc(bc_hi_ready, 1)

            def softplus():
                c = Chain(act, act_chain)
                take(act, dup_ready)
                flat = sp[:].rearrange("p c t -> p (c t)")
                c.link(nc.scalar.activation(flat, t2[:], ACT.Abs))
                c.link(nc.scalar.activation(flat, flat, ACT.Exp, scale=-1.0))
                nc.scalar.activation(flat, flat, ACT.Ln, bias=1.0).then_inc(sp_ready, 1)
                c.end()

            scanned = Lagged(act, decay_free, 3, PAIRS)
            spreads = Lagged(act, c_ready, 0, PAIRS, POOL_PAIRS)
            c_sb_read = Lagged(act, c_sb_free, PAIRS - 1 - POOL_PAIRS[-3], PAIRS, POOL_PAIRS)

            def decays(m, p):
                for n in range(2):
                    for c in range(DC):
                        ins = nc.scalar.activation(decay[:, m % 4, n, c, 1:T], delta[:, p, c, 1:T], ACT.Exp,
                                                   scale=neg_a[:, c, 2 * m + n:2 * m + n + 1])
                ins.then_inc(decay_ready, 1)

            def copy_c(m, n):
                nc.scalar.activation(c_sb[:, c_place(m)], c_ps[m % 2][:], ACT.Copy).then_inc(c_chain, 1)
                act.wait_ge(c_chain, n)
                act.sem_inc(c_sb_ready, 1)
                act.sem_inc(c_free, 1)

            def prologue():
                scale_hT()
                pad_x()
                silus(0)
                read_dbc(0)
                softplus()
                scale_hT()
                take(act, delta_ready)
                decays(0, 0)

            def body(b, p, first=False, ahead=True, last=False):
                for m in range(PAIRS):
                    if m < PAIRS - 1 or not last:
                        scanned.wait(m - 3, first)
                    if m == PAIRS - 1 and not last:
                        take(act, delta_ready)
                        decays(0, 1 - p)
                    elif m < PAIRS - 1:
                        decays(m + 1, p)
                    if m + 1 in POOL_PAIRS:
                        n = POOL_PAIRS.index(m + 1)
                        spreads.wait(m + 1, first)
                        c_sb_read.wait(POOL_PAIRS[n - 2] - (PAIRS if n < 2 else 0), first)
                        copy_c(m + 1, n + 1)
                    if not last:
                        if m == 0:
                            pad_x()
                        if m == 2:
                            silus(1 - p)
                        if m == 3:
                            read_dbc(1 - p)
                        if m == 4:
                            softplus()
                    if m == 6 and ahead:
                        scale_hT()
                scanned.end(first, last)
                spreads.end(first, last)
                c_sb_read.end(first, last)
                act.sem_inc(c_chain, -len(POOL_PAIRS))

            batches(act, body, prologue, lambda: None)

        @block.vector
        def _(dve):
            dve.wait_ge(w_ready["dve"], 1)
            dve.wait_ge(setup_done["dve"], 1)

            def statistics(b):
                c = Chain(dve, dve_chain)
                for tt in range(TT):
                    ins = nc.vector.bn_stats(stats[:, tt], tile(b, tt))
                c.link(ins)
                for tt in range(TT):
                    ins = nc.vector.bn_aggr(mv[:, tt], stats[:, tt])
                ins.then_inc(stats_ready, 1)
                c.end()

            def normalise(b):
                take(dve, norm_ready)
                for tt in range(TT):
                    ins = nc.vector.tensor_scalar(z[:, tt], x_sb[:, bass.ds(b * TT + tt, 1), :].rearrange("p o d -> p (o d)"), mv[:, tt, 0:1], nrm[:, 3, tt:tt + 1], ALU.subtract, ALU.mult)
                ins.then_inc(z_ready, 1)
                for tt in range(TT):
                    ins = nc.vector.tensor_scalar(xn[:, tt], x_sb[:, bass.ds(b * TT + tt, 1), :].rearrange("p o d -> p (o d)"), mv[:, tt, 0:1], nrm[:, 0, tt:tt + 1], ALU.subtract, ALU.mult)
                ins.then_inc(xn_ready, 1)

            def convolve():
                c = Chain(dve, dve_chain)
                take(dve, xpad_ready)
                for ch in range(DC):
                    ins = nc.vector.tensor_scalar(conv[:, ch], xpad[:, ch, 0:T], conv_w[:, ch, 0:1], None, ALU.mult)
                for k in range(1, KC):
                    c.link(ins)
                    for ch in range(DC):
                        ins = nc.vector.scalar_tensor_tensor(conv[:, ch], xpad[:, ch, k:k + T], conv_w[:, ch, k:k + 1], conv[:, ch], ALU.mult, ALU.add)
                ins.then_inc(conv_ready, 1)
                c.end()

            def make_delta(p):
                c = Chain(dve, dve_chain)
                take(dve, sp_ready)
                c.link(nc.vector.scalar_tensor_tensor(delta[:, p].rearrange("p c t -> p (c t)"), t2[:], 0.0, sp[:].rearrange("p c t -> p (c t)"), ALU.max, ALU.add))
                dve.sem_inc(t2_free, 1)
                dve.sem_inc(delta_ready, 1)
                dve.sem_inc(delta_made, 1)
                c.end()

            def gate_y(p):
                take(dve, y_ready)
                nc.vector.tensor_tensor(yg[:].rearrange("p c t -> p (c t)"), y_ps[:], gate[:, p].rearrange("p c t -> p (c t)"), ALU.mult).then_inc(yg_ready, 1)

            def update(b):
                take(dve, o_ready)
                take(dve, res_ready)
                own = x_sb[:, bass.ds(b * TT, TT), :]
                nc.vector.tensor_tensor(own, t2[:, 0:TT * DM].rearrange("p (a d) -> p a d", a=TT), own, ALU.add).then_inc(t2_free, 1)

            def inputs(m, p):
                out = h[:, m % 4]
                b4 = b_ps[m % 2][:].rearrange("p (n c t) -> p n c t", n=2, c=1).to_broadcast([P, 2, DC, T])
                d4 = dx[:, p].rearrange("p (n c) t -> p n c t", n=1).to_broadcast([P, 2, DC, T])
                nc.vector.tensor_tensor(out, b4, d4, ALU.mult).then_inc(core_chain, 1)

            states_read = Lagged(dve, h_free, 3, PAIRS, POOL_PAIRS)

            def flat(ap):
                return ap.rearrange("p n c t -> p (n c t)")

            def prologue():
                statistics(0)
                normalise(0)
                convolve()
                make_delta(0)
                statistics(1)
                normalise(1)
                take(dve, dx_ready)
                take(dve, b_ready)
                inputs(0, 0)

            def body(b, p, first=False, ahead=True, last=False):
                done = 1
                for m in range(PAIRS):
                    if m == LAG and not first:
                        gate_y(1 - p)
                    if m == 1 and ahead:
                        statistics(b + 2)
                    if m == 2 and not last:
                        convolve()
                    if m == 5 and ahead:
                        normalise(b + 2)
                    if m == 6 and not last:
                        make_delta(1 - p)
                    if m == LAG + 1 and not first:
                        update(b - 1)
                    dve.wait_ge(core_chain, done)
                    dve.sem_inc(b_free, 1)
                    dve.wait_ge(decay_ready, m + 1)
                    nc.vector.tensor_tensor_scan(flat(h[:, m % 4]), flat(decay[:, m % 4]), flat(h[:, m % 4]), 0.0, ALU.mult, ALU.add).then_inc(core_chain, 1)
                    done += 1
                    scanned = done
                    if m < PAIRS - 1 or not last:
                        dve.wait_ge(b_ready, m + 1)
                        states_read.wait(m - 3, first)
                        if m == PAIRS - 1:
                            take(dve, dx_ready)
                        inputs((m + 1) % PAIRS, p if m < PAIRS - 1 else 1 - p)
                        done += 1
                    dve.wait_ge(core_chain, scanned)
                    dve.sem_inc(decay_free, 1)
                    if m in POOL_PAIRS:
                        dve.sem_inc(h_ready, 1)
                    else:
                        c4 = c_ps[m % 2][:].rearrange("p (n c t) -> p n c t", n=2, c=1).to_broadcast([P, 2, DC, T])
                        nc.vector.tensor_tensor(hc[:, m % 4], h[:, m % 4], c4, ALU.mult).then_inc(hc_dve, 1)
                states_read.end(first, last)
                dve.sem_inc(decay_ready, -PAIRS)
                if not last:
                    dve.sem_inc(b_ready, -PAIRS)
                    dve.sem_inc(core_chain, 1 - done)

            def epilogue():
                gate_y((NB - 1) % 2)
                update(NB - 1)

            batches(dve, body, prologue, epilogue)


class ExpertWeights:

    def __init__(self, nc, ctx):
        def sb(name, shape, dt=FP16):
            return ctx.enter_context(nc.sbuf_tensor("ew_" + name, shape, dt))

        self.gate_up = [sb(f"gate_up{i}", [P, NE + 1, 2, P]) for i in range(2)]
        self.down = [sb(f"down{i}", [P, NE + 1, DM]) for i in range(2)]
        self.router = [sb(f"router{i}", [P, NE]) for i in range(2)]
        self.bias = sb("bias", [P, NE], FP32)
        self.pick = sb("pick", [4 * NE, NE, P])


def split_expert_weights(nc, ew, w):
    ctx = ExitStack()
    with ctx:
        def sb(name, shape):
            return ctx.enter_context(nc.sbuf_tensor("s_" + name, shape, FP32))

        raw = [sb("gate_up", [P, NE + 1, 2, P]), sb("down", [P, NE + 1, DM]), sb("router", [P, NE])]
        halves = [ew.gate_up, ew.down, ew.router]
        loaded = ctx.enter_context(nc.semaphore("s_loaded"))
        upper = ctx.enter_context(nc.semaphore("s_upper"))
        made = ctx.enter_context(nc.semaphore("s_made"))
        block = ctx.enter_context(nc.Block())

        @block.sync
        def _(sp):
            for dst, name in zip(raw, ("gate_up", "down", "router")):
                sp.dma_start(dst[:], w[name]).then_inc(loaded, 16)
            sp.dma_start(ew.bias[:], w["expert_bias"]).then_inc(loaded, 16)
            sp.wait_ge(loaded, 64)

        @block.scalar
        def _(act):
            act.wait_ge(loaded, 64)
            for src, dst in zip(raw, halves):
                nc.scalar.activation(dst[0][:], src[:], ACT.Copy).then_inc(upper, 1)

        @block.vector
        def _(dve):
            for n, (src, dst) in enumerate(zip(raw, halves)):
                dve.wait_ge(upper, n + 1)
                nc.vector.tensor_tensor(dst[1][:], src[:], dst[0][:], ALU.subtract)

        @block.gpsimd
        def _(pool):
            nc.gpsimd.memset(ew.pick[:], 0.0).then_inc(made, 1)
            for n, base in enumerate((0, -2 * NE)):
                pool.wait_ge(made, n + 1)
                nc.gpsimd.affine_select(out=ew.pick[:], in_=ew.pick[:], compare_op=ALU.not_equal, fill=1.0, base=base,
                                        pattern=[[-1, NE], [0, P]], channel_multiplier=1).then_inc(made, 1)


def expert_layer(nc, sems, layer, x_sb, ew, ident, half):
    ctx = ExitStack()
    with ctx:
        tag = f"e{layer}_"

        def sb(name, shape, dt=FP32):
            return ctx.enter_context(nc.sbuf_tensor(tag + name, shape, dt))

        def pb(name):
            return ctx.enter_context(nc.psum_tensor(tag + name, [P, 512], FP32))

        def sem(name):
            return sems.enter_context(nc.semaphore(tag + name))

        NTQ = QC // P
        STEPS = NE + 1
        RING = 4

        stats = sb("stats", [P, NTQ, 6])
        mv = sb("mv", [P, NTQ, 2])
        nrm = sb("nrm", [P, 2, NTQ])
        xn = sb("xn", [P, NTQ, DM])
        x_hi, x_lo = sb("x_hi", [P, 2, QC], FP16), sb("x_lo", [P, 2, QC], FP16)
        th = sb("th", [P, NTQ, NE])
        score = sb("score", [P, NTQ, NE])
        sel = sb("sel", [P, NTQ, NE])
        top = sb("top", [P, NTQ, TOPK])
        left = sb("left", [P, NTQ, NE])
        chosen = sb("chosen", [P, NTQ, NE])
        total = sb("total", [P, 2, NTQ])
        comb = sb("comb", [P, NTQ, 4 * NE])
        c_hi = sb("c_hi", [4 * NE, QC], FP16)
        cT = sb("cT", [4 * NE, 2, QC], FP16)
        s = sb("s", [P, 2, QC])
        su = sb("su", [P, 2, QC])
        h = sb("h", [P, RING + 1, QC])
        h_hi, h_lo = sb("h_hi", [P, RING + 1, QC], FP16), sb("h_lo", [P, RING + 1, QC], FP16)
        yT = sb("yT", [P, QC])

        g_ps, u_ps, c_ps = [pb("g0"), pb("g1")], [pb("u0"), pb("u1")], [pb("c0"), pb("c1")]
        y_ps, t_ps = pb("y"), pb("t")

        zeroed = {e: sem("zeroed_" + e) for e in ("dve",)}
        pool_chain, dve_chain, core_chain = sem("pool_chain"), sem("dve_chain"), sem("core_chain")
        stats_ready, norm_ready, xn_ready, xT_ready = (sem(n) for n in ("stats_ready", "norm_ready", "xn_ready", "xT_ready"))
        x_hi_ready, x_ready, gates_ready, th_ready = (sem(n) for n in ("x_hi_ready", "x_ready", "gates_ready", "th_ready"))
        comb_ready, combT_ready, c_hi_ready, cT_ready = (sem(n) for n in ("comb_ready", "combT_ready", "c_hi_ready", "cT_ready"))
        g_ready, u_ready, s_ready, h_ready, h_hi_ready, h_lo_ready = (sem(n) for n in ("g_ready", "u_ready", "s_ready", "h_ready", "h_hi_ready", "h_lo_ready"))
        banks_free = sem("banks_free")
        y_ready, yT_ready, o_ready = sem("y_ready"), sem("yT_ready"), sem("o_ready")

        def place(e):
            return e % RING if e < NE else RING

        def chunks(eng, body, prologue, epilogue):
            prologue()
            body(0, 0, first=True)
            with eng.Fori(0, NQ // 2 - 1) as i:
                body(i * 2 + 1, 1)
                body(i * 2 + 2, 0)
            body(NQ - 1, (NQ - 1) % 2, last=True)
            epilogue()

        def tile(q, tt):
            return x_sb[:, bass.ds(q * NTQ + tt, 1), :].rearrange("p o d -> p (o d)")

        block = ctx.enter_context(nc.Block())

        @block.gpsimd
        def _(pool):
            nc.gpsimd.memset(comb[:], 0.0).then_inc(zeroed["dve"], 1)

            def norm():
                c = Chain(pool, pool_chain)
                take(pool, stats_ready)
                c.link(nc.gpsimd.tensor_scalar(nrm[:, 1], mv[:, :, 1], LN_EPS, 1.0, ALU.add, ALU.mult))
                nc.gpsimd.tensor_tensor(nrm[:, 0], nrm[:, 1], half[:, 0:NTQ], ALU.pow).then_inc(norm_ready, 1)
                c.end()

            def lower(e):
                pool.wait_ge(h_hi_ready, e + 1)
                k = place(e)
                nc.gpsimd.tensor_tensor(h_lo[:, k], h[:, k], h_hi[:, k], ALU.subtract).then_inc(h_lo_ready, 1)

            def body(q, p, first=False, last=False):
                for e in range(STEPS):
                    if e == 5 and not last:
                        norm()
                    lower(e)
                pool.sem_inc(h_hi_ready, -STEPS)

            chunks(pool, body, norm, lambda: None)

        @block.tensor
        def _(pe):
            def transpose_x():
                take(pe, xn_ready)
                for tt in range(NTQ):
                    ins = nc.tensor.transpose(t_ps[:, tt * P:(tt + 1) * P], xn[:, tt], ident[:])
                ins.then_inc(xT_ready, 1)

            def route(p):
                take(pe, x_ready)
                for tt in range(NTQ):
                    own = slice(tt * P, (tt + 1) * P)
                    for n, (a, r) in enumerate(((x_hi, 0), (x_hi, 1), (x_lo, 0))):
                        ins = nc.tensor.matmul(t_ps[:, tt * NE:(tt + 1) * NE], a[:, p, own], ew.router[r][:], start=(n == 0), stop=(n == 2))
                ins.then_inc(gates_ready, 1)

            def transpose_comb():
                take(pe, comb_ready)
                for tt in range(NTQ):
                    ins = nc.tensor.transpose(t_ps[0:4 * NE, tt * P:(tt + 1) * P], comb[:, tt], ident[:])
                ins.then_inc(combT_ready, 1)

            def up(e, p, first):
                bank = (e + p) % 2
                if not first or e >= 2:
                    pe.wait_ge(banks_free, e - 1 if first else e + 1)
                for side, ps, ready in ((0, g_ps, g_ready), (1, u_ps, None)):
                    for n, (r, a) in enumerate(((0, x_hi), (0, x_lo), (1, x_hi))):
                        ins = nc.tensor.matmul(ps[bank][:], ew.gate_up[r][:, e, side], a[:, p], start=(n == 0), stop=(n == 2))
                    if ready:
                        ins.then_inc(ready, 1)
                if e < NE:
                    ins = nc.tensor.matmul(c_ps[bank][:], ew.pick[:, e], cT[:, p], start=True, stop=True)
                ins.then_inc(u_ready, 1)

            def down(e):
                for n, (r, a) in enumerate(((0, h_hi), (0, h_lo), (1, h_hi))):
                    ins = nc.tensor.matmul(y_ps[:], ew.down[r][:, e], a[:, place(e)], start=(e == 0 and n == 0), stop=(e == NE and n == 2))
                if e == NE:
                    ins.then_inc(y_ready, 1)

            def transpose_y():
                for tt in range(NTQ):
                    ins = nc.tensor.transpose(t_ps[:, tt * P:(tt + 1) * P], yT[:, tt * P:(tt + 1) * P], ident[:])
                ins.then_inc(o_ready, 1)

            def prologue():
                transpose_x()
                route(0)
                transpose_comb()
                take(pe, cT_ready)

            def body(q, p, first=False, last=False):
                for e in range(STEPS):
                    up(e, p, first)
                    if e == 3 and not first:
                        take(pe, yT_ready)
                        transpose_y()
                    if e >= 3 or not first:
                        pe.wait_ge(h_lo_ready, e - 2 if first else e + 1)
                        down((e - 3) % STEPS)
                    if not last:
                        if e == 7:
                            transpose_x()
                        if e == 9:
                            route(1 - p)
                        if e == 13:
                            transpose_comb()
                        if e == 16:
                            take(pe, cT_ready)
                if not last:
                    pe.sem_inc(banks_free, -(STEPS - 2 if first else STEPS))
                    pe.sem_inc(h_lo_ready, -(STEPS - 3 if first else STEPS))

            def epilogue():
                for n in range(3):
                    pe.wait_ge(h_lo_ready, STEPS + n + 1)
                    down(STEPS - 3 + n)
                take(pe, yT_ready)
                transpose_y()

            chunks(pe, body, prologue, epilogue)

        @block.scalar
        def _(act):
            nc.scalar.preload_act_table(ACT.Silu)

            def upper_x(p):
                take(act, xT_ready)
                nc.scalar.activation(x_hi[:, p], t_ps[:], ACT.Copy).then_inc(x_hi_ready, 1)

            def squash():
                take(act, gates_ready)
                nc.scalar.activation(th[:].rearrange("p a e -> p (a e)"), t_ps[:, 0:NTQ * NE], ACT.Tanh, scale=0.5).then_inc(th_ready, 1)

            def upper_c(p):
                take(act, combT_ready)
                nc.scalar.activation(cT[0:2 * NE, p], t_ps[0:2 * NE, :], ACT.Copy)
                nc.scalar.activation(c_hi[2 * NE:4 * NE], t_ps[2 * NE:4 * NE, :], ACT.Copy).then_inc(c_hi_ready, 1)

            def silu(e, p):
                act.wait_ge(g_ready, e + 1)
                nc.scalar.activation(s[:, (e + p) % 2], g_ps[(e + p) % 2][:], ACT.Silu).then_inc(s_ready, 1)

            def upper_h(e, n):
                act.wait_ge(h_ready, n)
                act.sem_inc(banks_free, 1)
                nc.scalar.activation(h_hi[:, place(e)], h[:, place(e)], ACT.Copy).then_inc(h_hi_ready, 1)

            def read_y():
                take(act, y_ready)
                nc.scalar.activation(yT[:], y_ps[:], ACT.Copy).then_inc(yT_ready, 1)

            def prologue():
                upper_x(0)
                squash()
                upper_c(0)

            def body(q, p, first=False, last=False):
                for e in range(STEPS):
                    silu(e, p)
                    if e > 0:
                        upper_h(e - 1, e if first else e + 1)
                    elif not first:
                        upper_h(NE, 1)
                    if e == 3 and not first:
                        read_y()
                    if not last:
                        if e == 8:
                            upper_x(1 - p)
                        if e == 10:
                            squash()
                        if e == 14:
                            upper_c(1 - p)
                act.sem_inc(g_ready, -STEPS)
                if not last:
                    act.sem_inc(h_ready, -(STEPS - 1 if first else STEPS))

            def epilogue():
                upper_h(NE, STEPS + 1)
                read_y()

            chunks(act, body, prologue, epilogue)

        @block.vector
        def _(dve):
            take(dve, zeroed["dve"])

            def statistics(q):
                c = Chain(dve, dve_chain)
                for tt in range(NTQ):
                    ins = nc.vector.bn_stats(stats[:, tt], tile(q, tt))
                c.link(ins)
                for tt in range(NTQ):
                    ins = nc.vector.bn_aggr(mv[:, tt], stats[:, tt])
                ins.then_inc(stats_ready, 1)
                c.end()

            def normalise(q):
                take(dve, norm_ready)
                for tt in range(NTQ):
                    ins = nc.vector.tensor_scalar(xn[:, tt], tile(q, tt), mv[:, tt, 0:1], nrm[:, 0, tt:tt + 1], ALU.subtract, ALU.mult)
                ins.then_inc(xn_ready, 1)

            def lower_x(p):
                take(dve, x_hi_ready)
                nc.vector.tensor_tensor(x_lo[:, p], t_ps[:], x_hi[:, p], ALU.subtract).then_inc(x_ready, 1)

            def choose():
                c = Chain(dve, dve_chain)
                take(dve, th_ready)
                c.link(nc.vector.tensor_scalar(score[:], th[:], 1.0, 0.5, ALU.add, ALU.mult))
                c.link(nc.vector.tensor_tensor(sel[:], score[:], ew.bias[:].rearrange("p (o e) -> p o e", o=1).to_broadcast([P, NTQ, NE]), ALU.add))
                for tt in range(NTQ):
                    ins = nc.vector.max(top[:, tt], sel[:, tt])
                c.link(ins)
                for tt in range(NTQ):
                    ins = nc.vector.match_replace(left[:, tt], top[:, tt], sel[:, tt], TAKEN)
                c.link(ins)
                c.link(nc.vector.scalar_tensor_tensor(chosen[:], left[:], TAKEN, score[:], ALU.is_equal, ALU.mult))
                c.link(nc.vector.tensor_reduce(total[:, 0], chosen[:], AX.X, ALU.add))
                c.link(nc.vector.reciprocal(total[:, 1], total[:, 0]))
                for k in range(2):
                    r = total[:, 1].rearrange("p (a o) -> p a o", o=1).to_broadcast([P, NTQ, NE])
                    ins = nc.vector.scalar_tensor_tensor(comb[:, :, 2 * k * NE:(2 * k + 1) * NE], chosen[:], ROUTE_SCALE, r, ALU.mult, ALU.mult)
                ins.then_inc(comb_ready, 1)
                c.end()

            def lower_c(p):
                take(dve, c_hi_ready)
                rows = slice(2 * NE, 4 * NE)
                nc.vector.tensor_tensor(cT[rows, p], t_ps[rows, :], c_hi[rows], ALU.subtract).then_inc(cT_ready, 1)

            def hidden(e, p):
                bank = (e + p) % 2
                dve.wait_ge(s_ready, e + 1)
                dve.wait_ge(u_ready, e + 1)
                if e == NE:
                    nc.vector.tensor_tensor(h[:, place(e)], s[:, bank], u_ps[bank][:], ALU.mult).then_inc(h_ready, 1)
                    return
                nc.vector.tensor_tensor(su[:, bank], s[:, bank], u_ps[bank][:], ALU.mult).then_inc(core_chain, 1)
                dve.wait_ge(core_chain, e + 1)
                nc.vector.tensor_tensor(h[:, place(e)], su[:, bank], c_ps[bank][:], ALU.mult).then_inc(h_ready, 1)

            def update(q):
                take(dve, o_ready)
                xs = x_sb[:, bass.ds(q * NTQ, NTQ), :]
                nc.vector.tensor_tensor(xs, t_ps[:].rearrange("p (a d) -> p a d", a=NTQ), xs, ALU.add)

            def prologue():
                statistics(0)
                normalise(0)
                lower_x(0)
                choose()
                lower_c(0)

            def body(q, p, first=False, last=False):
                for e in range(STEPS):
                    hidden(e, p)
                    if e == 4 and not first:
                        update(q - 1)
                    if not last:
                        if e == 4:
                            statistics(q + 1)
                        if e == 6:
                            normalise(q + 1)
                        if e == 8:
                            lower_x(1 - p)
                        if e == 11:
                            choose()
                        if e == 15:
                            lower_c(1 - p)
                dve.sem_inc(s_ready, -STEPS)
                dve.sem_inc(u_ready, -STEPS)
                dve.sem_inc(core_chain, -NE)

            chunks(dve, body, prologue, lambda: update(NQ - 1))


def attention_layer(nc, sems, x_sb, w, ident, ident16, half):
    ctx = ExitStack()
    with ctx:
        def sb(name, shape, dt=FP32):
            return ctx.enter_context(nc.sbuf_tensor("a_" + name, shape, dt))

        def pb(name, width=512):
            return ctx.enter_context(nc.psum_tensor("a_" + name, [P, width], FP32))

        def sem(name):
            return sems.enter_context(nc.semaphore("a_" + name))

        W = NH * DH
        SLOT = 32

        qkvg_w = sb("qkvg_w", [P, 4 * W])
        qkvg_b = sb("qkvg_b", [P, 4 * W])
        out_w = sb("out_w", [P, DM])
        out_b = sb("out_b", [P, DM])

        stats = sb("stats", [P, TT, 6])
        mv = sb("mv", [P, TT, 2])
        nrm = sb("nrm", [P, 4, TT])
        xn = sb("xn", [P, TT, DM])
        z = sb("z", [P, TT, DM])
        zT = sb("zT", [P, T])
        qkvg = sb("qkvg", [P, 2, TT, 4 * W])
        qk = sb("qk", [P, TT, 2, NH, SLOT], FP16)
        square = sb("square", [P, TT, 2 * W])
        norms = sb("norms", [P, 2, TT, 2 * NH])
        qkT = sb("qkT", [P, 2, 2, HG, T], FP16)
        v = sb("v", [P, 2, TT, NH, SLOT])
        gate = sb("gate", [P, 2, TT, W])
        d = sb("d", [P, 2, NH, TT * T])
        avT = sb("avT", [P, HG, T])
        den = sb("den", [P, 2, TT, NH])
        o = sb("o", [P, TT, W])
        oT = sb("oT", [P, T])

        near = sb("near", [P, 1])

        s_ps = [pb("s0"), pb("s1")]
        av_ps = [pb("av0"), pb("av1")]
        t_ps = [pb("t0"), pb("t1")]
        u_ps = pb("u", 1024)

        loaded = sem("loaded")
        near_made = sem("near_made")
        w_ready = {e: sem("w_ready_" + e) for e in ("dve", "pool", "pe")}
        made = {e: sem("made_" + e) for e in ("dve", "pe")}
        pool_chain, dve_chain, act_chain, d_chain = sem("pool_chain"), sem("dve_chain"), sem("act_chain"), sem("d_chain")
        stats_ready, norm_ready, z_ready, zT_ps_ready, zT_ready = (sem(n) for n in ("stats_ready", "norm_ready", "z_ready", "zT_ps_ready", "zT_ready"))
        p_ready, qkvg_ready, hi_ready, sq_ready, v_ready, res_ready = (sem(n) for n in ("p_ready", "qkvg_ready", "hi_ready", "sq_ready", "v_ready", "res_ready"))
        xn_ready, gate_ready, gate_free = sem("xn_ready"), sem("gate_ready"), sem("gate_free")
        qk_ready, qkT_ps_ready, qkT_ready = sem("qk_ready"), sem("qkT_ps_ready"), sem("qkT_ready")
        s_ready, s_free, d_ready, w_done = sem("s_ready"), sem("s_free"), sem("d_ready"), sem("w_done")
        av_ready, avT_ready, u_ready, o_ready, oT_ps_ready, oT_ready, y_ready = (
            sem(n) for n in ("av_ready", "avT_ready", "u_ready", "o_ready", "oT_ps_ready", "oT_ready", "y_ready"))

        def batches(eng, body, prologue, epilogue):
            prologue()
            body(-1, 1, core=False, tail=False)
            body(0, 0, tail=False)
            with eng.Fori(0, NB // 2 - 2) as i:
                body(i * 2 + 1, 1)
                body(i * 2 + 2, 0)
            body(NB - 3, 1, further=False)
            body(NB - 2, 0, further=False, ahead=False)
            body(NB - 1, 1, further=False, ahead=False, heads=False)
            epilogue()

        def tile(b, tt):
            return x_sb[:, bass.ds(b * TT + tt, 1), :].rearrange("p o d -> p (o d)")

        def by_head(p, part):
            return qkvg[:, p, :, part * W:(part + 1) * W].rearrange("p a (h d) -> p a h d", d=DH)

        block = ctx.enter_context(nc.Block())

        @block.sync
        def _(sp):
            for dst, name in ((qkvg_w, "qkvg_w"), (qkvg_b, "qkvg_b"), (out_w, "attn_out_w"), (out_b, "attn_out_b")):
                sp.dma_start(dst[:], w[name]).then_inc(loaded, 16)
            sp.wait_ge(loaded, 64)
            for s in w_ready.values():
                sp.sem_inc(s, 1)

        @block.gpsimd
        def _(pool):
            chain = Chain(pool, pool_chain)
            nc.gpsimd.memset(qk[:], 0.0)
            chain.link(nc.gpsimd.memset(v[:], 0.0))
            nc.gpsimd.memset(qk[:, :, 0, :, 26:28], 1.0)
            nc.gpsimd.memset(qk[:, :, 1, :, 24:26], 1.0)
            chain.link(nc.gpsimd.memset(v[:, :, :, :, DH:DH + 1], 1.0))
            chain.end()
            for s in made.values():
                pool.sem_inc(s, 1)
            pool.wait_ge(w_ready["pool"], 1)

            def norm():
                c = Chain(pool, pool_chain)
                take(pool, stats_ready)
                c.link(nc.gpsimd.tensor_scalar(nrm[:, 1], mv[:, :, 1], LN_EPS, 1.0, ALU.add, ALU.mult))
                c.link(nc.gpsimd.tensor_tensor(nrm[:, 0], nrm[:, 1], half[:, 0:TT], ALU.pow))
                c.link(nc.gpsimd.tensor_tensor(nrm[:, 1], nrm[:, 0], nrm[:, 0], ALU.mult))
                c.link(nc.gpsimd.tensor_tensor(nrm[:, 1], nrm[:, 1], mv[:, :, 1], ALU.mult))
                c.link(nc.gpsimd.tensor_scalar(nrm[:, 1], nrm[:, 1], LN_EPS, 1.0, ALU.add, ALU.mult))
                c.link(nc.gpsimd.tensor_tensor(nrm[:, 2], nrm[:, 1], half[:, 0:TT], ALU.pow))
                nc.gpsimd.tensor_tensor(nrm[:, 3], nrm[:, 2], nrm[:, 0], ALU.mult).then_inc(norm_ready, 1)
                c.end()

            def residual(b):
                c = Chain(pool, pool_chain)
                take(pool, xn_ready)
                own = x_sb[:, bass.ds(b * TT, TT), :]
                c.link(nc.gpsimd.tensor_tensor(own, own, xn[:], ALU.add))
                nc.gpsimd.tensor_tensor(own, own, out_b[:].rearrange("p (o d) -> p o d", o=1).to_broadcast([P, TT, DM]), ALU.add).then_inc(res_ready, 1)
                c.end()

            def pack(p):
                take(pool, qkvg_ready)
                for side in range(2):
                    ins = nc.gpsimd.tensor_scalar(qk[:, :, side, :, 0:DH], by_head(p, side), 1.0, 1.0, ALU.mult, ALU.mult)
                ins.then_inc(hi_ready, 1)
                qk_cols = qkvg[:, p, :, 0:2 * W]
                nc.gpsimd.tensor_tensor(square[:], qk_cols, qk_cols, ALU.mult).then_inc(sq_ready, 1)
                for side, at in ((0, 2 * DH), (1, DH)):
                    ins = nc.gpsimd.tensor_scalar(qk[:, :, side, :, at:at + DH], by_head(p, side), 1.0, 1.0, ALU.mult, ALU.mult)
                ins.then_inc(hi_ready, 1)

            def keep(p):
                nc.gpsimd.tensor_scalar(v[:, p, :, :, 0:DH], by_head(p, 2), 1.0, 1.0, ALU.mult, ALU.mult).then_inc(v_ready, 1)
                nc.gpsimd.tensor_scalar(gate[:, p], qkvg[:, p, :, 3 * W:4 * W], 1.0, 1.0, ALU.mult, ALU.mult).then_inc(gate_ready, 1)

            def prologue():
                norm()
                residual(0)
                pack(0)
                norm()

            def body(b, p, core=True, tail=True, heads=True, ahead=True, further=True):
                if ahead:
                    residual(b + 2)
                if tail:
                    take(pool, gate_free)
                if heads:
                    keep(1 - p)
                if ahead:
                    pack(p)
                if further:
                    norm()

            batches(pool, body, prologue, lambda: None)

        @block.tensor
        def _(pe):
            pe.wait_ge(w_ready["pe"], 1)
            pe.wait_ge(made["pe"], 1)
            scores_read, weights = Lagged(pe, s_free, 2, NH), Lagged(pe, w_done, 1, HG)

            def transpose_z():
                take(pe, z_ready)
                for tt in range(TT):
                    ins = nc.tensor.transpose(t_ps[0][:, tt * P:(tt + 1) * P], z[:, tt], ident[:])
                ins.then_inc(zT_ps_ready, 1)

            def project():
                take(pe, zT_ready)
                for tt in range(TT):
                    nc.tensor.matmul(t_ps[tt][:], zT[:, tt * P:(tt + 1) * P], qkvg_w[:], start=True, stop=True).then_inc(p_ready, 1)

            def transpose_qk():
                take(pe, qk_ready)
                for tt in range(TT):
                    t16 = t_ps[tt][:].bitcast(FP16)
                    for side in range(2):
                        for g in range(HG):
                            k = side * HG + g
                            ins = nc.tensor.transpose(t16[:, k * P:(k + 1) * P], qk[:, tt, side, 4 * g:4 * g + 4].rearrange("p h k -> p (h k)"), ident16[:])
                    ins.then_inc(qkT_ps_ready, 1)

            def score(h, p, first):
                g, j = divmod(h, 4)
                rows = slice(SLOT * j, SLOT * (j + 1))
                scores_read.wait(h - 2, first)
                for kc in range(TT):
                    ins = nc.tensor.matmul(s_ps[h % 2][:, kc * T:(kc + 1) * T], qkT[rows, p, 1, g, kc * P:(kc + 1) * P], qkT[rows, p, 0, g, :], start=True, stop=True)
                ins.then_inc(s_ready, 1)

            def weigh(g, p):
                for kc in range(TT):
                    for j in range(4):
                        h = 4 * g + j
                        ins = nc.tensor.matmul(av_ps[g // 2][SLOT * j:SLOT * (j + 1), (g % 2) * T:(g % 2 + 1) * T],
                                               v[:, p, kc, h], d[:, p, h, kc * T:(kc + 1) * T], start=(kc == 0), stop=(kc == TT - 1))
                if g % 2:
                    ins.then_inc(av_ready, 1)

            def transpose_av():
                take(pe, avT_ready)
                for tt in range(TT):
                    for g in range(HG):
                        ins = nc.tensor.transpose(u_ps[:, tt * 512 + g * P:tt * 512 + (g + 1) * P], avT[:, g, tt * P:(tt + 1) * P], ident[:])
                ins.then_inc(u_ready, 1)

            def transpose_o():
                take(pe, o_ready)
                for tt in range(TT):
                    ins = nc.tensor.transpose(u_ps[:, tt * P:(tt + 1) * P], o[:, tt], ident[:])
                ins.then_inc(oT_ps_ready, 1)

            def project_out():
                take(pe, oT_ready)
                for tt in range(TT):
                    ins = nc.tensor.matmul(u_ps[:, 512 + tt * DM:512 + (tt + 1) * DM], oT[:, tt * P:(tt + 1) * P], out_w[:], start=True, stop=True)
                ins.then_inc(y_ready, 1)

            def prologue():
                transpose_z()
                project()
                transpose_qk()

            def body(b, p, core=True, tail=True, heads=True, ahead=True, further=True):
                for h in range(NH):
                    if heads:
                        if h == 0:
                            take(pe, qkT_ready, TT)
                        score(h, 1 - p, not core)
                    if h == 1 and tail:
                        weights.wait(-1)
                        weigh(HG - 1, 1 - p)
                    if h == 2 and ahead:
                        transpose_z()
                    if h == 4 and tail:
                        transpose_av()
                    if h == 6 and ahead:
                        project()
                    if h == 8 and tail:
                        transpose_o()
                    if h == 11 and tail:
                        project_out()
                    if h == 9 and core:
                        take(pe, v_ready)
                    if h in (9, 11, 14) and core:
                        g = (9, 11, 14).index(h)
                        weights.wait(g, not tail)
                        weigh(g, p)
                    if h == 13 and ahead:
                        transpose_qk()
                if heads:
                    scores_read.end(not core, False)
                if core:
                    weights.end(not tail, not heads)

            def epilogue():
                weights.wait(HG - 1)
                weigh(HG - 1, 1)
                transpose_av()
                transpose_o()
                project_out()

            batches(pe, body, prologue, epilogue)

        @block.scalar
        def _(act):
            def body(b, p, core=True, tail=True, heads=True, ahead=True, further=True):
                def group(g):
                    return d[:, p, 4 * g:4 * g + 4].rearrange("p h k -> p (h k)")

                if not core:
                    return
                for g in range(HG):
                    if g % 2 == 0:
                        take(act, d_ready)
                    nc.scalar.activation(group(g), group(g), ACT.Sqrt).then_inc(act_chain, 1)
                nc.scalar.preload_act_table_set("natural_log_exp_and_others")
                for g in range(HG + 1):
                    if g < HG:
                        act.wait_ge(act_chain, g + 1)
                        nc.scalar.activation(group(g), group(g), ACT.Ln, bias=near[:, 0:1]).then_inc(act_chain, 1)
                    if g > 0:
                        act.wait_ge(act_chain, HG + g)
                        nc.scalar.activation(group(g - 1), group(g - 1), ACT.Exp, scale=-2.0).then_inc(w_done, 1)
                act.sem_inc(act_chain, -2 * HG)

            act.wait_ge(near_made, 1)
            batches(act, body, lambda: None, lambda: None)

        @block.vector
        def _(dve):
            nc.vector.memset(near[:], SHEP_EPS).then_inc(near_made, 1)
            dve.wait_ge(w_ready["dve"], 1)
            dve.wait_ge(made["dve"], 1)

            def statistics(b):
                c = Chain(dve, dve_chain)
                for tt in range(TT):
                    ins = nc.vector.bn_stats(stats[:, tt], tile(b, tt))
                c.link(ins)
                for tt in range(TT):
                    ins = nc.vector.bn_aggr(mv[:, tt], stats[:, tt])
                ins.then_inc(stats_ready, 1)
                c.end()

            def normalise(b):
                take(dve, norm_ready)
                for out, k, ready in ((z, 3, z_ready), (xn, 0, xn_ready)):
                    for tt in range(TT):
                        ins = nc.vector.tensor_scalar(out[:, tt], tile(b, tt), mv[:, tt, 0:1], nrm[:, k, tt:tt + 1], ALU.subtract, ALU.mult)
                    ins.then_inc(ready, 1)

            def read_zT():
                take(dve, zT_ps_ready)
                nc.vector.tensor_copy(zT[:], t_ps[0][:, 0:T]).then_inc(zT_ready, 1)

            def read_qkvg(p):
                for tt in range(TT):
                    dve.wait_ge(p_ready, tt + 1)
                    ins = nc.vector.tensor_tensor(qkvg[:, p, tt], t_ps[tt][:], qkvg_b[:], ALU.add)
                dve.sem_inc(p_ready, -TT)
                c = Chain(dve, dve_chain)
                c.link(ins)
                dve.sem_inc(qkvg_ready, 1)
                c.end()

            def split_qk(p):
                c = Chain(dve, dve_chain)
                take(dve, hi_ready, 2)
                for side, at in ((0, DH), (1, 2 * DH)):
                    nc.vector.tensor_tensor(qk[:, :, side, :, at:at + DH], by_head(p, side), qk[:, :, side, :, 0:DH], ALU.subtract)
                take(dve, sq_ready)
                c.link(nc.vector.tensor_reduce(norms[:, 0], square[:].rearrange("p a (h d) -> p a h d", d=DH), AX.X, ALU.add))
                c.link(nc.vector.tensor_scalar(norms[:, 1], norms[:, 0], -0.5, None, ALU.mult))
                for side, at in ((0, 24), (1, 26)):
                    ins = nc.vector.tensor_copy(qk[:, :, side, :, at], norms[:, 1, :, side * NH:(side + 1) * NH])
                c.link(ins)
                for side, at in ((0, 24), (1, 26)):
                    ins = nc.vector.tensor_tensor(qk[:, :, side, :, at + 1], norms[:, 1, :, side * NH:(side + 1) * NH], qk[:, :, side, :, at], ALU.subtract)
                ins.then_inc(qk_ready, 1)
                c.end()

            def read_qkT(p):
                for tt in range(TT):
                    dve.wait_ge(qkT_ps_ready, tt + 1)
                    nc.vector.tensor_copy(qkT[:, p, :, :, tt * P:(tt + 1) * P].rearrange("p s g t -> p (s g) t"),
                                          t_ps[tt][:].bitcast(FP16).rearrange("p (k t) -> p k t", t=P)).then_inc(qkT_ready, 1)
                dve.sem_inc(qkT_ps_ready, -TT)

            def distance(h, p):
                dve.wait_ge(s_ready, h + 1)
                ins = nc.vector.tensor_scalar(d[:, p, h], s_ps[h % 2][:], -2.0, 0.0, ALU.mult, ALU.max)
                if h % 8 == 7:
                    ins.then_inc(d_chain, 1)
                    take(dve, d_chain)
                    dve.sem_inc(s_free, 1)
                    dve.sem_inc(d_ready, 1)
                else:
                    ins.then_inc(s_free, 1)

            def read_av(k):
                take(dve, av_ready)
                ins = nc.vector.tensor_copy(avT[:, 2 * k:2 * k + 2].rearrange("p g t -> p (g t)"), av_ps[k][:])
                if k == 1:
                    ins.then_inc(avT_ready, 1)

            def norm_and_gate(p):
                c = Chain(dve, dve_chain)
                take(dve, u_ready)
                u = u_ps[:].rearrange("p (a h k) -> p a h k", a=TT, k=SLOT)
                oh = o[:].rearrange("p a (h d) -> p a h d", d=DH)
                c.link(nc.vector.tensor_scalar(den[:, 0], u[:, :, :, DH], SHEP_EPS, None, ALU.add))
                c.link(nc.vector.reciprocal(den[:, 1], den[:, 0]))
                c.link(nc.vector.tensor_tensor(oh, u[:, :, :, 0:DH], den[:, 1].rearrange("p a (h o) -> p a h o", o=1).to_broadcast([P, TT, NH, DH]), ALU.mult))
                c.link(nc.vector.tensor_tensor(o[:], o[:], gate[:, p], ALU.mult))
                dve.sem_inc(o_ready, 1)
                dve.sem_inc(gate_free, 1)
                c.end()

            def read_oT():
                take(dve, oT_ps_ready)
                nc.vector.tensor_copy(oT[:], u_ps[:, 0:T]).then_inc(oT_ready, 1)

            def update(b):
                take(dve, y_ready)
                take(dve, res_ready)
                own = x_sb[:, bass.ds(b * TT, TT), :]
                nc.vector.tensor_tensor(own, u_ps[:, 512:512 + TT * DM].rearrange("p (a d) -> p a d", a=TT), own, ALU.add)

            def prologue():
                statistics(0)
                normalise(0)
                statistics(1)
                read_zT()
                read_qkvg(0)
                split_qk(0)
                read_qkT(0)

            def body(b, p, core=True, tail=True, heads=True, ahead=True, further=True):
                for h in range(NH):
                    if heads:
                        distance(h, 1 - p)
                    if h == 0 and ahead:
                        normalise(b + 2)
                    if h == 1 and tail:
                        read_av(0)
                    if h == 3 and tail:
                        read_av(1)
                    if h == 4 and ahead:
                        read_zT()
                    if h == 6 and tail:
                        norm_and_gate(1 - p)
                    if h == 7 and core:
                        take(dve, gate_ready)
                    if h == 8 and ahead:
                        read_qkvg(p)
                    if h == 9 and tail:
                        read_oT()
                    if h == 11 and ahead:
                        split_qk(p)
                    if h == 13 and tail:
                        update(b - 1)
                    if h == 13 and further:
                        statistics(b + 3)
                    if h == 15 and ahead:
                        read_qkT(p)
                if heads:
                    dve.sem_inc(s_ready, -NH)

            def epilogue():
                read_av(0)
                read_av(1)
                norm_and_gate(1)
                read_oT()
                update(NB - 1)

            batches(dve, body, prologue, epilogue)


def program(nc, x, w, out, layers=("mamba", "experts", "attention", "experts")):
    ctx = ExitStack()
    sems = ctx
    with ctx:
        x_sb = ctx.enter_context(nc.sbuf_tensor("x_sb", [P, NT, DM], FP32))
        ident = ctx.enter_context(nc.sbuf_tensor("ident", [P, P], FP32))
        ident16 = ctx.enter_context(nc.sbuf_tensor("ident16", [P, P], FP16))
        half = ctx.enter_context(nc.sbuf_tensor("half", [P, QC // P], FP32))
        x_loaded = ctx.enter_context(nc.semaphore("x_loaded"))
        made = ctx.enter_context(nc.semaphore("constants_made"))

        with nc.Block() as block:
            @block.sync
            def _(sp):
                sp.dma_start(x_sb[:], x.rearrange("b (n p) d -> p (b n) d", p=P)).then_inc(x_loaded, 16)
                sp.wait_ge(x_loaded, 16)

            @block.gpsimd
            def _(pool):
                nc.gpsimd.memset(half[:], -0.5)
                nc.gpsimd.memset(ident[:], 0.0)
                nc.gpsimd.memset(ident16[:], 0.0).then_inc(made, 1)
                pool.wait_ge(made, 1)
                for i in (ident, ident16):
                    nc.gpsimd.affine_select(out=i[:], in_=i[:], compare_op=ALU.not_equal, fill=1.0, base=0,
                                            pattern=[[-1, P]], channel_multiplier=1)

        ew = ExpertWeights(nc, ctx)
        split_expert_weights(nc, ew, w)
        for n, layer in enumerate(layers):
            if layer == "mamba":
                mamba_layer(nc, sems, x_sb, w, ident, half)
            if layer == "experts":
                expert_layer(nc, sems, n, x_sb, ew, ident, half)
            if layer == "attention":
                attention_layer(nc, sems, x_sb, w, ident, ident16, half)

        stored = ctx.enter_context(nc.semaphore("stored"))
        with nc.Block() as block:
            @block.sync
            def _(sp):
                sp.dma_start(out.rearrange("b (n p) d -> p (b n) d", p=P), x_sb[:]).then_inc(stored, 16)
                sp.wait_ge(stored, 16)


def layout(v):
    import numpy as np
    g = {k: np.asarray(a) for k, a in v.items()}
    a = {k[len("L0_attn_a_"):]: g[k] for k in g if k.startswith("L0_attn_a_")}
    b = {k[len("L0_attn_b_"):]: g[k] for k in g if k.startswith("L0_attn_b_")}
    f = {k[len("L0_ffn_"):]: g[k] for k in g if k.startswith("L0_ffn_")}

    def chunks(m):
        return m.reshape(-1, P, *m.shape[1:]).swapaxes(0, 1)

    def spread(m, one):
        bc, dl = m[..., DTR:], m[..., :DTR]
        zero = np.zeros((*m.shape[:-1], 16), m.dtype)
        return np.concatenate([bc, dl, zero[..., :1] + one, zero[..., 1:], bc, zero, zero], -1)

    def rows(m):
        return np.repeat(m.reshape(1, -1), P, 0)

    w = {
        "in_w": a["in_W"], "in_b": a["in_b"].reshape(-1, P).T, "rms_w": a["rms_w"].reshape(P, 1),
        "conv_w": chunks(a["conv_w"]), "conv_b": a["conv_b"].reshape(-1, P).T, "a_log": chunks(a["A_log"]),
        "dbc_w": chunks(spread(a["dbc_W"], 0)), "dbc_b": spread(a["dbc_b"], 1).reshape(P, 1),
        "dup_w": np.concatenate([a["dup_W"], a["dup_b"][None]]),
        "out_w": chunks(a["out_W"]), "out_b": rows(a["out_b"]),
    }
    w["gate_up"] = np.stack([np.concatenate([f["w_gate"], f["shared_gate_w"][None]]),
                             np.concatenate([f["w_up"], f["shared_up_w"][None]])]).transpose(3, 1, 0, 2)
    w["down"] = np.concatenate([f["w_down"], f["shared_down_w"][None]]).transpose(2, 0, 1)
    w["router"] = f["gate_w"].T
    w["expert_bias"] = rows(f["expert_bias"])
    q = b["W_in"].reshape(NH, 4, DH, DM).transpose(1, 0, 2, 3).reshape(4 * NH * DH, DM)
    w["qkvg_w"] = q.T
    w["qkvg_b"] = rows(b["b_in"].reshape(NH, 4, DH).transpose(1, 0, 2))
    w["attn_out_w"] = b["W_out"].T
    w["attn_out_b"] = rows(b["b_out"])
    return {k: np.ascontiguousarray(m) for k, m in w.items()}


def kernel(**inputs):
    import numpy as np
    import concourse.bacc as bacc
    from concourse.bass_utils import run_bass_kernel_spmd as run

    nc = bacc.Bacc("TRN2", target_bir_lowering=False, num_devices=1)
    x = np.ascontiguousarray(inputs["L0_attn_a_x"])
    arrays = {"x": x, **{"w_" + k: m for k, m in layout(inputs).items()}}
    dram = {k: nc.dram_tensor(k, m.shape, FP32, kind="ExternalInput").ap() for k, m in arrays.items()}
    out = nc.dram_tensor("out", x.shape, FP32, kind="ExternalOutput").ap()
    program(nc, dram["x"], {k[2:]: a for k, a in dram.items() if k != "x"}, out)
    r = run(nc, [arrays], core_ids=[0])
    return r.results[0]["out"]
```

```python
import concourse.bass as bass
from concourse import mybir
from contextlib import ExitStack

FP32 = mybir.dt.float32
FP16 = mybir.dt.float16
ALU = mybir.AluOpType
ACT = mybir.ActivationFunctionType
AX = mybir.AxisListType

P = 128
NB, T, DM = 16, 256, 128
TT = T // P
NT = NB * TT
DI, NS, DTR, KC = 256, 16, 16, 4
DC = DI // P
NE = 16
TOPK = 8
ROUTE_SCALE = 2.826
QC = 4 * P
NQ = NB * T // QC
NH, DH = 16, 8
HG = 4
LN_EPS = 1e-5
RMS_EPS = 1e-6
SHEP_EPS = 1e-4
W_SCALE = 64.0
TAKEN = -1e30


class Chain:

    def __init__(self, eng, sem):
        self.eng, self.sem, self.n = eng, sem, 0

    def link(self, ins):
        self.n += 1
        ins.then_inc(self.sem, 1)
        self.eng.wait_ge(self.sem, self.n)

    def end(self):
        if self.n:
            self.eng.sem_inc(self.sem, -self.n)
        self.n = 0


def take(eng, sem, n=1):
    eng.wait_ge(sem, n)
    eng.sem_inc(sem, -n)


class Lagged:

    def __init__(self, eng, sem, lag, n, which=None):
        self.eng, self.sem, self.lag, self.n = eng, sem, lag, n
        self.which = range(n) if which is None else which

    def count(self, start, stop):
        return sum(1 for k in range(start, stop) if k % self.n in self.which)

    def start(self, first):
        return max(0, -self.lag) if first else -self.lag

    def wait(self, k, first=False):
        c = self.count(self.start(first), k + 1)
        if k % self.n in self.which and c > 0:
            self.eng.wait_ge(self.sem, c)

    def end(self, first, last):
        if not last:
            self.eng.sem_inc(self.sem, -self.count(self.start(first), self.n - self.lag))


def mamba_layer(nc, sems, x_sb, mw, loaded, later, ew, ident, half):
    ctx = ExitStack()
    with ctx:
        def sb(name, shape, dt=FP32):
            return ctx.enter_context(nc.sbuf_tensor("m_" + name, shape, dt))

        def pb(name, dt=FP32, width=512):
            return ctx.enter_context(nc.psum_tensor("m_" + name, [P, width], dt))

        def sem(name):
            return sems.enter_context(nc.semaphore("m_" + name))

        in_w, in_b, rms_w, conv_w, conv_b, neg_a, dbc_w, dbc_b, dup_w, out_w, out_b = (mw.sb[n] for n in mw.NAMES)
        pick = sb("pick", [96, 2 * NS, P], FP16)

        stats = sb("stats", [P, TT, 6])
        mv = sb("mv", [P, TT, 2])
        nrm = sb("nrm", [P, 4, TT])
        xn = sb("xn", [P, TT, DM])
        z = sb("z", [P, TT, DM])
        hT = sb("hT", [P, T])
        xpad = sb("xpad", [P, DC, KC - 1 + T])
        taps = sb("taps", [P, DC, KC, P])
        xs = sb("xs", [P, DC, T])
        bcd = sb("bcd", [P, T])
        bc_hi = sb("bc_hi", [96, T], FP16)
        sp = sb("sp", [P, DC, T])
        gate = sb("gate", [P, 2, DC, T])
        delta = sb("delta", [P, 2, DC, T])
        dx = sb("dx", [P, 2, DC, T])
        bc = sb("bc", [96, 2, T], FP16)
        decay = sb("decay", [P, 4, 2, DC, T])
        h = sb("h", [P, 4, 2, DC, T])
        c_sb = sb("c_sb", [P, 2, 2 * T])
        hc = sb("hc", [P, 4, 2, DC, T])
        yg = sb("yg", [P, DC, T])

        b_ps = [pb("b_ps0"), pb("b_ps1")]
        c_ps = [pb("c_ps0"), pb("c_ps1")]
        y_ps = pb("y_ps")
        t0, t1, t2 = pb("t0"), pb("t1"), pb("t2")

        raw_ready, upper = sem("raw_ready"), {e: sem("upper_" + e) for e in ("dve", "pool")}
        zeros_made = {e: sem("zeros_made_" + e) for e in ("act", "pe")}
        pick_zeroed = sem("pick_zeroed")
        pick_made, taps_made, z_read, gate_free = sem("pick_made"), sem("taps_made"), sem("z_read"), sem("gate_free")
        pool_chain, dve_chain, act_chain = sem("pool_chain"), sem("dve_chain"), sem("act_chain")
        stats_ready, norm_ready, xn_ready, res_ready = (sem(n) for n in ("stats_ready", "norm_ready", "xn_ready", "res_ready"))
        delta_made, dx_ready = sem("delta_made"), sem("dx_ready")
        z_ready, zT_ready, hT_ready = sem("z_ready"), sem("zT_ready"), sem("hT_ready")
        x1_ready, g_ready, xpad_ready, conv_ready, xs_ready = (sem(n) for n in ("x1_ready", "g_ready", "xpad_ready", "conv_ready", "xs_ready"))
        dbc_ready, bcd_ready, bc_hi_ready, bc_ready = (sem(n) for n in ("dbc_ready", "bcd_ready", "bc_hi_ready", "bc_ready"))
        dup_ready, sp_ready, delta_ready = (sem(n) for n in ("dup_ready", "sp_ready", "delta_ready"))
        t2_free = sem("t2_free")
        b_ready, c_ready, decay_ready = sem("b_ready"), sem("c_ready"), sem("decay_ready")
        core_chain, hc_chain, c_chain = sem("core_chain"), sem("hc_chain"), sem("c_chain")
        b_free, c_free, decay_free, h_free, c_sb_free = (sem(n) for n in ("b_free", "c_free", "decay_free", "h_free", "c_sb_free"))
        h_ready, c_sb_ready = sem("h_ready"), sem("c_sb_ready")
        hc_dve, hc_pool = sem("hc_dve"), sem("hc_pool")
        y_ready, yg_ready, o_ready = sem("y_ready"), sem("yg_ready"), sem("o_ready")

        PAIRS = NS // 2
        LAG = 2
        POOL_PAIRS = (1, 2, 3, 4, 5, 6)
        DVE_PAIRS = tuple(m for m in range(PAIRS) if m not in POOL_PAIRS)

        NORM_AFTER, RES_AFTER = 2, 6

        def c_place(m):
            return POOL_PAIRS.index(m) % 2

        def tile(b, tt):
            return x_sb[:, bass.ds(b * TT + tt, 1), :].rearrange("p o d -> p (o d)")

        def batches(eng, body, prologue, epilogue):
            prologue()
            body(0, 0, first=True)
            with eng.Fori(0, NB // 2 - 2) as i:
                body(i * 2 + 1, 1)
                body(i * 2 + 2, 0)
            body(NB - 3, (NB - 3) % 2)
            body(NB - 2, (NB - 2) % 2, ahead=False)
            body(NB - 1, (NB - 1) % 2, ahead=False, last=True)
            epilogue()

        block = ctx.enter_context(nc.Block())

        @block.sync
        def _(sp_eng):
            sp_eng.wait_ge(loaded["mamba"], 16 * len(mw.NAMES))
            for dst, src, ready in later:
                sp_eng.dma_start(dst, src).then_inc(ready, 16)
            sp_eng.wait_ge(loaded["experts"], 16 * len(ew.NAMES))
            sp_eng.sem_inc(raw_ready, 1)

        @block.gpsimd
        def _(pool):
            def zeros():
                c = Chain(pool, pool_chain)
                nc.gpsimd.memset(bc[:], 0.0)
                nc.gpsimd.memset(xpad[:, :, 0:KC - 1], 0.0)
                c.link(nc.gpsimd.memset(decay[:, :, :, :, 0:1], 0.0))
                c.end()
                for s in zeros_made.values():
                    pool.sem_inc(s, 1)

            def make_pick():
                c = Chain(pool, pool_chain)
                for base in (0, -64):
                    c.link(nc.gpsimd.affine_select(out=pick[:], in_=pick[:], compare_op=ALU.not_equal, fill=1.0,
                                                   base=base, pattern=[[-1, 2 * NS], [0, P]], channel_multiplier=1))
                c.end()
                pool.sem_inc(pick_made, 1)

            def norm():
                c = Chain(pool, pool_chain)
                take(pool, stats_ready)
                c.link(nc.gpsimd.tensor_scalar(nrm[:, 1, :], mv[:, :, 1], LN_EPS, 1.0, ALU.add, ALU.mult))
                c.link(nc.gpsimd.tensor_tensor(nrm[:, 0, :], nrm[:, 1, :], half[:, 0:TT], ALU.pow))
                c.link(nc.gpsimd.tensor_tensor(nrm[:, 1, :], nrm[:, 0, :], nrm[:, 0, :], ALU.mult))
                c.link(nc.gpsimd.tensor_tensor(nrm[:, 1, :], nrm[:, 1, :], mv[:, :, 1], ALU.mult))
                c.link(nc.gpsimd.tensor_scalar(nrm[:, 1, :], nrm[:, 1, :], RMS_EPS, 1.0, ALU.add, ALU.mult))
                c.link(nc.gpsimd.tensor_tensor(nrm[:, 2, :], nrm[:, 1, :], half[:, 0:TT], ALU.pow))
                nc.gpsimd.tensor_tensor(nrm[:, 3, :], nrm[:, 2, :], nrm[:, 0, :], ALU.mult).then_inc(norm_ready, 1)
                c.end()

            def residual(b):
                c = Chain(pool, pool_chain)
                take(pool, xn_ready)
                own = x_sb[:, bass.ds(b * TT, TT), :]
                c.link(nc.gpsimd.tensor_tensor(own, own, xn[:], ALU.add))
                c.link(nc.gpsimd.tensor_tensor(own, own, out_b[:].rearrange("p (o d) -> p o d", o=1).to_broadcast([P, TT, DM]), ALU.add))
                c.end()
                pool.sem_inc(res_ready, 1)

            def split_bc(p):
                take(pool, bc_hi_ready)
                c = Chain(pool, pool_chain)
                c.link(nc.gpsimd.tensor_tensor(bc[64:96, p], bcd[64:96], bc_hi[64:96], ALU.subtract))
                c.end()
                pool.sem_inc(bc_ready, 1)

            def make_dx(p):
                take(pool, delta_made)
                nc.gpsimd.tensor_tensor(dx[:, p], delta[:, p], xs[:], ALU.mult).then_inc(dx_ready, 1)

            def prologue():
                zeros()
                take(pool, pick_zeroed)
                ew.make_pick(nc, 0, Chain(pool, pool_chain))
                pool.wait_ge(loaded["mamba"], 16 * len(mw.NAMES))
                norm()
                residual(0)
                norm()
                make_pick()
                split_bc(0)
                residual(1)
                make_dx(0)
                ew.make_pick(nc, 1, Chain(pool, pool_chain))

            states, c_copied = Lagged(pool, h_ready, 0, PAIRS, POOL_PAIRS), Lagged(pool, c_sb_ready, 0, PAIRS, POOL_PAIRS)

            def body(b, p, first=False, ahead=True, last=False):
                for n, m in enumerate(POOL_PAIRS):
                    if m == 6 and not last:
                        make_dx(1 - p)
                    c_copied.wait(m, first)
                    states.wait(m, first)
                    for c in range(DC):
                        ins = nc.gpsimd.tensor_tensor(hc[:, m % 4, :, c], h[:, m % 4, :, c],
                                                      c_sb[:, c_place(m)].rearrange("p (n t) -> p n t", n=2), ALU.mult)
                    ins.then_inc(hc_chain, 1)
                    pool.wait_ge(hc_chain, n + 1)
                    pool.sem_inc(hc_pool, 1)
                    pool.sem_inc(h_free, 1)
                    pool.sem_inc(c_sb_free, 1)
                    if m == NORM_AFTER and ahead:
                        norm()
                    if m == 4 and not last:
                        split_bc(1 - p)
                    if m == RES_AFTER and ahead:
                        residual(b + 2)
                states.end(first, last)
                c_copied.end(first, last)
                pool.sem_inc(hc_chain, -len(POOL_PAIRS))

            def epilogue():
                take(pool, upper["pool"], 2)
                c = Chain(pool, pool_chain)
                for raw, halves in ew.parts[1:]:
                    c.link(nc.gpsimd.tensor_scalar(raw[:], raw[:], W_SCALE, 1.0, ALU.mult, ALU.mult))
                    nc.gpsimd.tensor_tensor(halves[1][:], raw[:], halves[0][:], ALU.subtract)
                c.end()

            batches(pool, body, prologue, epilogue)

        @block.tensor
        def _(pe):
            pe.wait_ge(loaded["mamba"], 16 * len(mw.NAMES))
            pe.sem_inc(t2_free, 1)
            inputs_made = Lagged(pe, b_free, 1, PAIRS)
            c_copied = Lagged(pe, c_free, 1, PAIRS, POOL_PAIRS)
            products = {"dve": Lagged(pe, hc_dve, LAG, PAIRS, DVE_PAIRS), "pool": Lagged(pe, hc_pool, LAG, PAIRS, POOL_PAIRS)}

            def transpose_z():
                take(pe, z_ready)
                for tt in range(TT):
                    ins = nc.tensor.transpose(t0[:, tt * P:(tt + 1) * P], z[:, tt], ident[:])
                ins.then_inc(zT_ready, 1)

            def project_in():
                take(pe, hT_ready)
                for c in range(DC):
                    ins = nc.tensor.matmul(t1[:, c * T:(c + 1) * T], in_w[:, c * P:(c + 1) * P], hT[:], start=True, stop=True)
                ins.then_inc(x1_ready, 1)
                for c in range(DC):
                    ins = nc.tensor.matmul(t0[:, c * T:(c + 1) * T], in_w[:, (DC + c) * P:(DC + c + 1) * P], hT[:], start=True, stop=True)
                ins.then_inc(g_ready, 1)

            def convolve():
                take(pe, xpad_ready)
                for c in range(DC):
                    for k in range(KC):
                        ins = nc.tensor.matmul(t1[:, c * T:(c + 1) * T], taps[:, c, k], xpad[:, c, k:k + T], start=(k == 0), stop=(k == KC - 1))
                ins.then_inc(conv_ready, 1)

            def project_dbc():
                take(pe, xs_ready)
                for c in range(DC):
                    ins = nc.tensor.matmul(t1[:, 0:T], dbc_w[:, c], xs[:, c], start=(c == 0), stop=(c == DC - 1))
                ins.then_inc(dbc_ready, 1)

            def project_delta():
                take(pe, bcd_ready)
                take(pe, t2_free)
                for c in range(DC):
                    ins = nc.tensor.matmul(t2[:, c * T:(c + 1) * T], dup_w[2 * DTR:3 * DTR + 1, c * P:(c + 1) * P],
                                           bcd[2 * DTR:3 * DTR + 1, :], start=True, stop=True)
                ins.then_inc(dup_ready, 1)

            def project_out():
                take(pe, t2_free)
                for tt in range(TT):
                    for c in range(DC):
                        ins = nc.tensor.matmul(t2[:, tt * DM:(tt + 1) * DM], yg[:, c, tt * P:(tt + 1) * P], out_w[:, c],
                                               start=(c == 0), stop=(c == DC - 1))
                ins.then_inc(o_ready, 1)

            def spread(m, p):
                for n in range(2):
                    ins = nc.tensor.matmul(c_ps[m % 2][:, n * T:(n + 1) * T], pick[:, NS + 2 * m + n], bc[:, p], start=True, stop=True)
                if m in POOL_PAIRS:
                    ins.then_inc(c_ready, 1)
                for n in range(2):
                    ins = nc.tensor.matmul(b_ps[m % 2][:, n * T:(n + 1) * T], pick[:, 2 * m + n], bc[:, p], start=True, stop=True)
                ins.then_inc(b_ready, 1)

            def wait_banks(m, first):
                inputs_made.wait(m, first)
                c_copied.wait(m, first)
                products["dve"].wait(m, first)

            def wait_products(m, first=False):
                products["dve"].wait(m, first)
                products["pool"].wait(m, first)

            def add_states(m):
                for n in range(2):
                    ins = nc.tensor.matmul(y_ps[:], ident[:], hc[:, m % 4, n].rearrange("p c t -> p (c t)"),
                                           start=(m == 0 and n == 0), stop=(m == PAIRS - 1 and n == 1))
                if m == PAIRS - 1:
                    ins.then_inc(y_ready, 1)

            def prologue():
                transpose_z()
                project_in()
                pe.sem_inc(z_read, 1)
                take(pe, zeros_made["pe"])
                take(pe, taps_made)
                convolve()
                project_dbc()
                transpose_z()
                project_delta()
                project_in()
                take(pe, pick_made)
                take(pe, bc_ready)
                spread(0, 0)

            def body(b, p, first=False, ahead=True, last=False):
                for m in range(PAIRS):
                    if m < PAIRS - 1 or not last:
                        wait_banks(m - 1, first)
                    if m == PAIRS - 1 and not last:
                        take(pe, bc_ready)
                        spread(0, 1 - p)
                    elif m < PAIRS - 1:
                        spread(m + 1, p)
                    if m == 2 and not last:
                        convolve()
                    if m == LAG and not first:
                        take(pe, yg_ready)
                        if not last:
                            pe.sem_inc(gate_free, 1)
                    if m >= LAG or not first:
                        wait_products(m - LAG, first)
                        add_states((m - LAG) % PAIRS)
                    if m == LAG and not first:
                        project_out()
                    if m == 2 and not last:
                        project_dbc()
                    if m == 4 and not last:
                        project_delta()
                    if m == 7 and ahead:
                        transpose_z()
                    if m == 7 and ahead:
                        project_in()
                inputs_made.end(first, last)
                c_copied.end(first, last)
                products["dve"].end(first, last)
                products["pool"].end(first, last)

            def epilogue():
                for m in range(PAIRS - LAG, PAIRS):
                    wait_products(m)
                    add_states(m)
                take(pe, yg_ready)
                project_out()

            batches(pe, body, prologue, epilogue)

        @block.scalar
        def _(act):
            act.wait_ge(loaded["mamba"], 16 * len(mw.NAMES))
            take(act, zeros_made["act"])
            chain = Chain(act, act_chain)
            nc.scalar.preload_act_table_set("natural_log_exp_and_others")
            chain.link(nc.scalar.activation(neg_a[:], neg_a[:], ACT.Exp))
            chain.link(nc.scalar.activation(neg_a[:], neg_a[:], ACT.Copy, scale=-1.0))
            chain.end()

            def scale_hT():
                take(act, zT_ready)
                nc.scalar.activation(hT[:], t0[:, 0:T], ACT.Copy, scale=rms_w[:, 0:1]).then_inc(hT_ready, 1)

            def pad_x():
                take(act, x1_ready)
                for c in range(DC):
                    ins = nc.scalar.activation(xpad[:, c, KC - 1:], t1[:, c * T:(c + 1) * T], ACT.Identity, bias=in_b[:, c:c + 1])
                ins.then_inc(xpad_ready, 1)

            def silus(p, first=False):
                take(act, g_ready)
                if not first:
                    take(act, gate_free)
                for c in range(DC):
                    nc.scalar.activation(gate[:, p, c], t0[:, c * T:(c + 1) * T], ACT.Silu, bias=in_b[:, DC + c:DC + c + 1])
                take(act, conv_ready)
                for c in range(DC):
                    ins = nc.scalar.activation(xs[:, c], t1[:, c * T:(c + 1) * T], ACT.Silu, bias=conv_b[:, c:c + 1])
                ins.then_inc(xs_ready, 1)
                nc.scalar.preload_act_table_set("natural_log_exp_and_others")

            def read_dbc(p):
                take(act, dbc_ready)
                nc.scalar.activation(bcd[:], t1[:, 0:T], ACT.Identity, bias=dbc_b[:, 0:1]).then_inc(bcd_ready, 1)
                nc.scalar.activation(bc[0:2 * NS, p], t1[0:2 * NS, 0:T], ACT.Identity, bias=dbc_b[0:2 * NS, 0:1])
                nc.scalar.activation(bc_hi[64:96], t1[64:96, 0:T], ACT.Identity, bias=dbc_b[64:96, 0:1]).then_inc(bc_hi_ready, 1)

            def softplus():
                c = Chain(act, act_chain)
                take(act, dup_ready)
                flat = sp[:].rearrange("p c t -> p (c t)")
                c.link(nc.scalar.activation(flat, t2[:], ACT.Abs))
                c.link(nc.scalar.activation(flat, flat, ACT.Exp, scale=-1.0))
                nc.scalar.activation(flat, flat, ACT.Ln, bias=1.0).then_inc(sp_ready, 1)
                c.end()

            scanned = Lagged(act, decay_free, 3, PAIRS)
            spreads = Lagged(act, c_ready, 0, PAIRS, POOL_PAIRS)
            c_sb_read = Lagged(act, c_sb_free, PAIRS - 1 - POOL_PAIRS[-3], PAIRS, POOL_PAIRS)

            def decays(m, p):
                for n in range(2):
                    for c in range(DC):
                        ins = nc.scalar.activation(decay[:, m % 4, n, c, 1:T], delta[:, p, c, 1:T], ACT.Exp,
                                                   scale=neg_a[:, c, 2 * m + n:2 * m + n + 1])
                ins.then_inc(decay_ready, 1)

            def copy_c(m, n):
                nc.scalar.activation(c_sb[:, c_place(m)], c_ps[m % 2][:], ACT.Copy).then_inc(c_chain, 1)
                act.wait_ge(c_chain, n)
                act.sem_inc(c_sb_ready, 1)
                act.sem_inc(c_free, 1)

            def prologue():
                scale_hT()
                pad_x()
                silus(0, first=True)
                read_dbc(0)
                scale_hT()
                softplus()
                take(act, delta_ready)
                decays(0, 0)

            def body(b, p, first=False, ahead=True, last=False):
                for m in range(PAIRS):
                    if m < PAIRS - 1 or not last:
                        scanned.wait(m - 3, first)
                    if m == PAIRS - 1 and not last:
                        take(act, delta_ready)
                        decays(0, 1 - p)
                    elif m < PAIRS - 1:
                        decays(m + 1, p)
                    if m + 1 in POOL_PAIRS:
                        n = POOL_PAIRS.index(m + 1)
                        spreads.wait(m + 1, first)
                        c_sb_read.wait(POOL_PAIRS[n - 2] - (PAIRS if n < 2 else 0), first)
                        copy_c(m + 1, n + 1)
                    if not last:
                        if m == 0:
                            pad_x()
                        if m == 2:
                            silus(1 - p, first)
                        if m == 3:
                            read_dbc(1 - p)
                        if m == 4:
                            softplus()
                    if m == 7 and ahead:
                        scale_hT()
                scanned.end(first, last)
                spreads.end(first, last)
                c_sb_read.end(first, last)
                act.sem_inc(c_chain, -len(POOL_PAIRS))

            def epilogue():
                take(act, raw_ready)
                for n, (raw, halves) in enumerate(ew.parts):
                    nc.scalar.activation(halves[0][:], raw[:], ACT.Copy, scale=W_SCALE).then_inc(upper["dve"] if n == 0 else upper["pool"], 1)

            batches(act, body, prologue, epilogue)

        @block.vector
        def _(dve):
            def statistics(b):
                c = Chain(dve, dve_chain)
                for tt in range(TT):
                    ins = nc.vector.bn_stats(stats[:, tt], tile(b, tt))
                c.link(ins)
                for tt in range(TT):
                    ins = nc.vector.bn_aggr(mv[:, tt], stats[:, tt])
                ins.then_inc(stats_ready, 1)
                c.end()

            def normalise(b):
                take(dve, norm_ready)
                for tt in range(TT):
                    ins = nc.vector.tensor_scalar(z[:, tt], x_sb[:, bass.ds(b * TT + tt, 1), :].rearrange("p o d -> p (o d)"), mv[:, tt, 0:1], nrm[:, 3, tt:tt + 1], ALU.subtract, ALU.mult)
                ins.then_inc(z_ready, 1)
                for tt in range(TT):
                    ins = nc.vector.tensor_scalar(xn[:, tt], x_sb[:, bass.ds(b * TT + tt, 1), :].rearrange("p o d -> p (o d)"), mv[:, tt, 0:1], nrm[:, 0, tt:tt + 1], ALU.subtract, ALU.mult)
                ins.then_inc(xn_ready, 1)

            def make_delta(p):
                c = Chain(dve, dve_chain)
                take(dve, sp_ready)
                c.link(nc.vector.scalar_tensor_tensor(delta[:, p].rearrange("p c t -> p (c t)"), t2[:], 0.0, sp[:].rearrange("p c t -> p (c t)"), ALU.max, ALU.add))
                dve.sem_inc(t2_free, 1)
                dve.sem_inc(delta_ready, 1)
                dve.sem_inc(delta_made, 1)
                c.end()

            def gate_y(p):
                take(dve, y_ready)
                nc.vector.tensor_tensor(yg[:].rearrange("p c t -> p (c t)"), y_ps[:], gate[:, p].rearrange("p c t -> p (c t)"), ALU.mult).then_inc(yg_ready, 1)

            def update(b):
                take(dve, o_ready)
                take(dve, res_ready)
                own = x_sb[:, bass.ds(b * TT, TT), :]
                nc.vector.tensor_tensor(own, t2[:, 0:TT * DM].rearrange("p (a d) -> p a d", a=TT), own, ALU.add).then_inc(t2_free, 1)

            def inputs(m, p):
                out = h[:, m % 4]
                b4 = b_ps[m % 2][:].rearrange("p (n c t) -> p n c t", n=2, c=1).to_broadcast([P, 2, DC, T])
                d4 = dx[:, p].rearrange("p (n c) t -> p n c t", n=1).to_broadcast([P, 2, DC, T])
                nc.vector.tensor_tensor(out, b4, d4, ALU.mult).then_inc(core_chain, 1)

            states_read = Lagged(dve, h_free, 3, PAIRS, POOL_PAIRS)

            def flat(ap):
                return ap.rearrange("p n c t -> p (n c t)")

            def prologue():
                nc.vector.memset(ew.pick[:], 0.0)
                nc.vector.memset(pick[:], 0.0).then_inc(pick_zeroed, 1)
                dve.wait_ge(loaded["x_head"], 16)
                statistics(0)
                normalise(0)
                statistics(1)
                dve.wait_ge(loaded["mamba"], 16 * len(mw.NAMES))
                for c in range(DC):
                    for k in range(KC):
                        ins = nc.vector.tensor_scalar(taps[:, c, k], ident[:], conv_w[:, c, k:k + 1], None, ALU.mult)
                ins.then_inc(taps_made, 1)
                take(dve, z_read)
                normalise(1)
                make_delta(0)
                take(dve, dx_ready)
                dve.wait_ge(loaded["x_rest"], 16)
                take(dve, b_ready)
                inputs(0, 0)

            def body(b, p, first=False, ahead=True, last=False):
                done = 1
                for m in range(PAIRS):
                    if m == LAG and not first:
                        gate_y(1 - p)
                    if m == 3 and ahead:
                        statistics(b + 2)
                    if m == 5 and ahead:
                        normalise(b + 2)
                    if m == 6 and not last:
                        make_delta(1 - p)
                    if m == 4 and not first:
                        update(b - 1)
                    dve.wait_ge(core_chain, done)
                    dve.sem_inc(b_free, 1)
                    dve.wait_ge(decay_ready, m + 1)
                    nc.vector.tensor_tensor_scan(flat(h[:, m % 4]), flat(decay[:, m % 4]), flat(h[:, m % 4]), 0.0, ALU.mult, ALU.add).then_inc(core_chain, 1)
                    done += 1
                    scanned = done
                    if m < PAIRS - 1 or not last:
                        dve.wait_ge(b_ready, m + 1)
                        states_read.wait(m - 3, first)
                        if m == PAIRS - 1:
                            take(dve, dx_ready)
                        inputs((m + 1) % PAIRS, p if m < PAIRS - 1 else 1 - p)
                        done += 1
                    dve.wait_ge(core_chain, scanned)
                    dve.sem_inc(decay_free, 1)
                    if m in POOL_PAIRS:
                        dve.sem_inc(h_ready, 1)
                    else:
                        c4 = c_ps[m % 2][:].rearrange("p (n c t) -> p n c t", n=2, c=1).to_broadcast([P, 2, DC, T])
                        nc.vector.tensor_tensor(hc[:, m % 4], h[:, m % 4], c4, ALU.mult).then_inc(hc_dve, 1)
                states_read.end(first, last)
                dve.sem_inc(decay_ready, -PAIRS)
                if not last:
                    dve.sem_inc(b_ready, -PAIRS)
                    dve.sem_inc(core_chain, 1 - done)

            def epilogue():
                gate_y((NB - 1) % 2)
                take(dve, upper["dve"])
                raw, halves = ew.parts[0]
                nc.vector.scalar_tensor_tensor(halves[1][:], raw[:], W_SCALE, halves[0][:], ALU.mult, ALU.subtract)
                update(NB - 1)

            batches(dve, body, prologue, epilogue)


class MambaWeights:

    NAMES = ("in_w", "in_b", "rms_w", "conv_w", "conv_b", "a_log", "dbc_w", "dbc_b", "dup_w", "out_w", "out_b")

    def __init__(self, nc, ctx):
        shapes = {"in_w": [P, 2 * DI], "in_b": [P, 2 * DC], "rms_w": [P, 1], "conv_w": [P, DC, KC], "conv_b": [P, DC],
                  "a_log": [P, DC, NS], "dbc_w": [P, DC, P], "dbc_b": [P, 1],
                  "dup_w": [3 * DTR + 1, DI],
                  "out_w": [P, DC, DM], "out_b": [P, DM]}
        self.sb = {n: ctx.enter_context(nc.sbuf_tensor("mw_" + n, shapes[n], FP32)) for n in self.NAMES}

    def loads(self, w):
        return [(self.sb[n][2 * DTR:3 * DTR + 1, :] if n == "dup_w" else self.sb[n][:], w[n]) for n in self.NAMES]


class AttentionWeights:

    NAMES = ("qkvg_w", "qkvg_b", "attn_out_w", "attn_out_b")

    def __init__(self, nc, ctx):
        self.sb = {n: ctx.enter_context(nc.sbuf_tensor("aw_" + n, [P, 4 * NH * DH if n[0] == "q" else DM], FP32)) for n in self.NAMES}

    def loads(self, w):
        return [(self.sb[n][:], w[n]) for n in self.NAMES]


class ExpertWeights:

    def __init__(self, nc, ctx):
        def sb(name, shape, dt=FP16):
            return ctx.enter_context(nc.sbuf_tensor("ew_" + name, shape, dt))

        self.gate_up = [sb(f"gate_up{i}", [P, NE + 1, 2, P]) for i in range(2)]
        self.down = [sb(f"down{i}", [P, NE + 1, DM]) for i in range(2)]
        self.router = [sb(f"router{i}", [P, NE]) for i in range(2)]
        self.bias = sb("bias", [P, NE], FP32)
        self.pick = sb("pick", [4 * NE, NE, P])
        self.raw = [sb("gate_up", [P, NE + 1, 2, P], FP32), sb("down", [P, NE + 1, DM], FP32), sb("router", [P, NE], FP32)]
        self.parts = list(zip(self.raw, (self.gate_up, self.down, self.router)))

    NAMES = ("gate_up", "down", "router", "expert_bias")

    def loads(self, w):
        return [(t[:], w[n]) for t, n in zip(self.raw + [self.bias], self.NAMES)]

    def make_pick(self, nc, part, chain):
        chain.link(nc.gpsimd.affine_select(out=self.pick[:], in_=self.pick[:], compare_op=ALU.not_equal, fill=1.0,
                                           base=-2 * NE * part, pattern=[[-1, NE], [0, P]], channel_multiplier=1))
        chain.end()


def expert_layer(nc, sems, layer, x_sb, ew, ident, half, out=None):
    ctx = ExitStack()
    with ctx:
        tag = f"e{layer}_"

        def sb(name, shape, dt=FP32):
            return ctx.enter_context(nc.sbuf_tensor(tag + name, shape, dt))

        def pb(name):
            return ctx.enter_context(nc.psum_tensor(tag + name, [P, 512], FP32))

        def sem(name):
            return sems.enter_context(nc.semaphore(tag + name))

        NTQ = QC // P
        STEPS = NE + 1
        RING = 4

        stats = sb("stats", [P, NTQ, 6])
        mv = sb("mv", [P, NTQ, 2])
        nrm = sb("nrm", [P, 2, NTQ])
        xn = sb("xn", [P, NTQ, DM])
        x_hi, x_lo = sb("x_hi", [P, 2, QC], FP16), sb("x_lo", [P, 2, QC], FP16)
        th = sb("th", [P, NTQ, NE])
        score = sb("score", [P, NTQ, NE])
        sel = sb("sel", [P, NTQ, NE])
        top = sb("top", [P, NTQ, TOPK])
        left = sb("left", [P, NTQ, NE])
        chosen = sb("chosen", [P, NTQ, NE])
        total = sb("total", [P, 2, NTQ])
        comb = sb("comb", [P, NTQ, 4 * NE])
        c_hi = sb("c_hi", [4 * NE, QC], FP16)
        cT = sb("cT", [4 * NE, 2, QC], FP16)
        s = sb("s", [P, 2, QC])
        su = sb("su", [P, 2, QC])
        h = sb("h", [P, RING + 1, QC])
        h_hi, h_lo = sb("h_hi", [P, RING + 1, QC], FP16), sb("h_lo", [P, RING + 1, QC], FP16)
        yT = sb("yT", [P, QC])

        g_ps, u_ps, c_ps = [pb("g0"), pb("g1")], [pb("u0"), pb("u1")], [pb("c0"), pb("c1")]
        y_ps, t_ps = pb("y"), pb("t")

        comb_zeroed = sem("comb_zeroed")
        pool_chain, dve_chain, core_chain = sem("pool_chain"), sem("dve_chain"), sem("core_chain")
        stats_ready, norm_ready, xn_ready, xT_ready = (sem(n) for n in ("stats_ready", "norm_ready", "xn_ready", "xT_ready"))
        x_hi_ready, x_ready, gates_ready, th_ready = (sem(n) for n in ("x_hi_ready", "x_ready", "gates_ready", "th_ready"))
        comb_ready, combT_ready, c_hi_ready, cT_ready = (sem(n) for n in ("comb_ready", "combT_ready", "c_hi_ready", "cT_ready"))
        g_ready, u_ready, s_ready, h_ready, h_hi_ready, h_lo_ready = (sem(n) for n in ("g_ready", "u_ready", "s_ready", "h_ready", "h_hi_ready", "h_lo_ready"))
        gu_free, c_free = sem("gu_free"), sem("c_free")
        y_ready, yT_ready, o_ready = sem("y_ready"), sem("yT_ready"), sem("o_ready")
        final_ready, stored = sem("final_ready"), sem("stored")

        def place(e):
            return e % RING if e < NE else RING

        def chunks(eng, body, prologue, epilogue):
            prologue()
            body(0, 0, first=True)
            with eng.Fori(0, NQ // 2 - 1) as i:
                body(i * 2 + 1, 1)
                body(i * 2 + 2, 0)
            body(NQ - 1, (NQ - 1) % 2, last=True)
            epilogue()

        def tile(q, tt):
            return x_sb[:, bass.ds(q * NTQ + tt, 1), :].rearrange("p o d -> p (o d)")

        block = ctx.enter_context(nc.Block())

        if out is not None:
            @block.sync
            def _(sp):
                with sp.Fori(0, NQ) as q:
                    take(sp, final_ready)
                    sp.dma_start(out[:, bass.ds(q * NTQ, NTQ), :], x_sb[:, bass.ds(q * NTQ, NTQ), :]).then_inc(stored, 16)
                sp.wait_ge(stored, 16 * NQ)

        @block.gpsimd
        def _(pool):
            nc.gpsimd.memset(comb[:], 0.0).then_inc(comb_zeroed, 1)

            def norm():
                c = Chain(pool, pool_chain)
                take(pool, stats_ready)
                c.link(nc.gpsimd.tensor_scalar(nrm[:, 1], mv[:, :, 1], LN_EPS, 1.0, ALU.add, ALU.mult))
                nc.gpsimd.tensor_tensor(nrm[:, 0], nrm[:, 1], half[:, 0:NTQ], ALU.pow).then_inc(norm_ready, 1)
                c.end()

            def lower(e):
                pool.wait_ge(h_hi_ready, e + 1)
                k = place(e)
                nc.gpsimd.tensor_tensor(h_lo[:, k], h[:, k], h_hi[:, k], ALU.subtract).then_inc(h_lo_ready, 1)

            def body(q, p, first=False, last=False):
                for e in range(STEPS):
                    if e == 2 and not last:
                        norm()
                    lower(e)
                pool.sem_inc(h_hi_ready, -STEPS)

            chunks(pool, body, norm, lambda: None)

        @block.tensor
        def _(pe):
            def transpose_x():
                take(pe, xn_ready)
                for tt in range(NTQ):
                    ins = nc.tensor.transpose(t_ps[:, tt * P:(tt + 1) * P], xn[:, tt], ident[:])
                ins.then_inc(xT_ready, 1)

            def route(p):
                take(pe, x_ready)
                for tt in range(NTQ):
                    own = slice(tt * P, (tt + 1) * P)
                    for n, (a, r) in enumerate(((x_hi, 0), (x_hi, 1), (x_lo, 0))):
                        ins = nc.tensor.matmul(t_ps[:, tt * NE:(tt + 1) * NE], a[:, p, own], ew.router[r][:], start=(n == 0), stop=(n == 2))
                ins.then_inc(gates_ready, 1)

            def transpose_comb():
                take(pe, comb_ready)
                for tt in range(NTQ):
                    ins = nc.tensor.transpose(t_ps[0:4 * NE, tt * P:(tt + 1) * P], comb[:, tt], ident[:])
                ins.then_inc(combT_ready, 1)

            def up(e, p, first):
                bank = (e + p) % 2
                if not first or e >= 2:
                    pe.wait_ge(gu_free, e - 1 if first else e + 1)
                for side, ps, ready in ((0, g_ps, g_ready), (1, u_ps, None)):
                    for n, (r, a) in enumerate(((0, x_hi), (0, x_lo), (1, x_hi))):
                        ins = nc.tensor.matmul(ps[bank][:], ew.gate_up[r][:, e, side], a[:, p], start=(n == 0), stop=(n == 2))
                    if ready:
                        ins.then_inc(ready, 1)
                if first and e == 0:
                    transpose_comb()
                    take(pe, cT_ready)
                if not first or e >= 2:
                    pe.wait_ge(c_free, e - 1 if first else e + 1)
                if e < NE:
                    ins = nc.tensor.matmul(c_ps[bank][:], ew.pick[:, e], cT[:, p], start=True, stop=True)
                ins.then_inc(u_ready, 1)

            def down(e):
                for n, (r, a) in enumerate(((0, h_hi), (0, h_lo), (1, h_hi))):
                    ins = nc.tensor.matmul(y_ps[:], ew.down[r][:, e], a[:, place(e)], start=(e == 0 and n == 0), stop=(e == NE and n == 2))
                if e == NE:
                    ins.then_inc(y_ready, 1)

            def transpose_y():
                for tt in range(NTQ):
                    ins = nc.tensor.transpose(t_ps[:, tt * P:(tt + 1) * P], yT[:, tt * P:(tt + 1) * P], ident[:])
                ins.then_inc(o_ready, 1)

            def prologue():
                transpose_x()
                route(0)

            def body(q, p, first=False, last=False):
                for e in range(STEPS):
                    up(e, p, first)
                    if e == 3 and not first:
                        take(pe, yT_ready)
                        transpose_y()
                    if e >= 3 or not first:
                        pe.wait_ge(h_lo_ready, e - 2 if first else e + 1)
                        down((e - 3) % STEPS)
                    if not last:
                        if e == 6:
                            transpose_x()
                        if e == 7:
                            route(1 - p)
                        if e == 13:
                            transpose_comb()
                        if e == 16:
                            take(pe, cT_ready)
                if not last:
                    pe.sem_inc(gu_free, -(STEPS - 2 if first else STEPS))
                    pe.sem_inc(c_free, -(STEPS - 2 if first else STEPS))
                    pe.sem_inc(h_lo_ready, -(STEPS - 3 if first else STEPS))

            def epilogue():
                for n in range(3):
                    pe.wait_ge(h_lo_ready, STEPS + n + 1)
                    down(STEPS - 3 + n)
                take(pe, yT_ready)
                transpose_y()

            chunks(pe, body, prologue, epilogue)

        @block.scalar
        def _(act):
            nc.scalar.preload_act_table(ACT.Silu)

            def upper_x(p):
                take(act, xT_ready)
                nc.scalar.activation(x_hi[:, p], t_ps[:], ACT.Copy).then_inc(x_hi_ready, 1)

            def squash():
                take(act, gates_ready)
                nc.scalar.activation(th[:].rearrange("p a e -> p (a e)"), t_ps[:, 0:NTQ * NE], ACT.Tanh, scale=0.5 / W_SCALE).then_inc(th_ready, 1)

            def upper_c(p):
                take(act, combT_ready)
                nc.scalar.activation(cT[0:2 * NE, p], t_ps[0:2 * NE, :], ACT.Copy)
                nc.scalar.activation(c_hi[2 * NE:4 * NE], t_ps[2 * NE:4 * NE, :], ACT.Copy).then_inc(c_hi_ready, 1)

            def silu(e, p):
                act.wait_ge(g_ready, e + 1)
                nc.scalar.activation(s[:, (e + p) % 2], g_ps[(e + p) % 2][:], ACT.Silu, scale=1 / W_SCALE).then_inc(s_ready, 1)

            def upper_h(e, n):
                act.wait_ge(h_ready, n)
                act.sem_inc(c_free, 1)
                nc.scalar.activation(h_hi[:, place(e)], h[:, place(e)], ACT.Copy).then_inc(h_hi_ready, 1)

            def read_y():
                take(act, y_ready)
                nc.scalar.activation(yT[:], y_ps[:], ACT.Copy, scale=W_SCALE ** -2).then_inc(yT_ready, 1)

            def prologue():
                upper_x(0)
                squash()
                upper_c(0)

            def body(q, p, first=False, last=False):
                for e in range(STEPS):
                    silu(e, p)
                    if e > 0:
                        upper_h(e - 1, e if first else e + 1)
                    elif not first:
                        upper_h(NE, 1)
                    if e == 2 and not first:
                        read_y()
                    if not last:
                        if e == 6:
                            upper_x(1 - p)
                        if e == 6:
                            squash()
                        if e == 13:
                            upper_c(1 - p)
                act.sem_inc(g_ready, -STEPS)
                if not last:
                    act.sem_inc(h_ready, -(STEPS - 1 if first else STEPS))

            def epilogue():
                upper_h(NE, STEPS + 1)
                read_y()

            chunks(act, body, prologue, epilogue)

        @block.vector
        def _(dve):
            take(dve, comb_zeroed)

            def statistics(q):
                c = Chain(dve, dve_chain)
                for tt in range(NTQ):
                    ins = nc.vector.bn_stats(stats[:, tt], tile(q, tt))
                c.link(ins)
                for tt in range(NTQ):
                    ins = nc.vector.bn_aggr(mv[:, tt], stats[:, tt])
                ins.then_inc(stats_ready, 1)
                c.end()

            def normalise(q):
                take(dve, norm_ready)
                for tt in range(NTQ):
                    ins = nc.vector.tensor_scalar(xn[:, tt], tile(q, tt), mv[:, tt, 0:1], nrm[:, 0, tt:tt + 1], ALU.subtract, ALU.mult)
                ins.then_inc(xn_ready, 1)

            def lower_x(p):
                take(dve, x_hi_ready)
                nc.vector.tensor_tensor(x_lo[:, p], t_ps[:], x_hi[:, p], ALU.subtract).then_inc(x_ready, 1)

            def choose(part):
                c = Chain(dve, dve_chain)
                if part == 0:
                    take(dve, th_ready)
                    c.link(nc.vector.tensor_scalar(score[:], th[:], 1.0, 0.5, ALU.add, ALU.mult))
                    c.link(nc.vector.tensor_tensor(sel[:], score[:], ew.bias[:].rearrange("p (o e) -> p o e", o=1).to_broadcast([P, NTQ, NE]), ALU.add))
                    for tt in range(NTQ):
                        ins = nc.vector.max(top[:, tt], sel[:, tt])
                    c.link(ins)
                if part == 1:
                    for tt in range(NTQ):
                        ins = nc.vector.match_replace(left[:, tt], top[:, tt], sel[:, tt], TAKEN)
                    c.link(ins)
                    c.link(nc.vector.scalar_tensor_tensor(chosen[:], left[:], TAKEN, score[:], ALU.is_equal, ALU.mult))
                if part == 2:
                    c.link(nc.vector.tensor_reduce(total[:, 0], chosen[:], AX.X, ALU.add))
                    c.link(nc.vector.reciprocal(total[:, 1], total[:, 0]))
                    for k in range(2):
                        r = total[:, 1].rearrange("p (a o) -> p a o", o=1).to_broadcast([P, NTQ, NE])
                        ins = nc.vector.scalar_tensor_tensor(comb[:, :, 2 * k * NE:(2 * k + 1) * NE], chosen[:], ROUTE_SCALE, r, ALU.mult, ALU.mult)
                    ins.then_inc(comb_ready, 1)
                c.end()

            def lower_c(p):
                take(dve, c_hi_ready)
                rows = slice(2 * NE, 4 * NE)
                nc.vector.tensor_tensor(cT[rows, p], t_ps[rows, :], c_hi[rows], ALU.subtract).then_inc(cT_ready, 1)

            def hidden(e, p):
                bank = (e + p) % 2
                dve.wait_ge(s_ready, e + 1)
                dve.wait_ge(u_ready, e + 1)
                if e == NE:
                    nc.vector.tensor_tensor(h[:, place(e)], s[:, bank], u_ps[bank][:], ALU.mult).then_inc(core_chain, 1)
                    dve.wait_ge(core_chain, e + 1)
                    dve.sem_inc(gu_free, 1)
                    dve.sem_inc(h_ready, 1)
                    return
                nc.vector.tensor_tensor(su[:, bank], s[:, bank], u_ps[bank][:], ALU.mult).then_inc(core_chain, 1)
                dve.wait_ge(core_chain, e + 1)
                dve.sem_inc(gu_free, 1)
                nc.vector.tensor_tensor(h[:, place(e)], su[:, bank], c_ps[bank][:], ALU.mult).then_inc(h_ready, 1)

            def update(q):
                take(dve, o_ready)
                xs = x_sb[:, bass.ds(q * NTQ, NTQ), :]
                nc.vector.tensor_tensor(xs, t_ps[:].rearrange("p (a d) -> p a d", a=NTQ), xs, ALU.add).then_inc(final_ready, 1)

            def prologue():
                statistics(0)
                normalise(0)
                lower_x(0)
                for part in range(3):
                    choose(part)
                lower_c(0)

            def body(q, p, first=False, last=False):
                for e in range(STEPS):
                    hidden(e, p)
                    if e == 4 and not first:
                        update(q - 1)
                    if not last:
                        if e == 1:
                            statistics(q + 1)
                        if e == 4:
                            normalise(q + 1)
                        if e == 6:
                            lower_x(1 - p)
                        if e == 9:
                            choose(0)
                        if e == 10:
                            choose(1)
                        if e == 11:
                            choose(2)
                        if e == 14:
                            lower_c(1 - p)
                dve.sem_inc(s_ready, -STEPS)
                dve.sem_inc(u_ready, -STEPS)
                dve.sem_inc(core_chain, -STEPS)

            chunks(dve, body, prologue, lambda: update(NQ - 1))


def attention_layer(nc, sems, x_sb, aw, loaded, ident, ident16, half):
    ctx = ExitStack()
    with ctx:
        def sb(name, shape, dt=FP32):
            return ctx.enter_context(nc.sbuf_tensor("a_" + name, shape, dt))

        def pb(name, width=512):
            return ctx.enter_context(nc.psum_tensor("a_" + name, [P, width], FP32))

        def sem(name):
            return sems.enter_context(nc.semaphore("a_" + name))

        W = NH * DH
        WEIGH_AT = (13, 14, 15)
        SLOT = 32

        qkvg_w, qkvg_b, out_w, out_b = (aw.sb[n] for n in aw.NAMES)

        stats = sb("stats", [P, TT, 6])
        mv = sb("mv", [P, TT, 2])
        nrm = sb("nrm", [P, 4, TT])
        xn = sb("xn", [P, TT, DM])
        z = sb("z", [P, TT, DM])
        zT = sb("zT", [P, T])
        qkvg = sb("qkvg", [P, 2, TT, 4 * W])
        qk = sb("qk", [P, TT, 2, NH, SLOT], FP16)
        square = sb("square", [P, TT, 2 * W])
        norms = sb("norms", [P, 2, TT, 2 * NH])
        qkT = sb("qkT", [P, 2, 2, HG, T], FP16)
        v = sb("v", [P, 2, TT, NH, SLOT])
        gate = sb("gate", [P, 2, TT, W])
        d = sb("d", [P, 2, NH, TT * T])
        avT = sb("avT", [P, HG, T])
        den = sb("den", [P, 2, TT, NH])
        o = sb("o", [P, TT, W])
        oT = sb("oT", [P, T])

        near = sb("near", [P, 1])

        s_ps = [pb("s0"), pb("s1")]
        av_ps = [pb("av0"), pb("av1")]
        t_ps = [pb("t0"), pb("t1")]
        u_ps = pb("u", 1024)

        near_made = sem("near_made")
        w_ready = {e: sem("w_ready_" + e) for e in ("dve", "pool", "pe")}
        made = {e: sem("made_" + e) for e in ("dve", "pe")}
        pool_chain, dve_chain, act_chain, d_chain = sem("pool_chain"), sem("dve_chain"), sem("act_chain"), sem("d_chain")
        stats_ready, norm_ready, z_ready, zT_ps_ready, zT_ready = (sem(n) for n in ("stats_ready", "norm_ready", "z_ready", "zT_ps_ready", "zT_ready"))
        p_ready, qkvg_ready, hi_ready, sq_ready, v_ready, res_ready = (sem(n) for n in ("p_ready", "qkvg_ready", "hi_ready", "sq_ready", "v_ready", "res_ready"))
        xn_ready, gate_ready, gate_free = sem("xn_ready"), sem("gate_ready"), sem("gate_free")
        qk_ready, qkT_ps_ready, qkT_ready = sem("qk_ready"), sem("qkT_ps_ready"), sem("qkT_ready")
        s_ready, s_free, d_ready, w_done = sem("s_ready"), sem("s_free"), sem("d_ready"), sem("w_done")
        av_ready, avT_ready, u_ready, o_ready, oT_ps_ready, oT_ready, y_ready = (
            sem(n) for n in ("av_ready", "avT_ready", "u_ready", "o_ready", "oT_ps_ready", "oT_ready", "y_ready"))

        def batches(eng, body, prologue, epilogue):
            prologue()
            body(-1, 1, core=False, tail=False)
            body(0, 0, tail=False)
            with eng.Fori(0, NB // 2 - 2) as i:
                body(i * 2 + 1, 1)
                body(i * 2 + 2, 0)
            body(NB - 3, 1, further=False)
            body(NB - 2, 0, further=False, ahead=False)
            body(NB - 1, 1, further=False, ahead=False, heads=False)
            epilogue()

        def tile(b, tt):
            return x_sb[:, bass.ds(b * TT + tt, 1), :].rearrange("p o d -> p (o d)")

        def by_head(p, part):
            return qkvg[:, p, :, part * W:(part + 1) * W].rearrange("p a (h d) -> p a h d", d=DH)

        block = ctx.enter_context(nc.Block())

        @block.sync
        def _(sp):
            sp.wait_ge(loaded["attention"], 16 * len(aw.NAMES))
            for s in w_ready.values():
                sp.sem_inc(s, 1)

        @block.gpsimd
        def _(pool):
            chain = Chain(pool, pool_chain)
            nc.gpsimd.memset(qk[:], 0.0)
            chain.link(nc.gpsimd.memset(v[:], 0.0))
            nc.gpsimd.memset(qk[:, :, 0, :, 26:28], 1.0)
            nc.gpsimd.memset(qk[:, :, 1, :, 24:26], 1.0)
            chain.link(nc.gpsimd.memset(v[:, :, :, :, DH:DH + 1], 1.0))
            chain.end()
            for s in made.values():
                pool.sem_inc(s, 1)
            pool.wait_ge(w_ready["pool"], 1)

            def norm():
                c = Chain(pool, pool_chain)
                take(pool, stats_ready)
                c.link(nc.gpsimd.tensor_scalar(nrm[:, 1], mv[:, :, 1], LN_EPS, 1.0, ALU.add, ALU.mult))
                c.link(nc.gpsimd.tensor_tensor(nrm[:, 0], nrm[:, 1], half[:, 0:TT], ALU.pow))
                c.link(nc.gpsimd.tensor_tensor(nrm[:, 1], nrm[:, 0], nrm[:, 0], ALU.mult))
                c.link(nc.gpsimd.tensor_tensor(nrm[:, 1], nrm[:, 1], mv[:, :, 1], ALU.mult))
                c.link(nc.gpsimd.tensor_scalar(nrm[:, 1], nrm[:, 1], LN_EPS, 1.0, ALU.add, ALU.mult))
                c.link(nc.gpsimd.tensor_tensor(nrm[:, 2], nrm[:, 1], half[:, 0:TT], ALU.pow))
                nc.gpsimd.tensor_tensor(nrm[:, 3], nrm[:, 2], nrm[:, 0], ALU.mult).then_inc(norm_ready, 1)
                c.end()

            def residual(b):
                c = Chain(pool, pool_chain)
                take(pool, xn_ready)
                own = x_sb[:, bass.ds(b * TT, TT), :]
                c.link(nc.gpsimd.tensor_tensor(own, own, xn[:], ALU.add))
                nc.gpsimd.tensor_tensor(own, own, out_b[:].rearrange("p (o d) -> p o d", o=1).to_broadcast([P, TT, DM]), ALU.add).then_inc(res_ready, 1)
                c.end()

            def pack(p):
                take(pool, qkvg_ready)
                for side in range(2):
                    ins = nc.gpsimd.tensor_scalar(qk[:, :, side, :, 0:DH], by_head(p, side), 1.0, 1.0, ALU.mult, ALU.mult)
                ins.then_inc(hi_ready, 1)
                qk_cols = qkvg[:, p, :, 0:2 * W]
                nc.gpsimd.tensor_tensor(square[:], qk_cols, qk_cols, ALU.mult).then_inc(sq_ready, 1)
                for side, at in ((0, 2 * DH), (1, DH)):
                    ins = nc.gpsimd.tensor_scalar(qk[:, :, side, :, at:at + DH], by_head(p, side), 1.0, 1.0, ALU.mult, ALU.mult)
                ins.then_inc(hi_ready, 1)

            def keep(p):
                nc.gpsimd.tensor_scalar(v[:, p, :, :, 0:DH], by_head(p, 2), 1.0, 1.0, ALU.mult, ALU.mult).then_inc(v_ready, 1)
                nc.gpsimd.tensor_scalar(gate[:, p], qkvg[:, p, :, 3 * W:4 * W], 1.0, 1.0, ALU.mult, ALU.mult).then_inc(gate_ready, 1)

            def prologue():
                norm()
                residual(0)
                pack(0)
                norm()

            def body(b, p, core=True, tail=True, heads=True, ahead=True, further=True):
                if ahead:
                    residual(b + 2)
                if tail:
                    take(pool, gate_free)
                if heads:
                    keep(1 - p)
                if ahead:
                    pack(p)
                if further:
                    norm()

            batches(pool, body, prologue, lambda: None)

        @block.tensor
        def _(pe):
            pe.wait_ge(w_ready["pe"], 1)
            pe.wait_ge(made["pe"], 1)
            scores_read, weights = Lagged(pe, s_free, 2, NH), Lagged(pe, w_done, 1, HG)

            def transpose_z():
                take(pe, z_ready)
                for tt in range(TT):
                    ins = nc.tensor.transpose(t_ps[0][:, tt * P:(tt + 1) * P], z[:, tt], ident[:])
                ins.then_inc(zT_ps_ready, 1)

            def project():
                take(pe, zT_ready)
                for tt in range(TT):
                    nc.tensor.matmul(t_ps[tt][:], zT[:, tt * P:(tt + 1) * P], qkvg_w[:], start=True, stop=True).then_inc(p_ready, 1)

            def transpose_qk():
                take(pe, qk_ready)
                for tt in range(TT):
                    t16 = t_ps[tt][:].bitcast(FP16)
                    for side in range(2):
                        for g in range(HG):
                            k = side * HG + g
                            ins = nc.tensor.transpose(t16[:, k * P:(k + 1) * P], qk[:, tt, side, 4 * g:4 * g + 4].rearrange("p h k -> p (h k)"), ident16[:])
                    ins.then_inc(qkT_ps_ready, 1)

            def score(h, p, first):
                g, j = divmod(h, 4)
                rows = slice(SLOT * j, SLOT * (j + 1))
                scores_read.wait(h - 2, first)
                for kc in range(TT):
                    ins = nc.tensor.matmul(s_ps[h % 2][:, kc * T:(kc + 1) * T], qkT[rows, p, 1, g, kc * P:(kc + 1) * P], qkT[rows, p, 0, g, :], start=True, stop=True)
                ins.then_inc(s_ready, 1)

            def weigh(g, p):
                for kc in range(TT):
                    for j in range(4):
                        h = 4 * g + j
                        ins = nc.tensor.matmul(av_ps[g // 2][SLOT * j:SLOT * (j + 1), (g % 2) * T:(g % 2 + 1) * T],
                                               v[:, p, kc, h], d[:, p, h, kc * T:(kc + 1) * T], start=(kc == 0), stop=(kc == TT - 1))
                if g % 2:
                    ins.then_inc(av_ready, 1)

            def transpose_av():
                take(pe, avT_ready)
                for tt in range(TT):
                    for g in range(HG):
                        ins = nc.tensor.transpose(u_ps[:, tt * 512 + g * P:tt * 512 + (g + 1) * P], avT[:, g, tt * P:(tt + 1) * P], ident[:])
                ins.then_inc(u_ready, 1)

            def transpose_o():
                take(pe, o_ready)
                for tt in range(TT):
                    ins = nc.tensor.transpose(u_ps[:, tt * P:(tt + 1) * P], o[:, tt], ident[:])
                ins.then_inc(oT_ps_ready, 1)

            def project_out():
                take(pe, oT_ready)
                for tt in range(TT):
                    ins = nc.tensor.matmul(u_ps[:, 512 + tt * DM:512 + (tt + 1) * DM], oT[:, tt * P:(tt + 1) * P], out_w[:], start=True, stop=True)
                ins.then_inc(y_ready, 1)

            def prologue():
                transpose_z()
                project()
                transpose_qk()

            def body(b, p, core=True, tail=True, heads=True, ahead=True, further=True):
                for h in range(NH):
                    if heads:
                        if h == 0:
                            take(pe, qkT_ready, TT)
                        score(h, 1 - p, not core)
                    if h == 1 and tail:
                        weights.wait(-1)
                        weigh(HG - 1, 1 - p)
                    if h == 1 and ahead:
                        transpose_z()
                    if h == 4 and tail:
                        transpose_av()
                    if h == 8 and ahead:
                        project()
                    if h == 8 and tail:
                        transpose_o()
                    if h == 12 and tail:
                        project_out()
                    if h == WEIGH_AT[0] and core:
                        take(pe, v_ready)
                    if h == 15 and ahead:
                        transpose_qk()
                    for g, at in enumerate(WEIGH_AT):
                        if h == at and core:
                            weights.wait(g, not tail)
                            weigh(g, p)
                if heads:
                    scores_read.end(not core, False)
                if core:
                    weights.end(not tail, not heads)

            def epilogue():
                weights.wait(HG - 1)
                weigh(HG - 1, 1)
                transpose_av()
                transpose_o()
                project_out()

            batches(pe, body, prologue, epilogue)

        @block.scalar
        def _(act):
            def body(b, p, core=True, tail=True, heads=True, ahead=True, further=True):
                def heads_of(first, n):
                    return d[:, p, first:first + n].rearrange("p h k -> p (h k)")

                if not core:
                    return
                for first, n in ((0, 8), (8, 4), (12, 4)):
                    take(act, d_ready)
                    nc.scalar.activation(heads_of(first, n), heads_of(first, n), ACT.Sqrt).then_inc(act_chain, 1)
                nc.scalar.preload_act_table_set("natural_log_exp_and_others")
                for half in range(2):
                    act.wait_ge(act_chain, 1 + 2 * half)
                    nc.scalar.activation(heads_of(8 * half, 8), heads_of(8 * half, 8), ACT.Ln, bias=near[:, 0:1]).then_inc(act_chain, 1)
                for g in range(HG):
                    if g % 2 == 0:
                        act.wait_ge(act_chain, g // 2 + 4)
                    nc.scalar.activation(heads_of(4 * g, 4), heads_of(4 * g, 4), ACT.Exp, scale=-2.0).then_inc(w_done, 1)
                act.sem_inc(act_chain, -5)

            act.wait_ge(near_made, 1)
            batches(act, body, lambda: None, lambda: None)

        @block.vector
        def _(dve):
            nc.vector.memset(near[:], SHEP_EPS).then_inc(near_made, 1)
            dve.wait_ge(w_ready["dve"], 1)
            dve.wait_ge(made["dve"], 1)

            def statistics(b):
                c = Chain(dve, dve_chain)
                for tt in range(TT):
                    ins = nc.vector.bn_stats(stats[:, tt], tile(b, tt))
                c.link(ins)
                for tt in range(TT):
                    ins = nc.vector.bn_aggr(mv[:, tt], stats[:, tt])
                ins.then_inc(stats_ready, 1)
                c.end()

            def normalise(b):
                take(dve, norm_ready)
                for out, k, ready in ((z, 3, z_ready), (xn, 0, xn_ready)):
                    for tt in range(TT):
                        ins = nc.vector.tensor_scalar(out[:, tt], tile(b, tt), mv[:, tt, 0:1], nrm[:, k, tt:tt + 1], ALU.subtract, ALU.mult)
                    ins.then_inc(ready, 1)

            def read_zT():
                take(dve, zT_ps_ready)
                nc.vector.tensor_copy(zT[:], t_ps[0][:, 0:T]).then_inc(zT_ready, 1)

            def read_qkvg(p):
                for tt in range(TT):
                    dve.wait_ge(p_ready, tt + 1)
                    ins = nc.vector.tensor_tensor(qkvg[:, p, tt], t_ps[tt][:], qkvg_b[:], ALU.add)
                dve.sem_inc(p_ready, -TT)
                c = Chain(dve, dve_chain)
                c.link(ins)
                dve.sem_inc(qkvg_ready, 1)
                c.end()

            def split_qk(p):
                c = Chain(dve, dve_chain)
                take(dve, hi_ready, 2)
                for side, at in ((0, DH), (1, 2 * DH)):
                    nc.vector.tensor_tensor(qk[:, :, side, :, at:at + DH], by_head(p, side), qk[:, :, side, :, 0:DH], ALU.subtract)
                take(dve, sq_ready)
                c.link(nc.vector.tensor_reduce(norms[:, 0], square[:].rearrange("p a (h d) -> p a h d", d=DH), AX.X, ALU.add))
                c.link(nc.vector.tensor_scalar(norms[:, 1], norms[:, 0], -0.5, None, ALU.mult))
                for side, at in ((0, 24), (1, 26)):
                    ins = nc.vector.tensor_copy(qk[:, :, side, :, at], norms[:, 1, :, side * NH:(side + 1) * NH])
                c.link(ins)
                for side, at in ((0, 24), (1, 26)):
                    ins = nc.vector.tensor_tensor(qk[:, :, side, :, at + 1], norms[:, 1, :, side * NH:(side + 1) * NH], qk[:, :, side, :, at], ALU.subtract)
                ins.then_inc(qk_ready, 1)
                c.end()

            def read_qkT(p):
                for tt in range(TT):
                    dve.wait_ge(qkT_ps_ready, tt + 1)
                    nc.vector.tensor_copy(qkT[:, p, :, :, tt * P:(tt + 1) * P].rearrange("p s g t -> p (s g) t"),
                                          t_ps[tt][:].bitcast(FP16).rearrange("p (k t) -> p k t", t=P)).then_inc(qkT_ready, 1)
                dve.sem_inc(qkT_ps_ready, -TT)

            def distance(h, p):
                dve.wait_ge(s_ready, h + 1)
                ins = nc.vector.tensor_scalar(d[:, p, h], s_ps[h % 2][:], -2.0, 0.0, ALU.mult, ALU.max)
                if h in (7, 11, 15):
                    ins.then_inc(d_chain, 1)
                    take(dve, d_chain)
                    dve.sem_inc(s_free, 1)
                    dve.sem_inc(d_ready, 1)
                else:
                    ins.then_inc(s_free, 1)

            def read_av(k):
                take(dve, av_ready)
                ins = nc.vector.tensor_copy(avT[:, 2 * k:2 * k + 2].rearrange("p g t -> p (g t)"), av_ps[k][:])
                if k == 1:
                    ins.then_inc(avT_ready, 1)

            def norm_and_gate(p):
                c = Chain(dve, dve_chain)
                take(dve, u_ready)
                u = u_ps[:].rearrange("p (a h k) -> p a h k", a=TT, k=SLOT)
                oh = o[:].rearrange("p a (h d) -> p a h d", d=DH)
                c.link(nc.vector.tensor_scalar(den[:, 0], u[:, :, :, DH], SHEP_EPS, None, ALU.add))
                c.link(nc.vector.reciprocal(den[:, 1], den[:, 0]))
                c.link(nc.vector.tensor_tensor(oh, u[:, :, :, 0:DH], den[:, 1].rearrange("p a (h o) -> p a h o", o=1).to_broadcast([P, TT, NH, DH]), ALU.mult))
                c.link(nc.vector.tensor_tensor(o[:], o[:], gate[:, p], ALU.mult))
                dve.sem_inc(o_ready, 1)
                dve.sem_inc(gate_free, 1)
                c.end()

            def read_oT():
                take(dve, oT_ps_ready)
                nc.vector.tensor_copy(oT[:], u_ps[:, 0:T]).then_inc(oT_ready, 1)

            def update(b):
                take(dve, y_ready)
                take(dve, res_ready)
                own = x_sb[:, bass.ds(b * TT, TT), :]
                nc.vector.tensor_tensor(own, u_ps[:, 512:512 + TT * DM].rearrange("p (a d) -> p a d", a=TT), own, ALU.add)

            def prologue():
                statistics(0)
                normalise(0)
                statistics(1)
                read_zT()
                read_qkvg(0)
                split_qk(0)
                read_qkT(0)

            def body(b, p, core=True, tail=True, heads=True, ahead=True, further=True):
                for h in range(NH):
                    if heads:
                        distance(h, 1 - p)
                    if h == 0 and ahead:
                        normalise(b + 2)
                    if h == 2 and tail:
                        read_av(0)
                    if h == 2 and tail:
                        read_av(1)
                    if h == 4 and ahead:
                        read_zT()
                    if h == 6 and tail:
                        norm_and_gate(1 - p)
                    if h == 7 and core:
                        take(dve, gate_ready)
                    if h == 8 and ahead:
                        read_qkvg(p)
                    if h == 10 and tail:
                        read_oT()
                    if h == 12 and ahead:
                        split_qk(p)
                    if h == 13 and tail:
                        update(b - 1)
                    if h == 14 and further:
                        statistics(b + 3)
                    if h == 15 and ahead:
                        read_qkT(p)
                if heads:
                    dve.sem_inc(s_ready, -NH)

            def epilogue():
                read_av(0)
                read_av(1)
                norm_and_gate(1)
                read_oT()
                update(NB - 1)

            batches(dve, body, prologue, epilogue)


def program(nc, x, w, out, layers=("mamba", "experts", "attention", "experts")):
    ctx = ExitStack()
    with ctx:
        x_sb = ctx.enter_context(nc.sbuf_tensor("x_sb", [P, NT, DM], FP32))
        ident = ctx.enter_context(nc.sbuf_tensor("ident", [P, P], FP32))
        ident16 = ctx.enter_context(nc.sbuf_tensor("ident16", [P, P], FP16))
        half = ctx.enter_context(nc.sbuf_tensor("half", [P, QC // P], FP32))
        mw, aw, ew = MambaWeights(nc, ctx), AttentionWeights(nc, ctx), ExpertWeights(nc, ctx)
        loaded = {n: ctx.enter_context(nc.semaphore("loaded_" + n)) for n in ("x_head", "x_rest", "mamba", "experts", "attention")}
        made = ctx.enter_context(nc.semaphore("constants_made"))
        x_tiles = x.rearrange("b (n p) d -> p (b n) d", p=P)
        HEAD = 2 * TT

        later = [(x_sb[:, HEAD:NT], x_tiles[:, HEAD:NT], loaded["x_rest"])]
        later += [(dst, src, loaded["experts"]) for dst, src in ew.loads(w)]
        if "attention" in layers:
            later += [(dst, src, loaded["attention"]) for dst, src in aw.loads(w)]

        with nc.Block() as block:
            @block.sync
            def _(sp):
                sp.dma_start(x_sb[:, 0:HEAD], x_tiles[:, 0:HEAD]).then_inc(loaded["x_head"], 16)
                for dst, src in mw.loads(w)[0::2]:
                    sp.dma_start(dst, src).then_inc(loaded["mamba"], 16)

            @block.scalar
            def _(act):
                for dst, src in mw.loads(w)[1::2]:
                    act.dma_start(dst, src).then_inc(loaded["mamba"], 16)

            @block.gpsimd
            def _(pool):
                nc.gpsimd.memset(half[:], -0.5)
                nc.gpsimd.memset(ident[:], 0.0)
                nc.gpsimd.memset(ident16[:], 0.0).then_inc(made, 1)
                pool.wait_ge(made, 1)
                for i in (ident, ident16):
                    nc.gpsimd.affine_select(out=i[:], in_=i[:], compare_op=ALU.not_equal, fill=1.0, base=0,
                                            pattern=[[-1, P]], channel_multiplier=1)

        for n, layer in enumerate(layers):
            if layer == "mamba":
                mamba_layer(nc, ctx, x_sb, mw, loaded, later, ew, ident, half)
            if layer == "experts":
                last = n == len(layers) - 1
                expert_layer(nc, ctx, n, x_sb, ew, ident, half, out.rearrange("b (n p) d -> p (b n) d", p=P) if last else None)
            if layer == "attention":
                attention_layer(nc, ctx, x_sb, aw, loaded, ident, ident16, half)


def layout(v):
    import numpy as np
    g = {k: np.asarray(a) for k, a in v.items()}
    a = {k[len("L0_attn_a_"):]: g[k] for k in g if k.startswith("L0_attn_a_")}
    b = {k[len("L0_attn_b_"):]: g[k] for k in g if k.startswith("L0_attn_b_")}
    f = {k[len("L0_ffn_"):]: g[k] for k in g if k.startswith("L0_ffn_")}

    def chunks(m):
        return m.reshape(-1, P, *m.shape[1:]).swapaxes(0, 1)

    def spread(m, one):
        bc, dl = m[..., DTR:], m[..., :DTR]
        zero = np.zeros((*m.shape[:-1], 16), m.dtype)
        return np.concatenate([bc, dl, zero[..., :1] + one, zero[..., 1:], bc, zero, zero], -1)

    def rows(m):
        return np.repeat(m.reshape(1, -1), P, 0)

    w = {
        "in_w": a["in_W"], "in_b": a["in_b"].reshape(-1, P).T, "rms_w": a["rms_w"].reshape(P, 1),
        "conv_w": chunks(a["conv_w"]), "conv_b": a["conv_b"].reshape(-1, P).T, "a_log": chunks(a["A_log"]),
        "dbc_w": chunks(spread(a["dbc_W"], 0)), "dbc_b": spread(a["dbc_b"], 1).reshape(P, 1),
        "dup_w": np.concatenate([a["dup_W"], a["dup_b"][None]]),
        "out_w": chunks(a["out_W"]), "out_b": rows(a["out_b"]),
    }
    w["gate_up"] = np.stack([np.concatenate([f["w_gate"], f["shared_gate_w"][None]]),
                             np.concatenate([f["w_up"], f["shared_up_w"][None]])]).transpose(3, 1, 0, 2)
    w["down"] = np.concatenate([f["w_down"], f["shared_down_w"][None]]).transpose(2, 0, 1)
    w["router"] = f["gate_w"].T
    w["expert_bias"] = rows(f["expert_bias"])
    q = b["W_in"].reshape(NH, 4, DH, DM).transpose(1, 0, 2, 3).reshape(4 * NH * DH, DM)
    w["qkvg_w"] = q.T
    w["qkvg_b"] = rows(b["b_in"].reshape(NH, 4, DH).transpose(1, 0, 2))
    w["attn_out_w"] = b["W_out"].T
    w["attn_out_b"] = rows(b["b_out"])
    return {k: np.ascontiguousarray(m) for k, m in w.items()}


def kernel(**inputs):
    import numpy as np
    import concourse.bacc as bacc
    from concourse.bass_utils import run_bass_kernel_spmd as run

    nc = bacc.Bacc("TRN2", target_bir_lowering=False, num_devices=1)
    x = np.ascontiguousarray(inputs["L0_attn_a_x"])
    arrays = {"x": x, **{"w_" + k: m for k, m in layout(inputs).items()}}
    dram = {k: nc.dram_tensor(k, m.shape, FP32, kind="ExternalInput").ap() for k, m in arrays.items()}
    out = nc.dram_tensor("out", x.shape, FP32, kind="ExternalOutput").ap()
    program(nc, dram["x"], {k[2:]: a for k, a in dram.items() if k != "x"}, out)
    r = run(nc, [arrays], core_ids=[0])
    return r.results[0]["out"]
```
